# Optimizing a Trainium2 kernel written in Bass

```python
import numpy as np
import jax
import jax.numpy as jnp

def _softmax(x, axis=-1):
    return jax.nn.softmax(x, axis=axis)

def _gelu(x):
    return jax.nn.gelu(x, approximate=True)

def _silu(x):
    return jax.nn.silu(x)

def _sigmoid(x):
    return jax.nn.sigmoid(x)

def _layernorm(x, axis=-1, eps=1e-05):
    m = jnp.mean(x, axis=axis, keepdims=True)
    v = jnp.var(x, axis=axis, keepdims=True)
    return (x - m) / jnp.sqrt(v + eps)

def _scatter_add(tgt, idx, src, axis=0):
    return tgt.at[idx].add(src)

def _segment_sum(src, seg, n):
    return jax.ops.segment_sum(src, seg, n)
kernel_name = 'mk_recurrent_d2_jaxref_r8_7e8f4d'

def setup_inputs(seed: int=0):
    np.random.seed(seed)
    _w = jnp.asarray

    def _L0_attn_setup():
        import jax, jax.numpy as jnp
        import numpy as np
        B, S, D, H, I, A = (2, 256, 128, 16, 512, 2)
        HD = D // H

        def _gen_param(sub, Wl, W, Bp):
            p = jnp.einsum('a...,a->...', sub, Wl[0])
            return jnp.tanh(p) * W + Bp

        def _student_linear(x, sub_w, Wl_w, W_w, B_w, sub_b, Wl_b, W_b, B_b):
            w = _gen_param(sub_w, Wl_w, W_w, B_w)
            b = _gen_param(sub_b, Wl_b, W_b, B_b)
            return x @ w.T + b

        def _layernorm(x, g, b, eps=1e-05):
            m = jnp.mean(x, axis=-1, keepdims=True)
            v = jnp.mean((x - m) ** 2, axis=-1, keepdims=True)
            return (x - m) * jax.lax.rsqrt(v + eps) * g + b

        def _gelu_new(x):
            c = 0.7978845608028654
            return 0.5 * x * (1.0 + jnp.tanh(c * (x + 0.044715 * x ** 3)))

        def _block(hs, ln1_g, ln1_b, ln2_g, ln2_b, *p):
            ca, cp, cf, cm = (p[0:8], p[8:16], p[16:24], p[24:32])
            b_, s_, d_ = hs.shape
            h = _layernorm(hs, ln1_g, ln1_b)
            qkv = _student_linear(h, *ca)
            q, k, v = jnp.split(qkv, 3, axis=-1)
            split = lambda t: t.reshape(b_, s_, H, HD).transpose(0, 2, 1, 3)
            q, k, v = (split(q), split(k), split(v))
            scores = jnp.einsum('bhqd,bhkd->bhqk', q, k) / float(HD) ** 0.5
            causal = jnp.tril(jnp.ones((s_, s_), dtype=bool))
            scores = jnp.where(causal, scores, jnp.asarray(-10000.0, scores.dtype))
            attn = jax.nn.softmax(scores, axis=-1)
            o = jnp.einsum('bhqk,bhkd->bhqd', attn, v)
            o = o.transpose(0, 2, 1, 3).reshape(b_, s_, d_)
            o = _student_linear(o, *cp)
            hs = hs + o
            h2 = _layernorm(hs, ln2_g, ln2_b)
            m = _student_linear(h2, *cf)
            m = _gelu_new(m)
            m = _student_linear(m, *cm)
            return hs + m
        key = jax.random.key(seed)
        ks = iter(jax.random.split(key, 32))

        def lin(out_f, in_f):
            return {'sub_w': jax.random.normal(next(ks), (A, out_f, in_f), jnp.float32) * 0.02, 'Wl_w': jax.random.normal(next(ks), (1, A), jnp.float32) * 0.5, 'W_w': jnp.ones((out_f, in_f), jnp.float32), 'B_w': jnp.zeros((out_f, in_f), jnp.float32), 'sub_b': jax.random.normal(next(ks), (A, out_f), jnp.float32) * 0.02, 'Wl_b': jax.random.normal(next(ks), (1, A), jnp.float32) * 0.5, 'W_b': jnp.ones((out_f,), jnp.float32), 'B_b': jnp.zeros((out_f,), jnp.float32)}
        inp = {'hs': jax.random.normal(next(ks), (B, S, D), jnp.float32)}
        for name, (o, i) in (('ca', (3 * D, D)), ('cp', (D, D)), ('cf', (I, D)), ('cm', (D, I))):
            for k2, v in lin(o, i).items():
                inp[name + '_' + k2] = v
        inp['ln1_g'] = jnp.ones((D,), jnp.float32)
        inp['ln1_b'] = jnp.zeros((D,), jnp.float32)
        inp['ln2_g'] = jnp.ones((D,), jnp.float32)
        inp['ln2_b'] = jnp.zeros((D,), jnp.float32)
        return inp
    _L0_attn_in = _L0_attn_setup()

    def _L0_ffn_setup():
        import jax, jax.numpy as jnp
        import numpy as np
        B, S, DIM = (4, 512, 128)
        BASE_COUPLING = 0.1
        NUM_CYCLES = 3

        def _gelu(x):
            return jax.nn.gelu(x, approximate=False)

        def _coupling_net(h, w1, b1, w2, b2, w3, b3, w4, b4):
            h = _gelu(h @ w1 + b1)
            h = _gelu(h @ w2 + b2)
            h = _gelu(h @ w3 + b3)
            return jax.nn.sigmoid(h @ w4 + b4)

        def _global_net(h, w1, b1, w2, b2, w3, b3):
            h = _gelu(h @ w1 + b1)
            h = _gelu(h @ w2 + b2)
            return jax.nn.sigmoid(h @ w3 + b3)

        def _twist(x):
            o_r, o_i, p_r, p_i = jnp.split(x, 4, axis=-1)
            return jnp.concatenate([p_r, -p_i, -o_r, o_i], axis=-1)
        key = jax.random.key(seed)
        ks = jax.random.split(key, 9)
        d = DIM

        def w(k, fan_in, fan_out):
            return jax.random.normal(k, (fan_in, fan_out), dtype=jnp.float32) / np.sqrt(fan_in).astype(np.float32)
        inp = {'x': jax.random.normal(ks[0], (B, S, d), dtype=jnp.float32)}
        cn_dims = [(d, d), (d, d // 2), (d // 2, d // 4), (d // 4, 1)]
        for i, (a, b) in enumerate(cn_dims):
            inp[f'cn_w{i + 1}'] = w(ks[1 + i], a, b)
            inp[f'cn_b{i + 1}'] = jnp.zeros((b,), dtype=jnp.float32)
        gc_dims = [(d, d // 2), (d // 2, d // 4), (d // 4, 1)]
        for i, (a, b) in enumerate(gc_dims):
            inp[f'gc_w{i + 1}'] = w(ks[5 + i], a, b)
            inp[f'gc_b{i + 1}'] = jnp.zeros((b,), dtype=jnp.float32)
        inp['adaptive_range'] = jnp.full((1,), 0.2, dtype=jnp.float32)
        return inp
    _L0_ffn_in = _L0_ffn_setup()

    def _L1_attn_setup():
        import jax, jax.numpy as jnp
        import numpy as np
        import math
        B, S, D = (8, 256, 128)

        def _trunc_normal(key, shape, fan_in, fan_out):
            std = math.sqrt(2.0 / (fan_in + fan_out))
            return jax.random.truncated_normal(key, -3.0, 3.0, shape, jnp.float32) * std
        key = jax.random.key(seed)
        kx, kq, kk, kv, ko = jax.random.split(key, 5)
        return {'in_features': jax.random.normal(kx, (B, S, D), jnp.float32), 'Wq': _trunc_normal(kq, (D, D), D, D), 'Wk': _trunc_normal(kk, (D, D), D, D), 'Wv': _trunc_normal(kv, (D, D), D, D), 'Wo': _trunc_normal(ko, (D, D), D, D)}
    _L1_attn_in = _L1_attn_setup()

    def _L1_ffn_setup():
        import jax, jax.numpy as jnp
        import numpy as np
        HIDDEN = 128
        INTER = 512
        N_EXPERTS = 8

        def geglu(x, w1, w2, w3):
            return jax.nn.gelu(x @ w1, approximate=False) * (x @ w2) @ w3
        key = jax.random.key(seed)
        ks = jax.random.split(key, 8)
        s = 0.02
        x = jax.random.normal(ks[0], (2, 256, HIDDEN), dtype=jnp.float32)
        w1s = jax.random.normal(ks[1], (HIDDEN, INTER), dtype=jnp.float32) * s
        w2s = jax.random.normal(ks[2], (HIDDEN, INTER), dtype=jnp.float32) * s
        w3s = jax.random.normal(ks[3], (INTER, HIDDEN), dtype=jnp.float32) * s
        W1 = jax.random.normal(ks[4], (N_EXPERTS, HIDDEN, INTER), dtype=jnp.float32) * s
        W2 = jax.random.normal(ks[5], (N_EXPERTS, HIDDEN, INTER), dtype=jnp.float32) * s
        W3 = jax.random.normal(ks[6], (N_EXPERTS, INTER, HIDDEN), dtype=jnp.float32) * s
        Wg = jax.random.normal(ks[7], (HIDDEN, N_EXPERTS), dtype=jnp.float32) * s
        return {'x': x, 'w1s': w1s, 'w2s': w2s, 'w3s': w3s, 'W1': W1, 'W2': W2, 'W3': W3, 'Wg': Wg}
    _L1_ffn_in = _L1_ffn_setup()
    _d = {'L0_attn_hs': _L0_attn_in['hs'], 'L0_attn_ln1_g': _L0_attn_in['ln1_g'], 'L0_attn_ln1_b': _L0_attn_in['ln1_b'], 'L0_attn_ln2_g': _L0_attn_in['ln2_g'], 'L0_attn_ln2_b': _L0_attn_in['ln2_b'], 'L0_attn_ca_sub_w': _L0_attn_in['ca_sub_w'], 'L0_attn_ca_Wl_w': _L0_attn_in['ca_Wl_w'], 'L0_attn_ca_W_w': _L0_attn_in['ca_W_w'], 'L0_attn_ca_B_w': _L0_attn_in['ca_B_w'], 'L0_attn_ca_sub_b': _L0_attn_in['ca_sub_b'], 'L0_attn_ca_Wl_b': _L0_attn_in['ca_Wl_b'], 'L0_attn_ca_W_b': _L0_attn_in['ca_W_b'], 'L0_attn_ca_B_b': _L0_attn_in['ca_B_b'], 'L0_attn_cp_sub_w': _L0_attn_in['cp_sub_w'], 'L0_attn_cp_Wl_w': _L0_attn_in['cp_Wl_w'], 'L0_attn_cp_W_w': _L0_attn_in['cp_W_w'], 'L0_attn_cp_B_w': _L0_attn_in['cp_B_w'], 'L0_attn_cp_sub_b': _L0_attn_in['cp_sub_b'], 'L0_attn_cp_Wl_b': _L0_attn_in['cp_Wl_b'], 'L0_attn_cp_W_b': _L0_attn_in['cp_W_b'], 'L0_attn_cp_B_b': _L0_attn_in['cp_B_b'], 'L0_attn_cf_sub_w': _L0_attn_in['cf_sub_w'], 'L0_attn_cf_Wl_w': _L0_attn_in['cf_Wl_w'], 'L0_attn_cf_W_w': _L0_attn_in['cf_W_w'], 'L0_attn_cf_B_w': _L0_attn_in['cf_B_w'], 'L0_attn_cf_sub_b': _L0_attn_in['cf_sub_b'], 'L0_attn_cf_Wl_b': _L0_attn_in['cf_Wl_b'], 'L0_attn_cf_W_b': _L0_attn_in['cf_W_b'], 'L0_attn_cf_B_b': _L0_attn_in['cf_B_b'], 'L0_attn_cm_sub_w': _L0_attn_in['cm_sub_w'], 'L0_attn_cm_Wl_w': _L0_attn_in['cm_Wl_w'], 'L0_attn_cm_W_w': _L0_attn_in['cm_W_w'], 'L0_attn_cm_B_w': _L0_attn_in['cm_B_w'], 'L0_attn_cm_sub_b': _L0_attn_in['cm_sub_b'], 'L0_attn_cm_Wl_b': _L0_attn_in['cm_Wl_b'], 'L0_attn_cm_W_b': _L0_attn_in['cm_W_b'], 'L0_attn_cm_B_b': _L0_attn_in['cm_B_b'], 'L0_ffn_cn_w1': _L0_ffn_in['cn_w1'], 'L0_ffn_cn_b1': _L0_ffn_in['cn_b1'], 'L0_ffn_cn_w2': _L0_ffn_in['cn_w2'], 'L0_ffn_cn_b2': _L0_ffn_in['cn_b2'], 'L0_ffn_cn_w3': _L0_ffn_in['cn_w3'], 'L0_ffn_cn_b3': _L0_ffn_in['cn_b3'], 'L0_ffn_cn_w4': _L0_ffn_in['cn_w4'], 'L0_ffn_cn_b4': _L0_ffn_in['cn_b4'], 'L0_ffn_gc_w1': _L0_ffn_in['gc_w1'], 'L0_ffn_gc_b1': _L0_ffn_in['gc_b1'], 'L0_ffn_gc_w2': _L0_ffn_in['gc_w2'], 'L0_ffn_gc_b2': _L0_ffn_in['gc_b2'], 'L0_ffn_gc_w3': _L0_ffn_in['gc_w3'], 'L0_ffn_gc_b3': _L0_ffn_in['gc_b3'], 'L0_ffn_adaptive_range': _L0_ffn_in['adaptive_range'], 'L1_attn_Wq': _L1_attn_in['Wq'], 'L1_attn_Wk': _L1_attn_in['Wk'], 'L1_attn_Wv': _L1_attn_in['Wv'], 'L1_attn_Wo': _L1_attn_in['Wo'], 'L1_ffn_w1s': _L1_ffn_in['w1s'], 'L1_ffn_w2s': _L1_ffn_in['w2s'], 'L1_ffn_w3s': _L1_ffn_in['w3s'], 'L1_ffn_W1': _L1_ffn_in['W1'], 'L1_ffn_W2': _L1_ffn_in['W2'], 'L1_ffn_W3': _L1_ffn_in['W3'], 'L1_ffn_Wg': _L1_ffn_in['Wg']}
    _x0 = _d['L0_attn_hs']
    _d['L0_attn_hs'] = jax.random.normal(jax.random.fold_in(jax.random.key(seed), 1), (4, 1024, 128), dtype=_x0.dtype)
    del _x0
    return _d

def reference(L0_attn_hs, L0_attn_ln1_g, L0_attn_ln1_b, L0_attn_ln2_g, L0_attn_ln2_b, L0_attn_ca_sub_w, L0_attn_ca_Wl_w, L0_attn_ca_W_w, L0_attn_ca_B_w, L0_attn_ca_sub_b, L0_attn_ca_Wl_b, L0_attn_ca_W_b, L0_attn_ca_B_b, L0_attn_cp_sub_w, L0_attn_cp_Wl_w, L0_attn_cp_W_w, L0_attn_cp_B_w, L0_attn_cp_sub_b, L0_attn_cp_Wl_b, L0_attn_cp_W_b, L0_attn_cp_B_b, L0_attn_cf_sub_w, L0_attn_cf_Wl_w, L0_attn_cf_W_w, L0_attn_cf_B_w, L0_attn_cf_sub_b, L0_attn_cf_Wl_b, L0_attn_cf_W_b, L0_attn_cf_B_b, L0_attn_cm_sub_w, L0_attn_cm_Wl_w, L0_attn_cm_W_w, L0_attn_cm_B_w, L0_attn_cm_sub_b, L0_attn_cm_Wl_b, L0_attn_cm_W_b, L0_attn_cm_B_b, L0_ffn_cn_w1, L0_ffn_cn_b1, L0_ffn_cn_w2, L0_ffn_cn_b2, L0_ffn_cn_w3, L0_ffn_cn_b3, L0_ffn_cn_w4, L0_ffn_cn_b4, L0_ffn_gc_w1, L0_ffn_gc_b1, L0_ffn_gc_w2, L0_ffn_gc_b2, L0_ffn_gc_w3, L0_ffn_gc_b3, L0_ffn_adaptive_range, L1_attn_Wq, L1_attn_Wk, L1_attn_Wv, L1_attn_Wo, L1_ffn_w1s, L1_ffn_w2s, L1_ffn_w3s, L1_ffn_W1, L1_ffn_W2, L1_ffn_W3, L1_ffn_Wg):

    def _L0_attn_ref(hs, ln1_g, ln1_b, ln2_g, ln2_b, ca_sub_w, ca_Wl_w, ca_W_w, ca_B_w, ca_sub_b, ca_Wl_b, ca_W_b, ca_B_b, cp_sub_w, cp_Wl_w, cp_W_w, cp_B_w, cp_sub_b, cp_Wl_b, cp_W_b, cp_B_b, cf_sub_w, cf_Wl_w, cf_W_w, cf_B_w, cf_sub_b, cf_Wl_b, cf_W_b, cf_B_b, cm_sub_w, cm_Wl_w, cm_W_w, cm_B_w, cm_sub_b, cm_Wl_b, cm_W_b, cm_B_b):
        import jax, jax.numpy as jnp
        import numpy as np
        B, S, D, H, I, A = (2, 256, 128, 16, 512, 2)
        HD = D // H

        def _gen_param(sub, Wl, W, Bp):
            p = jnp.einsum('a...,a->...', sub, Wl[0])
            return jnp.tanh(p) * W + Bp

        def _student_linear(x, sub_w, Wl_w, W_w, B_w, sub_b, Wl_b, W_b, B_b):
            w = _gen_param(sub_w, Wl_w, W_w, B_w)
            b = _gen_param(sub_b, Wl_b, W_b, B_b)
            return x @ w.T + b

        def _layernorm(x, g, b, eps=1e-05):
            m = jnp.mean(x, axis=-1, keepdims=True)
            v = jnp.mean((x - m) ** 2, axis=-1, keepdims=True)
            return (x - m) * jax.lax.rsqrt(v + eps) * g + b

        def _gelu_new(x):
            c = 0.7978845608028654
            return 0.5 * x * (1.0 + jnp.tanh(c * (x + 0.044715 * x ** 3)))

        def _block(hs, ln1_g, ln1_b, ln2_g, ln2_b, *p):
            ca, cp, cf, cm = (p[0:8], p[8:16], p[16:24], p[24:32])
            b_, s_, d_ = hs.shape
            h = _layernorm(hs, ln1_g, ln1_b)
            qkv = _student_linear(h, *ca)
            q, k, v = jnp.split(qkv, 3, axis=-1)
            split = lambda t: t.reshape(b_, s_, H, HD).transpose(0, 2, 1, 3)
            q, k, v = (split(q), split(k), split(v))
            scores = jnp.einsum('bhqd,bhkd->bhqk', q, k) / float(HD) ** 0.5
            causal = jnp.tril(jnp.ones((s_, s_), dtype=bool))
            scores = jnp.where(causal, scores, jnp.asarray(-10000.0, scores.dtype))
            attn = jax.nn.softmax(scores, axis=-1)
            o = jnp.einsum('bhqk,bhkd->bhqd', attn, v)
            o = o.transpose(0, 2, 1, 3).reshape(b_, s_, d_)
            o = _student_linear(o, *cp)
            hs = hs + o
            h2 = _layernorm(hs, ln2_g, ln2_b)
            m = _student_linear(h2, *cf)
            m = _gelu_new(m)
            m = _student_linear(m, *cm)
            return hs + m
        return _block(hs, ln1_g, ln1_b, ln2_g, ln2_b, ca_sub_w, ca_Wl_w, ca_W_w, ca_B_w, ca_sub_b, ca_Wl_b, ca_W_b, ca_B_b, cp_sub_w, cp_Wl_w, cp_W_w, cp_B_w, cp_sub_b, cp_Wl_b, cp_W_b, cp_B_b, cf_sub_w, cf_Wl_w, cf_W_w, cf_B_w, cf_sub_b, cf_Wl_b, cf_W_b, cf_B_b, cm_sub_w, cm_Wl_w, cm_W_w, cm_B_w, cm_sub_b, cm_Wl_b, cm_W_b, cm_B_b)

    def _L0_ffn_ref(x, cn_w1, cn_b1, cn_w2, cn_b2, cn_w3, cn_b3, cn_w4, cn_b4, gc_w1, gc_b1, gc_w2, gc_b2, gc_w3, gc_b3, adaptive_range):
        import jax, jax.numpy as jnp
        import numpy as np
        B, S, DIM = (4, 512, 128)
        BASE_COUPLING = 0.1
        NUM_CYCLES = 3

        def _gelu(x):
            return jax.nn.gelu(x, approximate=False)

        def _coupling_net(h, w1, b1, w2, b2, w3, b3, w4, b4):
            h = _gelu(h @ w1 + b1)
            h = _gelu(h @ w2 + b2)
            h = _gelu(h @ w3 + b3)
            return jax.nn.sigmoid(h @ w4 + b4)

        def _global_net(h, w1, b1, w2, b2, w3, b3):
            h = _gelu(h @ w1 + b1)
            h = _gelu(h @ w2 + b2)
            return jax.nn.sigmoid(h @ w3 + b3)

        def _twist(x):
            o_r, o_i, p_r, p_i = jnp.split(x, 4, axis=-1)
            return jnp.concatenate([p_r, -p_i, -o_r, o_i], axis=-1)
        global_context = x.mean(axis=1, keepdims=True)
        gf = _global_net(global_context, gc_w1, gc_b1, gc_w2, gc_b2, gc_w3, gc_b3)
        out = x
        for _ in range(NUM_CYCLES):
            tf = _coupling_net(out, cn_w1, cn_b1, cn_w2, cn_b2, cn_w3, cn_b3, cn_w4, cn_b4)
            combined = 0.7 * gf + 0.3 * tf
            coupling = BASE_COUPLING + adaptive_range * (combined - 0.5) * 2.0
            out = out + coupling * _twist(out)
        return out

    def _L1_attn_ref(in_features, Wq, Wk, Wv, Wo):
        import jax, jax.numpy as jnp
        import numpy as np
        import math
        B, S, D = (8, 256, 128)

        def _trunc_normal(key, shape, fan_in, fan_out):
            std = math.sqrt(2.0 / (fan_in + fan_out))
            return jax.random.truncated_normal(key, -3.0, 3.0, shape, jnp.float32) * std
        d_k = Wq.shape[0]
        scale = 1.0 / math.sqrt(d_k)
        x = in_features
        Q = x @ Wq.T
        K = x @ Wk.T
        V = x @ Wv.T
        scores = jnp.einsum('bqd,bkd->bqk', Q, K) * scale
        seq_len = x.shape[-2]
        causal = jnp.tril(jnp.ones((seq_len, seq_len), dtype=bool))
        scores = jnp.where(causal, scores, -jnp.inf)
        attn = jax.nn.softmax(scores, axis=-1)
        out = jnp.einsum('bqk,bkd->bqd', attn, V)
        return out @ Wo.T

    def _L1_ffn_ref(x, w1s, w2s, w3s, W1, W2, W3, Wg):
        import jax, jax.numpy as jnp
        import numpy as np
        HIDDEN = 128
        INTER = 512
        N_EXPERTS = 8

        def geglu(x, w1, w2, w3):
            return jax.nn.gelu(x @ w1, approximate=False) * (x @ w2) @ w3
        B, T, C = x.shape
        xf = x.reshape(-1, C)
        shared = geglu(xf, w1s, w2s, w3s)
        logits = xf @ Wg
        idx = jnp.argmax(logits, axis=-1)
        final = jnp.zeros_like(xf)
        for e in range(N_EXPERTS):
            y = geglu(xf, W1[e], W2[e], W3[e])
            final = final + jnp.where((idx == e)[:, None], y, 0.0)
        return (shared + final).reshape(B, T, C)
    x = L0_attn_hs
    xn = _layernorm(x, axis=-1)
    s = _L0_attn_ref(xn, L0_attn_ln1_g, L0_attn_ln1_b, L0_attn_ln2_g, L0_attn_ln2_b, L0_attn_ca_sub_w, L0_attn_ca_Wl_w, L0_attn_ca_W_w, L0_attn_ca_B_w, L0_attn_ca_sub_b, L0_attn_ca_Wl_b, L0_attn_ca_W_b, L0_attn_ca_B_b, L0_attn_cp_sub_w, L0_attn_cp_Wl_w, L0_attn_cp_W_w, L0_attn_cp_B_w, L0_attn_cp_sub_b, L0_attn_cp_Wl_b, L0_attn_cp_W_b, L0_attn_cp_B_b, L0_attn_cf_sub_w, L0_attn_cf_Wl_w, L0_attn_cf_W_w, L0_attn_cf_B_w, L0_attn_cf_sub_b, L0_attn_cf_Wl_b, L0_attn_cf_W_b, L0_attn_cf_B_b, L0_attn_cm_sub_w, L0_attn_cm_Wl_w, L0_attn_cm_W_w, L0_attn_cm_B_w, L0_attn_cm_sub_b, L0_attn_cm_Wl_b, L0_attn_cm_W_b, L0_attn_cm_B_b)
    g = _silu(_L0_ffn_ref(xn, L0_ffn_cn_w1, L0_ffn_cn_b1, L0_ffn_cn_w2, L0_ffn_cn_b2, L0_ffn_cn_w3, L0_ffn_cn_b3, L0_ffn_cn_w4, L0_ffn_cn_b4, L0_ffn_gc_w1, L0_ffn_gc_b1, L0_ffn_gc_w2, L0_ffn_gc_b2, L0_ffn_gc_w3, L0_ffn_gc_b3, L0_ffn_adaptive_range))
    x = x + s * g
    xn = _layernorm(x, axis=-1)
    s = _L1_attn_ref(xn, L1_attn_Wq, L1_attn_Wk, L1_attn_Wv, L1_attn_Wo)
    g = _silu(_L1_ffn_ref(xn, L1_ffn_w1s, L1_ffn_w2s, L1_ffn_w3s, L1_ffn_W1, L1_ffn_W2, L1_ffn_W3, L1_ffn_Wg))
    x = x + s * g
    return x

_drawn_inputs = setup_inputs


def setup_inputs(seed=0):
    import zlib

    import numpy as np

    out = dict(_drawn_inputs(seed))
    spreads = {'L0_attn_ln1_g': (1.0, 0.2),
     'L0_attn_ln1_b': (0.0, 0.1),
     'L0_attn_ln2_g': (1.0, 0.2),
     'L0_attn_ln2_b': (0.0, 0.1),
     'L0_attn_ca_W_w': (1.0, 0.6),
     'L0_attn_ca_B_w': (0.0, 0.1),
     'L0_attn_ca_W_b': (1.0, 0.6),
     'L0_attn_ca_B_b': (0.0, 0.1),
     'L0_attn_cp_W_w': (1.0, 0.6),
     'L0_attn_cp_B_w': (0.0, 0.1),
     'L0_attn_cp_W_b': (1.0, 0.6),
     'L0_attn_cp_B_b': (0.0, 0.1),
     'L0_attn_cf_W_w': (1.0, 0.6),
     'L0_attn_cf_B_w': (0.0, 0.1),
     'L0_attn_cf_W_b': (1.0, 0.6),
     'L0_attn_cf_B_b': (0.0, 0.1),
     'L0_attn_cm_W_w': (1.0, 0.6),
     'L0_attn_cm_B_w': (0.0, 0.1),
     'L0_attn_cm_W_b': (1.0, 0.6),
     'L0_attn_cm_B_b': (0.0, 0.285),
     'L0_ffn_cn_b1': (0.0, 0.8),
     'L0_ffn_cn_b2': (0.0, 0.8),
     'L0_ffn_cn_b3': (0.0, 0.8),
     'L0_ffn_gc_b1': (0.0, 0.8),
     'L0_ffn_gc_b2': (0.0, 2.0)}
    factors = {'L0_attn_ca_Wl_w': 8.0,
     'L0_attn_ca_sub_b': 6.539,
     'L0_attn_ca_Wl_b': 5.3,
     'L0_attn_cp_sub_b': 5.191,
     'L0_attn_cp_Wl_b': 8.0,
     'L0_attn_cf_Wl_w': 4.845,
     'L0_attn_cf_sub_b': 8.0,
     'L0_attn_cf_Wl_b': 8.0,
     'L0_attn_cm_sub_b': 8.0,
     'L0_attn_cm_Wl_b': 8.0,
     'L0_ffn_cn_w1': 6.377,
     'L0_ffn_cn_w2': 6.041,
     'L0_ffn_cn_w3': 5.187,
     'L0_ffn_cn_w4': 3.309,
     'L0_ffn_gc_w1': 64.0,
     'L0_ffn_gc_w2': 64.0,
     'L0_ffn_gc_w3': 8.0,
     'L1_attn_Wq': 8.0,
     'L1_attn_Wk': 8.0,
     'L1_attn_Wv': 8.0,
     'L1_attn_Wo': 8.0,
     'L1_ffn_w1s': 8.0,
     'L1_ffn_w2s': 8.0,
     'L1_ffn_w3s': 8.0,
     'L1_ffn_W1': 8.0,
     'L1_ffn_W2': 8.0,
     'L1_ffn_W3': 8.0,
     'L1_ffn_Wg': 8.0}
    for name, (base, spread) in spreads.items():
        noise = np.random.default_rng([zlib.crc32(name.encode()), seed]).standard_normal(out[name].shape)
        drawn = base * np.exp(spread * noise) if base else spread * noise
        out[name] = jnp.asarray(drawn.astype(out[name].dtype))
    for name, factor in factors.items():
        out[name] = (out[name] * factor).astype(out[name].dtype)
    return out
```

```python
from contextlib import ExitStack

import concourse.bass as bass
from concourse import mybir

ALU = mybir.AluOpType
ACT = mybir.ActivationFunctionType
AX = mybir.AxisListType
F32 = mybir.dt.float32
BF16 = mybir.dt.bfloat16

P = 128
B, S, D = 4, 1024, 128
T = B * S
NT = T // P
TPB = S // P
CH = 512
NC = T // CH
H, HD = 16, 8
PAIRS = B * H // 2
INTER = 512
NI = INTER // P
NE = 8
EPS = 1e-5
BIG = -1e30
TERMS = [(0, 0), (0, 1), (1, 0), (0, 2), (1, 1), (2, 0)]
QROWS = len(TERMS) * HD
SROWS = QROWS + 3

W_CA, W_CP, W_CF, W_CM = 0, 384, 512, 1024
C_CA, C_CP, C_CF, C_CM = 1536, 1539, 1540, 1544
R_V, R_CP, R_CM = 1545, 1673, 1801
GEN = 1929


def tokens(x):
    return x.rearrange("b s d -> (b s) d").rearrange("(t p) d -> p t d", p=P)


def after(engine, semaphore, count):
    if isinstance(count, int) and count <= 0:
        return
    engine.wait_ge(semaphore, count)


def stage_weights(nc, sem, io, k):
    with ExitStack() as ctx:
        sb = lambda n, s, d=F32: ctx.enter_context(nc.sbuf_tensor(n, s, d))
        gs = {n: sb(f"gen_{n}", [P, GEN]) for n in ("s0", "s1", "W", "B")}
        gen = sb("gen_out", [P, GEN])
        wl = sb("wl", [P, 16])
        l1w = sb("l1w", [P, 4, P])
        loaded, consts, blended, squashed, scaled, done, turned = (
            sem(n) for n in ("w_loaded", "w_consts", "w_blended", "w_squashed", "w_scaled", "w_done", "w_turned"))
        consts0 = sem("w_consts0")
        lin = {n: {m: io[f"L0_attn_{n}_{m}"] for m in ("sub_w", "Wl_w", "W_w", "B_w", "sub_b", "Wl_b", "W_b", "B_b")}
               for n in ("ca", "cp", "cf", "cm")}
        order = ("ca", "cp", "cf", "cm")
        loads = []
        for g in ("s0", "s1", "W", "B"):
            for n, at, cols in (("ca", W_CA, 3), ("cp", W_CP, 1), ("cf", W_CF, 4)):
                src = lin[n]["sub_w"][int(g[1])] if g[0] == "s" else lin[n][g + "_w"]
                loads.append((gs[g][:, at:at + cols * P].rearrange("p (c i) -> p c i", i=P),
                              src.rearrange("(c p) i -> p c i", p=P)))
            src = lin["cm"]["sub_w"][int(g[1])] if g[0] == "s" else lin["cm"][g + "_w"]
            loads.append((gs[g][:, W_CM:W_CM + INTER], src))
            for n, at, cols in (("ca", C_CA, 3), ("cp", C_CP, 1), ("cf", C_CF, 4), ("cm", C_CM, 1)):
                src = lin[n]["sub_b"][int(g[1])] if g[0] == "s" else lin[n][g + "_b"]
                loads.append((gs[g][:, at:at + cols], src.rearrange("(c p) -> p c", p=P)))
            for n, at, lo in (("ca", R_V, 256), ("cp", R_CP, 0), ("cm", R_CM, 0)):
                src = lin[n]["sub_b"][int(g[1])] if g[0] == "s" else lin[n][g + "_b"]
                loads.append((gs[g][:, at:at + P], src[lo:lo + P].partition_broadcast(P)))
        for j, n in enumerate(order):
            loads.append((wl[:, 2 * j:2 * j + 2], lin[n]["Wl_w"][0].partition_broadcast(P)))
            loads.append((wl[:, 8 + 2 * j:10 + 2 * j], lin[n]["Wl_b"][0].partition_broadcast(P)))
        for j, n in enumerate(("Wq", "Wk", "Wv", "Wo")):
            loads.append((l1w[:, j, :], io["L1_attn_" + n]))
        parts = [(W_CA, 384, 0), (W_CP, P, 2), (W_CF, 512, 4), (W_CM, 512, 6), (C_CA, 3, 8), (C_CP, 1, 10),
                 (C_CF, 4, 12), (C_CM, 1, 14), (R_V, P, 8), (R_CP, P, 10), (R_CM, P, 14)]
        xv = tokens(io["L0_attn_hs"])
        ln_cols = [(k.ln_cols[:, j:j + 1], io["L0_attn_" + n].rearrange("(p a) -> p a", a=1))
                   for j, n in enumerate(("ln1_g", "ln1_b", "ln2_g", "ln2_b"))]
        loads += ln_cols
        half = len(loads) // 2

        with nc.Block() as block:
            @block.sync
            def _(sp):
                for q in range(4):
                    sp.dma_start(k.x[:, 8 * q:8 * q + 8, :], xv[:, 8 * q:8 * q + 8, :]).then_inc(k.x_loaded[q], 16)
                for dst, src in loads[:half]:
                    sp.dma_start(dst, src).then_inc(loaded, 16)

            @block.scalar
            def _(act):
                for dst, src in loads[half:]:
                    act.dma_start(dst, src).then_inc(loaded, 16)
                act.wait_ge(blended, 2 * len(parts))
                act.activation(gen[:, :], gen[:, :], ACT.Tanh).then_inc(squashed, 1)
                for c in range(2):
                    act.wait_ge(done, 4 * c + 4)
                    act.copy(k.wT[:, c * CH:(c + 1) * CH], k.ps[:, c, :]).then_inc(turned, 1)

            @block.gpsimd
            def _(pool):
                pool.memset(k.ident[:, :], 0.0).then_inc(consts0, 1)
                pool.memset(k.identb[:, :], 0.0).then_inc(consts0, 1)
                pool.memset(k.half_ident[:, :, :], 0.0).then_inc(consts0, 1)
                pool.memset(k.half_mask[:, :, :], 0.0).then_inc(consts0, 1)
                pool.memset(k.half_maskT[:, :, :], 0.0).then_inc(consts0, 1)
                pool.memset(k.mask[:, :], 0.0).then_inc(consts0, 1)
                pool.memset(k.perm[:, :], 0.0).then_inc(consts0, 1)
                pool.memset(k.eps[:, :], EPS).then_inc(consts, 1)
                pool.memset(k.ones_row[:, :], 1.0).then_inc(consts, 1)
                pool.wait_ge(consts0, 7)
                for t in (k.ident, k.identb):
                    pool.affine_select(out=t[:, :], in_=t[:, :], compare_op=ALU.not_equal, fill=1.0, base=0,
                                       pattern=[[-1, P]], channel_multiplier=1).then_inc(consts, 1)
                pool.affine_select(out=k.mask[:, :], in_=k.mask[:, :], compare_op=ALU.is_ge, fill=BIG, base=0,
                                   pattern=[[-1, P]], channel_multiplier=1).then_inc(consts, 1)
                n = 5
                for lo in (0, 64):
                    for t, fill, compare, pattern, step in (
                            (k.half_ident, 1.0, ALU.not_equal, [[64, 2], [-1, P]], 1),
                            (k.half_mask, BIG, ALU.is_ge, [[64, 2], [-1, P]], 1),
                            (k.half_maskT, BIG, ALU.is_ge, [[-64, 2], [1, P]], -1)):
                        pool.wait_ge(consts, n)
                        t = t[lo:lo + 64, :, :]
                        pool.affine_select(out=t, in_=t, compare_op=compare, fill=fill, base=0,
                                           pattern=pattern, channel_multiplier=step).then_inc(consts, 1)
                        n += 1
                for lo, at, sign in ((64, 0, 1.0), (96, 32, -1.0), (0, 64, -1.0), (32, 96, 1.0)):
                    pool.wait_ge(consts, n)
                    t = k.perm[lo:lo + 32, at:at + 32]
                    pool.affine_select(out=t, in_=t, compare_op=ALU.not_equal, fill=sign, base=0,
                                       pattern=[[-1, 32]], channel_multiplier=1).then_inc(consts, 1)
                    n += 1

            @block.vector
            def _(v):
                v.wait_ge(loaded, 16 * len(loads))
                for n, (at, cols, w) in enumerate(parts):
                    v.tensor_scalar(gen[:, at:at + cols], gs["s0"][:, at:at + cols], wl[:, w:w + 1], None,
                                    ALU.mult).then_inc(blended, 1)
                v.wait_ge(blended, len(parts))
                for n, (at, cols, w) in enumerate(parts):
                    v.scalar_tensor_tensor(out=gen[:, at:at + cols], in0=gs["s1"][:, at:at + cols],
                                           scalar=wl[:, w + 1:w + 2], in1=gen[:, at:at + cols],
                                           op0=ALU.mult, op1=ALU.add).then_inc(blended, 1)
                v.wait_ge(squashed, 1)
                v.tensor_tensor(gen[:, :], gen[:, :], gs["W"][:, :], ALU.mult).then_inc(scaled, 1)
                v.wait_ge(scaled, 1)
                v.tensor_tensor(gen[:, :], gen[:, :], gs["B"][:, :], ALU.add).then_inc(scaled, 1)
                v.wait_ge(scaled, 2)
                v.tensor_copy(k.bias_cols[:, :], gen[:, C_CA:C_CA + 9]).then_inc(turned, 1)
                v.tensor_copy(k.bias_rows[:, :], gen[:, R_V:R_V + 3 * P]).then_inc(turned, 1)
                for c in range(2, 4):
                    v.wait_ge(done, 4 * c + 4)
                    v.tensor_copy(k.wT[:, c * CH:(c + 1) * CH], k.ps[:, c, :]).then_inc(turned, 1)

            @block.tensor
            def _(pe):
                pe.wait_ge(consts, 15)
                pe.wait_ge(scaled, 2)
                for n in range(16):
                    src = gen[:, n * P:(n + 1) * P] if n < 12 else l1w[:, n - 12, :]
                    pe.transpose(k.ps[:, n // 4, (n % 4) * P:(n % 4 + 1) * P], src, k.ident[:, :]).then_inc(done, 1)


def layer_norm_vector(v, src, out, work, s, ready):
    for t in range(NT):
        ready(t)
        v.bn_stats(work.stats[:, t, :], src[:, t, :]).then_inc(s.stats, 1)
    v.wait_ge(s.stats, NT)
    for t in range(NT):
        v.bn_aggr(work.mv[:, t, :], work.stats[:, t, :]).then_inc(s.mv, 1)
    v.wait_ge(s.std, 1)
    v.reciprocal(work.rstd[:, :], work.std[:, :]).then_inc(s.rstd, 1)
    v.wait_ge(s.rstd, 1)
    for t in range(NT):
        v.tensor_scalar(out[:, t, :], src[:, t, :], work.mv[:, t, 0:1], work.rstd[:, t:t + 1],
                        ALU.subtract, ALU.mult).then_inc(s.out, 1)


def layer_norm_scalar(act, k, work, s):
    act.wait_ge(s.mv, NT)
    act.activation(work.std[:, :], work.mv[:, :, 1], ACT.Sqrt, bias=k.eps[:, 0:1]).then_inc(s.std, 1)


class Names:
    pass


def layer_norm_names(sem, tag):
    s = Names()
    s.stats, s.mv, s.std, s.rstd, s.out = (sem(f"{tag}_{n}") for n in ("stats", "mv", "std", "rstd", "out"))
    return s


def layer_norm_work(sb, tag):
    w = Names()
    w.stats = sb(f"{tag}_w_stats", [P, NT, 6])
    w.mv = sb(f"{tag}_w_mv", [P, NT, 2])
    w.std = sb(f"{tag}_w_std", [P, NT])
    w.rstd = sb(f"{tag}_w_rstd", [P, NT])
    return w


def turn_tensor(pe, k, src, ready, bank0, free, turned):
    for t in range(NT):
        ready(t)
        if t % 4 == 0:
            after(pe, free, t // 4 - 1)
        pe.transpose(k.ps[:, bank0 + t // 4 % 2, (t % 4) * P:(t % 4 + 1) * P], src[:, t, :],
                     k.ident[:, :]).then_inc(turned, 1)


def stage_norms(nc, sem, io, k):
    with ExitStack() as ctx:
        sb = lambda n, s, d=F32: ctx.enter_context(nc.sbuf_tensor(n, s, d))
        w0, w1 = layer_norm_work(sb, "n0"), layer_norm_work(sb, "n1")
        h = sb("h_rows", [P, NT, D])
        s0, s1 = layer_norm_names(sem, "n0"), layer_norm_names(sem, "n1")
        xn_turned, h_turned, xn_out, h_out = (sem(n) for n in ("xn_turned", "h_turned", "xn_out", "h_out"))
        with nc.Block() as block:
            @block.vector
            def _(v):
                layer_norm_vector(v, k.x, k.xn, w0, s0,
                                  lambda t: v.wait_ge(k.x_loaded[t // 8], 16) if t % 8 == 0 else None)
                layer_norm_vector(v, k.xn, h, w1, s1, lambda t: v.wait_ge(s0.out, t + 1))
                for c in range(NC):
                    v.wait_ge(h_turned, 4 * c + 4)
                    v.tensor_scalar(k.hT[:, c * CH:(c + 1) * CH], k.ps[:, 2 + c % 2, :], k.ln_cols[:, 0:1],
                                    k.ln_cols[:, 1:2], ALU.mult, ALU.add).then_inc(h_out, 1)

            @block.scalar
            def _(act):
                layer_norm_scalar(act, k, w0, s0)
                layer_norm_scalar(act, k, w1, s1)
                for c in range(NC):
                    act.wait_ge(xn_turned, 4 * c + 4)
                    act.copy(k.xnT[:, c * CH:(c + 1) * CH], k.ps[:, c % 2, :]).then_inc(xn_out, 1)

            @block.tensor
            def _(pe):
                turn_tensor(pe, k, k.xn, lambda t: pe.wait_ge(s0.out, t + 1), 0, xn_out, xn_turned)
                turn_tensor(pe, k, h, lambda t: pe.wait_ge(s1.out, t + 1), 2, h_out, h_turned)


def stage_qkv(nc, sem, k):
    with ExitStack() as ctx:
        sb = lambda n, s, d=F32: ctx.enter_context(nc.sbuf_tensor(n, s, d))
        whole = [sb(f"whole{i}", [P, 2, CH]) for i in range(2)]
        rest = [sb(f"rest{i}", [P, 2, CH]) for i in range(2)]
        part = [sb(f"part{i}", [P, 2, 3, S], BF16) for i in range(2)]
        proj, whole_out = sem("qk_proj"), sem("qk_whole")
        chain = [sem(f"qk_chain{i}") for i in range(2)]
        stored = [[sem(f"qk_stored{i}_{j}") for j in range(2)] for i in range(2)]
        v_proj, v_out, v_ones = sem("v_proj"), sem("v_out"), sem("v_ones")
        WAYS = len(TERMS)
        with nc.Block() as block:
            @block.tensor
            def _(pe):
                for c in range(NC):
                    for i in range(2):
                        after(pe, whole_out, 2 * (c - 1) + i)
                        pe.matmul(k.ps[:, 2 * (c % 2) + i, :], k.wT[:, i * P:(i + 1) * P],
                                  k.hT[:, c * CH:(c + 1) * CH], start=True, stop=True).then_inc(proj, 1)
                    after(pe, v_out, 4 * (c - 1))
                    for t in range(4 * c, 4 * c + 4):
                        pe.matmul(k.ps[:, 4 + c % 2, (t % 4) * P:(t % 4 + 1) * P], k.hT[:, t * P:(t + 1) * P],
                                  k.wT[:, 2 * P:3 * P], start=True, stop=True).then_inc(v_proj, 1)

            @block.scalar
            def _(act):
                for c in range(NC):
                    for i in range(2):
                        act.wait_ge(proj, 2 * c + i + 1)
                        after(act, chain[i], 5 * (c - 1))
                        act.activation(whole[i][:, c % 2, :], k.ps[:, 2 * (c % 2) + i, :], ACT.Identity,
                                       bias=k.bias_cols[:, i:i + 1]).then_inc(whole_out, 1)

            def split(e, i, between):
                for c in range(NC):
                    b, at = c // 2, (c % 2) * CH
                    w, r = whole[i][:, c % 2, :], rest[i][:, c % 2, :]
                    p0, p1, p2 = (part[i][:, b % 2, j, at:at + CH] for j in range(3))
                    e.wait_ge(whole_out, 2 * c + i + 1)
                    if c % 2 == 0:
                        after(e, stored[i][b % 2], 16 * WAYS * (b // 2))
                    e.tensor_copy(p0, w).then_inc(chain[i], 1)
                    e.wait_ge(chain[i], 5 * c + 1)
                    e.tensor_tensor(r, w, p0, ALU.subtract).then_inc(chain[i], 1)
                    e.wait_ge(chain[i], 5 * c + 2)
                    e.tensor_copy(p1, r).then_inc(chain[i], 1)
                    e.wait_ge(chain[i], 5 * c + 3)
                    e.tensor_tensor(p2, r, p1, ALU.subtract).then_inc(chain[i], 2)
                    between(c)

            @block.gpsimd
            def _(pool):
                split(pool, 1, lambda c: None)

            @block.vector
            def _(v):
                v.memset(k.v_rows[:, :, :, :, :, :], 1.0).then_inc(v_ones, 1)
                v.wait_ge(v_ones, 1)

                def v_rows(c):
                    v.wait_ge(v_proj, 4 * c + 4)
                    for t in range(4 * c, 4 * c + 4):
                        v.tensor_tensor(k.v_rows[:, t // TPB, :, t % TPB, :, 0:HD],
                                        k.ps[:, 4 + c % 2, (t % 4) * P:(t % 4 + 1) * P].rearrange(
                                            "p (a h d) -> p a h d", a=H // 2, h=2),
                                        k.bias_rows[:, 0:P].rearrange("p (a h d) -> p a h d", a=H // 2, h=2),
                                        ALU.add).then_inc(v_out, 1)
                split(v, 0, v_rows)

            @block.sync
            def _(sp):
                for b in range(B):
                    for i in range(2):
                        sp.wait_ge(chain[i], 5 * (2 * b + 2))
                        dst = k.split_dram[i][b * (H // 2):(b + 1) * (H // 2)].rearrange(
                            "a h (t d) s -> t (a h) d s", d=HD)
                        for t, term in enumerate(TERMS):
                            sp.dma_start(dst[t], part[i][:, b % 2, term[i], :]).then_inc(stored[i][b % 2], 16)
                for i in range(2):
                    for j in range(2):
                        sp.wait_ge(stored[i][j], 16 * WAYS * (B // 2))


MAX_UNITS = [(t, c * CH, min(CH, (t + 1) * P - c * CH), c == t * P // CH)
             for t in range(TPB) for c in range(t * P // CH + 1)]
EXP_UNITS = [(t, max(c * CH, t * P), (c + 1) * CH - max(c * CH, t * P), t * P >= c * CH)
             for c in range(S // CH) for t in range(4 * c + 4)]
NU = len(MAX_UNITS)
GROUPS = len(EXP_UNITS) // 2


def stage_attention0(nc, sem, k):
    with ExitStack() as ctx:
        sb = lambda n, s, d=F32: ctx.enter_context(nc.sbuf_tensor(n, s, d))
        Q = [sb(f"q{i}", [P, S], BF16) for i in range(4)]
        K = [sb(f"k{i}", [P, S], BF16) for i in range(4)]
        V = [sb(f"v{i}", [P, TPB, 2, HD + 1]) for i in range(4)]
        probs = sb("probs", [P, 8, CH])
        nmax = [sb(f"nmax{i}", [P, 2, TPB]) for i in range(2)]
        nmax2 = [sb(f"nmax2{i}", [P, 2, 4]) for i in range(2)]
        nrest = [sb(f"nrest{i}", [P, 2, TPB]) for i in range(2)]
        nrest2 = [sb(f"nrest2{i}", [P, 2, TPB]) for i in range(2)]
        zero = sb("zero", [P, 2, TPB])
        shift = [sb(f"shift{i}", [P, 2, 32], BF16) for i in range(2)]
        shiftT = [sb(f"shiftT{i}", [P, 2, 32], BF16) for i in range(2)]
        ev = [sb(f"ev{i}", [P, CH]) for i in range(2)]
        loaded = [sem(f"a_loaded{i}") for i in range(4)]
        shift_in = [sem(f"a_shift_in{i}") for i in range(4)]
        scored, maxed, split, shifted = sem("a_scored"), sem("a_maxed"), sem("a_split"), sem("a_shifted")
        scoredT, exped, pv_done, ev_ready = sem("a_scoredT"), sem("a_exped"), sem("a_pv"), sem("a_ev")
        ev_stored = [sem(f"a_ev_stored{i}") for i in range(2)]
        ready, joined = sem("a_ready"), sem("a_joined")
        PV = k.ps[:, 7, :]
        LOADS, SHIFTS = 16 * 5, 16 * 8

        def bodies(run):
            for j in range(4):
                run(0, j)
            with run.engine.Fori(1, PAIRS // 4 - 1) as r:
                for j in range(4):
                    run(r, j)
            for j in range(4):
                run(PAIRS // 4 - 1, j)

        def has(r, j, ahead):
            return not (isinstance(r, int) and 4 * r + j + ahead >= PAIRS)

        with nc.Block() as block:
            @block.sync
            def _(sp):
                def load(r, j):
                    p = r * 4 + j
                    r, j = r + j // 4, j % 4
                    after(sp, pv_done, (p - 3) * GROUPS)
                    for h in range(2):
                        lo = 64 * h
                        sp.dma_start(Q[j][lo:lo + QROWS, :], k.split_dram[0][bass.ds(p, 1), h]
                                     .rearrange("a r s -> (a r) s")).then_inc(loaded[j], 16)
                        sp.dma_start(K[j][lo:lo + QROWS, :], k.split_dram[1][bass.ds(p, 1), h]
                                     .rearrange("a r s -> (a r) s")).then_inc(loaded[j], 16)
                    sp.dma_start(V[j][:, :, :, :], k.v_pairs[:, bass.ds(p, 1), :, :, :]
                                 .rearrange("p a t h d -> p (a t) h d")).then_inc(loaded[j], 16)

                def put_shift(r, j):
                    p = r * 4 + j
                    r, j = r + j // 4, j % 4
                    sp.wait_ge(shifted, p + 1)
                    for h in range(2):
                        dst = Q[j][64 * h + QROWS:64 * h + SROWS, :].rearrange("r (t a i) -> r t a i", a=4, i=32)
                        for a in range(4):
                            sp.dma_start(dst[:, :, a, :], shiftT[j % 2][32 * a:32 * a + 24, h, :])\
                              .then_inc(shift_in[j], 16)

                def store(r, j, c):
                    p = r * 4 + j
                    sp.wait_ge(ev_ready, p * 2 + (c + 1))
                    for par in range(2):
                        for h in range(2):
                            g = 32 * (2 * par + h)
                            sp.dma_start(k.o_dram[par][bass.ds(p * 2 + h, 1), :, c * CH:(c + 1) * CH]
                                         .rearrange("a r s -> (a r) s"),
                                         ev[c][g:g + HD + 1, :]).then_inc(ev_stored[c], 16)

                sp.wait_ge(ready, 9)
                for j in range(3):
                    load(0, j)
                put_shift(0, 0)

                def run(r, j):
                    if not (isinstance(r, int) and r * 4 + j == 0):
                        store(r if j else r - 1, (j - 1) % 4, 1)
                    if has(r, j, 1):
                        put_shift(r, j + 1)
                    if has(r, j, 3):
                        load(r, j + 3)
                    store(r, j, 0)
                run.engine = sp
                bodies(run)
                store(PAIRS // 4 - 1, 3, 1)
                for c in range(2):
                    sp.wait_ge(ev_stored[c], 64 * PAIRS)

            @block.gpsimd
            def _(pool):
                for j in range(4):
                    pool.memset(K[j][:, :], 1.0).then_inc(ready, 1)
                pool.memset(zero[:, :, :], 0.0).then_inc(ready, 1)
                for i in range(2):
                    pool.memset(shift[i][:, :, :], 0.0).then_inc(ready, 1)
                    pool.memset(ev[i][:, :], 0.0).then_inc(ready, 1)

                def parts(r, j):
                    p = r * 4 + j
                    i = j % 2
                    part = [shift[i][:, :, 8 * n:8 * n + 8] for n in range(3)]
                    pool.wait_ge(joined, p + 1)
                    after(pool, shifted, p - 1)
                    pool.tensor_tensor(part[0], nmax[i][:, :, :], zero[:, :, :], ALU.add).then_inc(split, 1)
                    pool.wait_ge(split, p * 4 + 1)
                    pool.tensor_tensor(nrest[i][:, :, :], nmax[i][:, :, :], part[0], ALU.subtract).then_inc(split, 1)
                    pool.wait_ge(split, p * 4 + 2)
                    pool.tensor_tensor(part[1], nrest[i][:, :, :], zero[:, :, :], ALU.add).then_inc(split, 1)
                    pool.wait_ge(split, p * 4 + 3)
                    pool.tensor_tensor(part[2], nrest[i][:, :, :], part[1], ALU.subtract).then_inc(split, 1)

                parts(0, 0)
                parts(0, 1)

                def run(r, j):
                    if has(r, j, 2):
                        parts(r + (j + 2) // 4, (j + 2) % 4)
                run.engine = pool
                bodies(run)

            @block.vector
            def _(v):
                def row_max(r, j, u):
                    p = r * 4 + j
                    t, c0, n, _ = MAX_UNITS[u]
                    if u == 0:
                        after(v, split, (p - 1) * 4)
                    v.wait_ge(scored, p * NU + (u + 1))
                    out = nmax[j % 2][:, :, t:t + 1] if c0 == 0 else nmax2[j % 2][:, :, t - 4:t - 3]
                    v.tensor_reduce(out, k.ps[:, 2 * (u % 2):2 * (u % 2) + 2, 0:n], AX.X, ALU.max,
                                    negate=True).then_inc(maxed, 1)
                    if u == NU - 1:
                        v.wait_ge(maxed, (p + 1) * NU)
                        v.tensor_tensor(nmax[j % 2][:, :, 4:8], nmax[j % 2][:, :, 4:8], nmax2[j % 2][:, :, :], ALU.min)\
                         .then_inc(joined, 1)

                def turn(r, j):
                    p = r * 4 + j
                    r2, j2 = (r, j - 2) if j >= 2 else (r - 1, j + 2)
                    v.wait_ge(split, p * 4 + 4)
                    if not (isinstance(p, int) and p < 2):
                        after(v, shift_in[j2], SHIFTS * (r2 + 1))
                    v.transpose(shiftT[j % 2][:, :, :], shift[j % 2][:, :, :]).then_inc(shifted, 1)

                def evacuate(r, j, c):
                    p = r * 4 + j
                    after(v, ev_stored[c], p * 64)
                    v.wait_ge(pv_done, p * GROUPS + (2 if c == 0 else GROUPS))
                    if c == 0:
                        v.tensor_copy(ev[0][0:64, 0:P], PV[0:64, 0:P])
                        v.tensor_copy(ev[0][:, P:CH], PV[:, P:CH]).then_inc(ev_ready, 1)
                    else:
                        v.tensor_copy(ev[1][:, :], PV[:, :]).then_inc(ev_ready, 1)

                v.wait_ge(ready, 9)
                v.memset(PV, 0.0).then_inc(ready, 1)
                for j in range(2):
                    for u in range(NU):
                        row_max(0, j, u)
                turn(0, 0)

                def run(r, j):
                    for u in range(NU):
                        if has(r, j, 2):
                            row_max(r + (j + 2) // 4, (j + 2) % 4, u)
                        if u == 2 and has(r, j, 1):
                            turn(r + (j + 1) // 4, (j + 1) % 4)
                        if u == 5:
                            evacuate(r, j, 0)
                    evacuate(r, j, 1)
                run.engine = v
                bodies(run)

            @block.scalar
            def _(act):
                def run(r, j):
                    p = r * 4 + j
                    for e in range(4 * GROUPS):
                        n = EXP_UNITS[e // 2][2]
                        if e % 4 == 0:
                            after(act, pv_done, p * GROUPS + (e // 4 - 1))
                        act.wait_ge(scoredT, p * (4 * GROUPS) + (e + 1))
                        act.activation(probs[:, e % 8, 0:n], k.ps[:, 4 + e % 3, 0:n], ACT.Exp,
                                       scale=float(HD) ** -0.5).then_inc(exped, 1)
                run.engine = act
                bodies(run)

            @block.tensor
            def _(pe):
                def scores(r, j, u):
                    p = r * 4 + j
                    t, c0, n, diag = MAX_UNITS[u]
                    out = [k.ps[:, 2 * (u % 2) + h, :] for h in range(2)]
                    if u == 0:
                        pe.wait_ge(loaded[j], LOADS * (r + 1))
                    after(pe, maxed, p * NU + (u - 1))
                    pe.wait_ge(ready, 10)
                    for h in range(2):
                        lo = 64 * h
                        mm = pe.matmul(out[h][:, 0:n], Q[j][lo:lo + QROWS, t * P:(t + 1) * P],
                                       K[j][lo:lo + QROWS, c0:c0 + n], start=True, stop=True)
                    if diag:
                        for a in range(2):
                            for h in range(2):
                                lo = 64 * h
                                mm = pe.matmul(out[h][:, n - P + 64 * a:n], k.half_ident[lo:lo + 64, a, :],
                                               k.half_mask[lo:lo + 64, a, 64 * a:P], start=False, stop=True,
                                               skip_group_check=True)
                    mm.then_inc(scored, 1)

                def scores_t(r, j, u):
                    p = r * 4 + j
                    t, q0, n, diag = EXP_UNITS[u]
                    out = [k.ps[:, 4 + (2 * u + h) % 3, :] for h in range(2)]
                    if u == 0:
                        pe.wait_ge(shift_in[j], SHIFTS * (r + 1))
                    for h in range(2):
                        lo = 64 * h
                        after(pe, exped, p * (4 * GROUPS) + (2 * u + h - 2))
                        pe.wait_ge(ready, 10)
                        mm = pe.matmul(out[h][:, 0:n], K[j][lo:lo + SROWS, t * P:(t + 1) * P],
                                       Q[j][lo:lo + SROWS, q0:q0 + n], start=True, stop=True)
                        if not diag:
                            mm.then_inc(scoredT, 1)
                    if diag:
                        for a in range(2):
                            for h in range(2):
                                lo = 64 * h
                                mm = pe.matmul(out[h][:, 0:64 + 64 * a], k.half_ident[lo:lo + 64, a, :],
                                               k.half_maskT[lo:lo + 64, a, 0:64 + 64 * a], start=False,
                                               stop=True, skip_group_check=True)
                                if a == 1:
                                    mm.then_inc(scoredT, 1)

                def weigh(r, j, g):
                    p = r * 4 + j
                    pe.wait_ge(exped, p * (4 * GROUPS) + 4 * (g + 1))
                    if g in (0, 2):
                        after(pe, ev_ready, p * 2 + (1 if g else 0))
                    for par in range(2):
                        t, q0, n, _ = EXP_UNITS[2 * g + par]
                        for h in range(2):
                            e = 4 * g + 2 * par + h
                            lo = 32 * (2 * par + h)
                            mm = pe.matmul(PV[lo:lo + HD + 1, CH - n:CH], V[j][:, t, h, :], probs[:, e % 8, 0:n],
                                           start=(g in (0, 2)), stop=True, skip_group_check=True)
                    mm.then_inc(pv_done, 1)

                for j in range(2):
                    for u in range(NU):
                        scores(0, j, u)

                def run(r, j):
                    for u in range(NU):
                        scores_t(r, j, u)
                        if has(r, j, 2):
                            if u:
                                scores(r + (j + 2) // 4, (j + 2) % 4, u - 1)
                            if u == NU - 1:
                                scores(r + (j + 2) // 4, (j + 2) % 4, u)
                        if u % 2 and u > 1:
                            weigh(r, j, u // 2 - 1)
                    weigh(r, j, GROUPS - 1)
                run.engine = pe
                bodies(run)


def stage_project(nc, sem, k):
    with ExitStack() as ctx:
        sb = lambda n, s, d=F32: ctx.enter_context(nc.sbuf_tensor(n, s, d))
        even, odd, over = sb("o_even", [P, T]), sb("o_odd", [P, T]), sb("o_over", [P, T])
        sums = sb("sums", [P, 2, CH])
        rsum = sb("rsum", [P, CH])
        in_sums, in_o, in_over = sem("p_in_sums"), [sem(f"p_in_o{b}") for b in range(B)], sem("p_in_over")
        total, inverse, joined, normed, rstored = (sem(f"p_{n}") for n in ("total", "inverse", "joined", "normed", "rstored"))
        proj, biased, hs_out = sem("p_proj"), sem("p_biased"), sem("p_hs")
        with nc.Block() as block:
            @block.sync
            def _(sp):
                for par in range(2):
                    sp.dma_start(sums[:, par, :], k.o_dram[par][:, HD, :].rearrange("g (c s) -> g c s", s=CH))\
                      .then_inc(in_sums, 16)
                for b in range(B):
                    for par, dst in enumerate((even, odd)):
                        sp.dma_start(dst[:, b * S:(b + 1) * S], k.o_dram[par][b * H:(b + 1) * H, 0:HD, :])\
                          .then_inc(in_o[b], 16)
                sp.wait_ge(inverse, 1)
                sp.dma_start(k.r_dram.rearrange("g (c s) -> g c s", s=CH), rsum[:, :]).then_inc(rstored, 16)
                sp.wait_ge(rstored, 16)
                for b in range(B):
                    src = k.r_dram[b * H:(b + 1) * H, :].unsqueeze(1).broadcast_to([H, HD, S])
                    sp.dma_start(over[:, b * S:(b + 1) * S], src).then_inc(in_over, 16)

            @block.vector
            def _(v):
                v.wait_ge(in_sums, 32)
                v.tensor_tensor(sums[:, 0, :], sums[:, 0, :], sums[:, 1, :], ALU.add).then_inc(total, 1)
                v.wait_ge(total, 1)
                v.reciprocal(rsum[:, :], sums[:, 0, :]).then_inc(inverse, 1)
                v.wait_ge(in_over, 64)
                for b in range(B):
                    at = slice(b * S, (b + 1) * S)
                    v.wait_ge(joined, b + 1)
                    v.tensor_tensor(even[:, at], even[:, at], over[:, at], ALU.mult).then_inc(normed, 1)
                for c in range(NC):
                    v.wait_ge(proj, 4 * c + 4)
                    rows = k.hs[:, 4 * c:4 * c + 4, :]
                    v.tensor_tensor(rows, k.ps[:, c % 2, :].rearrange("p (t d) -> p t d", d=D),
                                    k.xn[:, 4 * c:4 * c + 4, :], ALU.add).then_inc(biased, 1)
                    for t in range(4 * c, 4 * c + 4):
                        if t % 4 == 0:
                            v.wait_ge(biased, c + 1)
                        v.tensor_tensor(k.hs[:, t, :], k.hs[:, t, :], k.bias_rows[:, P:2 * P], ALU.add)\
                         .then_inc(hs_out, 1)

            @block.gpsimd
            def _(pool):
                for b in range(B):
                    at = slice(b * S, (b + 1) * S)
                    pool.wait_ge(in_o[b], 32)
                    pool.tensor_tensor(even[:, at], even[:, at], odd[:, at], ALU.add).then_inc(joined, 1)

            @block.tensor
            def _(pe):
                for t in range(NT):
                    pe.wait_ge(normed, t // TPB + 1)
                    if t % 4 == 0:
                        after(pe, biased, t // 4 - 1)
                    pe.matmul(k.ps[:, t // 4 % 2, (t % 4) * P:(t % 4 + 1) * P], even[:, t * P:(t + 1) * P],
                              k.wT[:, W_CP:W_CP + P], start=True, stop=True).then_inc(proj, 1)

    with ExitStack() as ctx:
        sb = lambda n, s, d=F32: ctx.enter_context(nc.sbuf_tensor(n, s, d))
        w = layer_norm_work(sb, "n2")
        s = layer_norm_names(sem, "n2")
        rows = sb("h2_rows", [P, NT, D])
        hT = sb("h2T", [P, T])
        mid = sb("mid", [P, 4, CH])
        turned, hT_out, up, act_out, down, summed, s_out = (sem(f"m_{n}") for n in ("turned", "hT", "up", "act", "down", "summed", "s"))
        with nc.Block() as block:
            @block.vector
            def _(v):
                layer_norm_vector(v, k.hs, rows, w, s, lambda t: None)
                for c in range(NC):
                    v.wait_ge(turned, 4 * c + 4)
                    v.tensor_scalar(hT[:, c * CH:(c + 1) * CH], k.ps[:, c % 2, :], k.ln_cols[:, 2:3],
                                    k.ln_cols[:, 3:4], ALU.mult, ALU.add).then_inc(hT_out, 1)
                for c in range(NC):
                    v.wait_ge(down, c + 1)
                    v.tensor_tensor(k.hs[:, 4 * c:4 * c + 4, :], k.hs[:, 4 * c:4 * c + 4, :],
                                    k.ps[:, 6 + c % 2, :].rearrange("p (t d) -> p t d", d=D), ALU.add).then_inc(summed, 1)
                    v.wait_ge(summed, c + 1)
                    for t in range(4 * c, 4 * c + 4):
                        v.tensor_tensor(k.hs[:, t, :], k.hs[:, t, :], k.bias_rows[:, 2 * P:3 * P], ALU.add)\
                         .then_inc(s_out, 1)

            @block.scalar
            def _(act):
                layer_norm_scalar(act, k, w, s)
                for c in range(NC):
                    for i in range(NI):
                        n = NI * c + i
                        act.wait_ge(up, n + 1)
                        after(act, down, c)
                        act.activation(mid[:, i, :], k.ps[:, 2 + n % 4, :], ACT.Gelu_apprx_tanh,
                                       bias=k.bias_cols[:, 4 + i:5 + i]).then_inc(act_out, 1)

            @block.tensor
            def _(pe):
                turn_tensor(pe, k, rows, lambda t: pe.wait_ge(s.out, t + 1), 0, hT_out, turned)
                for c in range(NC):
                    pe.wait_ge(hT_out, c + 1)
                    for i in range(NI):
                        n = NI * c + i
                        after(pe, act_out, n - 3)
                        pe.matmul(k.ps[:, 2 + n % 4, :], k.wT[:, W_CF + i * P:W_CF + (i + 1) * P],
                                  hT[:, c * CH:(c + 1) * CH], start=True, stop=True).then_inc(up, 1)
                    pe.wait_ge(act_out, NI * c + NI)
                    after(pe, summed, c - 1)
                    for t in range(4):
                        for i in range(NI):
                            mm = pe.matmul(k.ps[:, 6 + c % 2, t * P:(t + 1) * P], mid[:, i, t * P:(t + 1) * P],
                                           k.wT[:, W_CM + i * P:W_CM + (i + 1) * P], start=(i == 0), stop=(i == NI - 1))
                    mm.then_inc(down, 1)


CYCLES = 3


def stage_gate0(nc, sem, io, k):
    with ExitStack() as ctx:
        sb = lambda n, s, d=F32: ctx.enter_context(nc.sbuf_tensor(n, s, d))
        w1, w2, w3, w4 = sb("cn1", [P, 128]), sb("cn2", [P, 64]), sb("cn3", [64, 32]), sb("cn4", [32, 1])
        b1, b2, b3, b4 = sb("cb1", [P, 1]), sb("cb2", [64, 1]), sb("cb3", [32, 1]), sb("cb4", [P, 1])
        u1, u2, u3 = sb("gc1", [P, 64]), sb("gc2", [64, 32]), sb("gc3", [32, 1])
        d1, d2, d3 = sb("gb1", [64, 1]), sb("gb2", [32, 1]), sb("gb3", [P, 1])
        w4w, u3w = sb("cn4w", [32, P]), sb("gc3w", [32, P])
        rng = sb("range", [P, 1])
        mean, g1, g2, gf = sb("mean", [P, B]), sb("g1", [64, B]), sb("g2", [32, B]), sb("gf", [P, B])
        c0, c1 = sb("c0", [P, B]), sb("c1", [P, 1])
        a1, a2, a3 = sb("a1", [P, CH]), sb("a2", [64, CH]), sb("a3", [32, CH])
        z = sb("z", [P, T])
        move = sb("move", [P, 2, CH])
        pre = [(w1, io["L0_ffn_cn_w1"]), (w2, io["L0_ffn_cn_w2"]), (w3, io["L0_ffn_cn_w3"]), (w4, io["L0_ffn_cn_w4"]),
               (u1, io["L0_ffn_gc_w1"]), (u2, io["L0_ffn_gc_w2"]), (u3, io["L0_ffn_gc_w3"])]
        pre = [(a[:, :], b) for a, b in pre]
        pre += [(a[:, :], io["L0_ffn_" + n].rearrange("(p a) -> p a", a=1)) for a, n in
                ((b1, "cn_b1"), (b2, "cn_b2"), (b3, "cn_b3"), (d1, "gc_b1"), (d2, "gc_b2"))]
        pre += [(a[:, :], io["L0_ffn_" + n].partition_broadcast(P)) for a, n in
                ((b4, "cn_b4"), (d3, "gc_b3"), (rng, "adaptive_range"))]
        loaded, small, gl_mm, gl_act, coef = (sem(f"g_{n}") for n in ("loaded", "small", "gl_mm", "gl_act", "coef"))
        mm1, mm2, mm3, mm4 = (sem(f"g_mm{i}") for i in range(4))
        ac1, ac2, ac3, z_out, tf_out, twisted, moved, stepped, coupled = (
            sem(f"g_{n}") for n in ("ac1", "ac2", "ac3", "z", "tf", "twisted", "moved", "stepped", "coupled"))
        with nc.Block() as block:
            @block.sync
            def _(sp):
                for dst, src in pre:
                    sp.dma_start(dst, src).then_inc(loaded, 16)

            @block.vector
            def _(v):
                v.wait_ge(loaded, 16 * len(pre))
                v.tensor_scalar(w4w[:, :], k.ones_row[0:32, :], w4[:, 0:1], None, ALU.mult).then_inc(small, 1)
                v.tensor_scalar(u3w[:, :], k.ones_row[0:32, :], u3[:, 0:1], None, ALU.mult).then_inc(small, 1)
                v.tensor_reduce(mean[:, :], k.xnT[:, :].rearrange("p (b s) -> p b s", s=S), AX.X, ALU.add).then_inc(small, 1)
                v.wait_ge(small, 3)
                v.tensor_scalar(mean[:, :], mean[:, :], 1.0 / S, None, ALU.mult).then_inc(small, 1)
                v.wait_ge(gl_act, 3)
                v.tensor_scalar(c0[:, :], gf[:, :], 1.4, -1.0, ALU.mult, ALU.add).then_inc(coef, 1)
                v.wait_ge(coef, 1)
                v.tensor_scalar(c0[:, :], c0[:, :], rng[:, 0:1], 0.1, ALU.mult, ALU.add).then_inc(coef, 1)
                v.tensor_scalar(c1[:, :], rng[:, :], 0.6, None, ALU.mult).then_inc(coef, 1)
                v.wait_ge(coef, 3)
                for y in range(CYCLES):
                    for c in range(NC):
                        n = y * NC + c
                        v.wait_ge(mm4, n + 1)
                        after(v, moved, n - NC + 1)
                        v.tensor_copy(z[:, c * CH:(c + 1) * CH], k.ps[:, 6, :]).then_inc(z_out, 1)
                    for c in range(NC):
                        n = y * NC + c
                        at = slice(c * CH, (c + 1) * CH)
                        v.wait_ge(tf_out, y + 1)
                        v.tensor_scalar(z[:, at], z[:, at], c1[:, 0:1], c0[:, c // 2:c // 2 + 1], ALU.mult, ALU.add)\
                         .then_inc(coupled, 1)
                        v.wait_ge(twisted, n + 1)
                        v.wait_ge(coupled, n + 1)
                        after(v, stepped, n - 1)
                        v.tensor_tensor(move[:, c % 2, :], z[:, at], k.ps[:, c % 2, :], ALU.mult).then_inc(moved, 1)

            @block.gpsimd
            def _(pool):
                for n in range(CYCLES * NC):
                    at = slice(n % NC * CH, (n % NC + 1) * CH)
                    pool.wait_ge(moved, n + 1)
                    pool.tensor_tensor(k.xnT[:, at], k.xnT[:, at], move[:, n % 2, :], ALU.add).then_inc(stepped, 1)

            @block.scalar
            def _(act):
                for src, dst, b, f, rows, n in ((2, g1, d1, ACT.Gelu, 64, 1), (3, g2, d2, ACT.Gelu, 32, 2),
                                                (4, gf, d3, ACT.Sigmoid, P, 3)):
                    act.wait_ge(gl_mm, n)
                    act.activation(dst[:, :], k.ps[0:rows, src, 0:B], f, bias=b[:, 0:1]).then_inc(gl_act, 1)
                for y in range(CYCLES):
                    for c in range(NC):
                        n = y * NC + c
                        for bank, dst, b, rows, mm, ac, used in ((2 + n % 2, a1, b1, P, mm1, ac1, mm2),
                                                                 (4, a2, b2, 64, mm2, ac2, mm3),
                                                                 (5, a3, b3, 32, mm3, ac3, mm4)):
                            act.wait_ge(mm, n + 1)
                            after(act, used, n)
                            act.activation(dst[:, :], k.ps[0:rows, bank, :], ACT.Gelu, bias=b[:, 0:1]).then_inc(ac, 1)
                    act.wait_ge(z_out, (y + 1) * NC)
                    act.activation(z[:, :], z[:, :], ACT.Sigmoid, bias=b4[:, 0:1]).then_inc(tf_out, 1)

            @block.tensor
            def _(pe):
                pe.wait_ge(small, 4)
                pe.matmul(k.ps[0:64, 2, 0:B], u1[:, :], mean[:, :], start=True, stop=True).then_inc(gl_mm, 1)
                pe.wait_ge(gl_act, 1)
                pe.matmul(k.ps[0:32, 3, 0:B], u2[:, :], g1[:, :], start=True, stop=True).then_inc(gl_mm, 1)
                pe.wait_ge(gl_act, 2)
                pe.matmul(k.ps[:, 4, 0:B], u3w[:, :], g2[:, :], start=True, stop=True).then_inc(gl_mm, 1)
                pe.wait_ge(gl_act, 3)
                for y in range(CYCLES):
                    for c in range(NC + 1):
                        n = y * NC + c
                        if c < NC:
                            after(pe, stepped, n - NC + 1)
                            after(pe, ac1, n - 1)
                            pe.matmul(k.ps[:, 2 + n % 2, :], w1[:, :], k.xnT[:, c * CH:(c + 1) * CH], start=True,
                                      stop=True).then_inc(mm1, 1)
                        if c:
                            n -= 1
                            pe.wait_ge(ac1, n + 1)
                            after(pe, ac2, n)
                            pe.matmul(k.ps[0:64, 4, :], w2[:, :], a1[:, :], start=True, stop=True).then_inc(mm2, 1)
                            pe.wait_ge(ac2, n + 1)
                            after(pe, ac3, n)
                            pe.matmul(k.ps[0:32, 5, :], w3[:, :], a2[:, :], start=True, stop=True).then_inc(mm3, 1)
                            pe.wait_ge(ac3, n + 1)
                            after(pe, z_out, n)
                            pe.matmul(k.ps[:, 6, :], w4w[:, :], a3[:, :], start=True, stop=True).then_inc(mm4, 1)
                    for c in range(NC):
                        n = y * NC + c
                        after(pe, moved, n - 1)
                        pe.matmul(k.ps[:, c % 2, :], k.perm[:, :], k.xnT[:, c * CH:(c + 1) * CH], start=True,
                                  stop=True).then_inc(twisted, 1)
    stage_gate(nc, sem, k, "g0", k.xnT)


def stage_gate(nc, sem, k, tag, outT):
    with ExitStack() as ctx:
        sb = lambda n, s, d=F32: ctx.enter_context(nc.sbuf_tensor(n, s, d))
        sig, rows = sb(tag + "sig", [P, 2, CH]), sb(tag + "rows", [P, 2, CH])
        turned, sig_out, gated, weighed, added = (sem(f"{tag}_{n}") for n in ("turned", "sig", "gated", "weighed", "added"))
        with nc.Block() as block:
            @block.tensor
            def _(pe):
                for t in range(NT):
                    if t % 4 == 0:
                        after(pe, gated, t // 4 - 1)
                    pe.transpose(k.ps[:, t // 4 % 2, (t % 4) * P:(t % 4 + 1) * P], outT[:, t * P:(t + 1) * P],
                                 k.ident[:, :]).then_inc(turned, 1)

            @block.scalar
            def _(act):
                for c in range(NC):
                    act.wait_ge(turned, 4 * c + 4)
                    after(act, gated, c - 1)
                    act.activation(sig[:, c % 2, :], k.ps[:, c % 2, :], ACT.Sigmoid).then_inc(sig_out, 1)

            @block.vector
            def _(v):
                for c in range(NC):
                    v.wait_ge(sig_out, c + 1)
                    after(v, weighed, c - 1)
                    v.tensor_tensor(rows[:, c % 2, :], sig[:, c % 2, :], k.ps[:, c % 2, :], ALU.mult).then_inc(gated, 1)

            @block.gpsimd
            def _(pool):
                for c in range(NC):
                    r = rows[:, c % 2, :].rearrange("p (t d) -> p t d", d=D)
                    at = slice(4 * c, 4 * c + 4)
                    pool.wait_ge(gated, c + 1)
                    pool.tensor_tensor(k.hs[:, at, :], r, k.hs[:, at, :], ALU.mult).then_inc(weighed, 1)
                    pool.wait_ge(weighed, c + 1)
                    pool.tensor_tensor(k.x[:, at, :], k.x[:, at, :], k.hs[:, at, :], ALU.add).then_inc(added, 1)


def stage_attention1(nc, sem, k):
    with ExitStack() as ctx:
        sb = lambda n, s, d=F32: ctx.enter_context(nc.sbuf_tensor(n, s, d))
        w = layer_norm_work(sb, "n3")
        s = layer_norm_names(sem, "n3")
        turned, xnT_out = sem("n3_turned"), sem("n3_T")
        with nc.Block() as block:
            @block.vector
            def _(v):
                layer_norm_vector(v, k.x, k.xn, w, s, lambda t: None)

            @block.scalar
            def _(act):
                layer_norm_scalar(act, k, w, s)
                for c in range(NC):
                    act.wait_ge(turned, 4 * c + 4)
                    act.copy(k.xnT[:, c * CH:(c + 1) * CH], k.ps[:, c % 2, :]).then_inc(xnT_out, 1)

            @block.tensor
            def _(pe):
                turn_tensor(pe, k, k.xn, lambda t: pe.wait_ge(s.out, t + 1), 0, xnT_out, turned)

    with ExitStack() as ctx:
        sb = lambda n, s, d=F32: ctx.enter_context(nc.sbuf_tensor(n, s, d))
        qT, kT = sb("qT", [P, T]), sb("kT", [P, T])
        vr = sb("vr", [P, NT, D])
        probs = sb("probs1", [P, 2, S])
        probsT = sb("probsT1", [P, 2, S])
        outT = sb("outT1", [P, 2, P])
        nmax, bias, sums, inv = (sb("l1_" + n, [P, NT]) for n in ("nmax", "bias", "sums", "inv"))
        qk, qk_out, vv, v_out = (sem(f"l_{n}") for n in ("qk", "qk_out", "v", "v_out"))
        scored, maxed, biased, exped, inverse, normed, turned, turned_out, pv, pv_out, last, last_out = (
            sem(f"l_{n}") for n in ("scored", "maxed", "biased", "exped", "inverse", "normed", "turned", "turned_out",
                                    "pv", "pv_out", "last", "last_out"))
        with nc.Block() as block:
            @block.tensor
            def _(pe):
                for c in range(NC):
                    for i in range(2):
                        after(pe, qk_out, 2 * (c - 1) + i)
                        pe.matmul(k.ps[:, 2 * (c % 2) + i, :], k.wT[:, 1536 + i * P:1536 + (i + 1) * P],
                                  k.xnT[:, c * CH:(c + 1) * CH], start=True, stop=True).then_inc(qk, 1)
                    after(pe, v_out, c - 1)
                    for t in range(4 * c, 4 * c + 4):
                        pe.matmul(k.ps[:, 4 + c % 2, (t % 4) * P:(t % 4 + 1) * P], k.xnT[:, t * P:(t + 1) * P],
                                  k.wT[:, 1536 + 2 * P:1536 + 3 * P], start=True, stop=True).then_inc(vv, 1)

            @block.scalar
            def _(act):
                for c in range(NC):
                    for i, dst in enumerate((qT, kT)):
                        act.wait_ge(qk, 2 * c + i + 1)
                        act.copy(dst[:, c * CH:(c + 1) * CH], k.ps[:, 2 * (c % 2) + i, :]).then_inc(qk_out, 1)

            @block.vector
            def _(v):
                for c in range(NC):
                    v.wait_ge(vv, 4 * c + 4)
                    v.tensor_copy(vr[:, 4 * c:4 * c + 4, :], k.ps[:, 4 + c % 2, :].rearrange("p (t d) -> p t d", d=D))\
                     .then_inc(v_out, 1)

        SC = float(D) ** -0.5
        turns = []
        for t in range(NT):
            q = t % TPB
            turns += [(t, a, min(4, q + 1 - a)) for a in range(0, q + 1, 4)]
        upto = [sum(1 for x in turns if x[0] <= t) for t in range(NT)]
        with nc.Block() as block:
            @block.tensor
            def _(pe):
                def score(t):
                    b, q = t // TPB, t % TPB
                    n = (q + 1) * P
                    after(pe, exped, t - 1)
                    for c in range(0, n, CH):
                        m = min(CH, n - c)
                        diag = c + m == n
                        mm = pe.matmul(k.ps[:, 2 * (t % 2) + c // CH, 0:m], qT[:, t * P:(t + 1) * P],
                                       kT[:, b * S + c:b * S + c + m], start=True, stop=True)
                        if diag:
                            mm = pe.matmul(k.ps[:, 2 * (t % 2) + c // CH, m - P:m], k.identb[:, :], k.mask[:, :],
                                           start=False, stop=True, skip_group_check=True)
                    mm.then_inc(scored, 1)

                def weigh(t):
                    b, q = t // TPB, t % TPB
                    pe.wait_ge(turned_out, upto[t])
                    after(pe, pv_out, t)
                    for a in range(q + 1):
                        mm = pe.matmul(k.ps[:, 6, 0:P], vr[:, b * TPB + a, :], probsT[:, t % 2, a * P:(a + 1) * P],
                                       start=(a == 0), stop=(a == q))
                    mm.then_inc(pv, 1)

                def project(t):
                    pe.wait_ge(pv_out, t + 1)
                    after(pe, last_out, t)
                    pe.matmul(k.ps[:, 7, 0:P], outT[:, t % 2, :], k.wT[:, 1536 + 3 * P:1536 + 4 * P], start=True,
                              stop=True).then_inc(last, 1)

                score(0)
                n = 0
                for t in range(NT):
                    if t + 1 < NT:
                        score(t + 1)
                    if t:
                        weigh(t - 1)
                    pe.wait_ge(normed, t + 1)
                    while n < len(turns) and turns[n][0] == t:
                        _, a, m = turns[n]
                        after(pe, turned_out, n - 1)
                        for i in range(m):
                            mm = pe.transpose(k.ps[:, 4 + n % 2, i * P:(i + 1) * P],
                                              probs[:, t % 2, (a + i) * P:(a + i + 1) * P], k.ident[:, :])
                        mm.then_inc(turned, 1)
                        n += 1
                    if t:
                        project(t - 1)
                weigh(NT - 1)
                project(NT - 1)

            @block.vector
            def _(v):
                for t in range(NT):
                    n = (t % TPB + 1) * P
                    v.wait_ge(scored, t + 1)
                    v.tensor_reduce(nmax[:, t:t + 1], k.ps[:, 2 * (t % 2):2 * (t % 2) + 2, :].rearrange("p a n -> p (a n)")[:, 0:n],
                                    AX.X, ALU.max, negate=True).then_inc(maxed, 1)
                    v.wait_ge(maxed, t + 1)
                    v.tensor_scalar(bias[:, t:t + 1], nmax[:, t:t + 1], SC, None, ALU.mult).then_inc(biased, 1)
                    v.wait_ge(exped, t + 1)
                    v.reciprocal(inv[:, t:t + 1], sums[:, t:t + 1]).then_inc(inverse, 1)
                    v.wait_ge(inverse, t + 1)
                    v.tensor_scalar(probs[:, t % 2, 0:n], probs[:, t % 2, 0:n], inv[:, t:t + 1], None, ALU.mult)\
                     .then_inc(normed, 1)
                    if t:
                        v.wait_ge(last, t)
                        v.tensor_copy(k.hs[:, t - 1, :], k.ps[:, 7, 0:P]).then_inc(last_out, 1)
                v.wait_ge(last, NT)
                v.tensor_copy(k.hs[:, NT - 1, :], k.ps[:, 7, 0:P]).then_inc(last_out, 1)

            @block.scalar
            def _(act):
                n = 0

                def pv_copy(t):
                    act.wait_ge(pv, t + 1)
                    after(act, last, t - 1)
                    act.copy(outT[:, t % 2, :], k.ps[:, 6, 0:P]).then_inc(pv_out, 1)

                for t in range(NT):
                    m = (t % TPB + 1) * P
                    act.wait_ge(biased, t + 1)
                    after(act, turned, upto[t - 2] if t >= 2 else 0)
                    act.activation(probs[:, t % 2, 0:m], k.ps[:, 2 * (t % 2):2 * (t % 2) + 2, :].rearrange("p a n -> p (a n)")[:, 0:m],
                                   ACT.Exp, bias=bias[:, t:t + 1], scale=SC, accum_out=sums[:, t:t + 1]).then_inc(exped, 1)
                    if t:
                        pv_copy(t - 1)
                    while n < len(turns) and turns[n][0] == t:
                        _, a, mm = turns[n]
                        act.wait_ge(turned, n + 1)
                        after(act, pv, t - 1)
                        act.copy(probsT[:, t % 2, a * P:(a + mm) * P], k.ps[:, 4 + n % 2, 0:mm * P]).then_inc(turned_out, 1)
                        n += 1
                pv_copy(NT - 1)


def stage_experts(nc, sem, io, k, out):
    with ExitStack() as ctx:
        sb = lambda n, s, d=F32: ctx.enter_context(nc.sbuf_tensor(n, s, d))
        wg = sb("wg", [P, NE])
        expert = sb("expert", [P, NT, NE])
        hundred = sb("hundred", [P, NT, NE])
        logit, best = sb("logit", [P, NT, NE]), sb("best", [P, NT])
        choice = sb("choice", [P, NT])
        chosen = sb("chosen", [P, T])
        W1, W2 = sb("W1", [P, NE + 1, INTER]), sb("W2", [P, NE + 1, INTER])
        W3 = sb("W3", [P, NE + 1, NI, D])
        loaded, wg_in, counted, scored, step, stored, spread = (
            sem(f"e_{n}") for n in ("loaded", "wg_in", "counted", "scored", "step", "stored", "spread"))
        with nc.Block() as block:
            @block.sync
            def _(sp):
                sp.dma_start(wg[:, :], io["L1_ffn_Wg"]).then_inc(wg_in, 16)
                sp.dma_start(W1[:, 0, :], io["L1_ffn_w1s"]).then_inc(loaded, 16)
                sp.dma_start(W2[:, 0, :], io["L1_ffn_w2s"]).then_inc(loaded, 16)
                sp.dma_start(W3[:, 0, :, :], io["L1_ffn_w3s"].rearrange("(c p) d -> p c d", p=P)).then_inc(loaded, 16)
                for e in range(NE):
                    sp.dma_start(W1[:, e + 1, :], io["L1_ffn_W1"][e]).then_inc(loaded, 16)
                    sp.dma_start(W2[:, e + 1, :], io["L1_ffn_W2"][e]).then_inc(loaded, 16)
                    sp.dma_start(W3[:, e + 1, :, :], io["L1_ffn_W3"][e].rearrange("(c p) d -> p c d", p=P)).then_inc(loaded, 16)
                sp.wait_ge(step, 7)
                sp.dma_start(k.choice_dram.rearrange("(t p) -> p t", p=P), choice[:, :]).then_inc(stored, 16)
                sp.wait_ge(stored, 16)
                sp.dma_start(chosen[:, :], k.choice_dram.partition_broadcast(P)).then_inc(spread, 16)
                sp.wait_ge(spread, 16)
                sp.wait_ge(loaded, 16 * 3 * (NE + 1))

            @block.gpsimd
            def _(pool):
                for e in range(NE):
                    pool.memset(expert[:, :, e:e + 1], float(e)).then_inc(counted, 1)

            @block.tensor
            def _(pe):
                pe.wait_ge(wg_in, 16)
                for t in range(NT):
                    pe.matmul(k.ps[:, 0, t * NE:(t + 1) * NE], k.xnT[:, t * P:(t + 1) * P], wg[:, :], start=True,
                              stop=True).then_inc(scored, 1)

            @block.vector
            def _(v):
                v.wait_ge(scored, NT)
                v.tensor_copy(logit[:, :, :], k.ps[:, 0, 0:NT * NE].rearrange("p (t e) -> p t e", e=NE)).then_inc(step, 1)
                v.wait_ge(step, 1)
                v.tensor_reduce(best[:, :], logit[:, :, :], AX.X, ALU.max).then_inc(step, 1)
                v.wait_ge(step, 2)
                v.tensor_tensor(logit[:, :, :], logit[:, :, :], best[:, :].unsqueeze(2).broadcast_to([P, NT, NE]),
                                ALU.is_equal).then_inc(step, 1)
                v.wait_ge(counted, NE)
                v.tensor_scalar(hundred[:, :, :], expert[:, :, :], -1.0, float(NE), ALU.mult, ALU.add).then_inc(step, 1)
                v.wait_ge(step, 4)
                v.tensor_tensor(logit[:, :, :], logit[:, :, :], hundred[:, :, :], ALU.mult).then_inc(step, 1)
                v.wait_ge(step, 5)
                v.tensor_reduce(best[:, :], logit[:, :, :], AX.X, ALU.max).then_inc(step, 1)
                v.wait_ge(step, 6)
                v.tensor_scalar(choice[:, :], best[:, :], -1.0, float(NE), ALU.mult, ALU.add).then_inc(step, 1)

        xc = sb("xc", [P, 2, CH])
        gel = sb("gel", [P, 3, CH])
        hid = sb("hid", [P, 3, CH])
        sig, rows = sb("e_sig", [P, CH]), sb("e_rows", [P, CH])
        picked, up, gel_out, hid_out, down, sig_out, gated, weighed, added, sent = (
            sem(f"e_{n}") for n in ("picked", "up", "gelu", "hid", "down", "sig", "gated", "weighed", "added", "sent"))
        E1 = NE + 1
        U = E1 * NI
        ov = tokens(out)
        with nc.Block() as block:
            @block.tensor
            def _(pe):
                def lower(c, u):
                    e, i = u // NI, u % NI
                    n = c * U + u
                    pe.wait_ge(hid_out, n + 1)
                    if u == 0:
                        after(pe, gated, c)
                    for t in range(4):
                        mm = pe.matmul(k.ps[:, 6, t * P:(t + 1) * P], hid[:, u % 3, t * P:(t + 1) * P], W3[:, e, i, :],
                                       start=(u == 0 and t == 0), stop=True, skip_group_check=True)
                    mm.then_inc(down, 1)

                with pe.Fori(0, NC) as c:
                    for u in range(U):
                        e, i = u // NI, u % NI
                        n = c * U + u
                        if i == 0:
                            pe.wait_ge(picked, c * E1 + (e + 1))
                        if u >= 3:
                            pe.wait_ge(hid_out, n - 2)
                        for b, w in ((2 * (u % 3), W1), (2 * (u % 3) + 1, W2)):
                            mm = pe.matmul(k.ps[:, b, :], w[:, e, i * P:(i + 1) * P], xc[:, e % 2, :], start=True, stop=True)
                        mm.then_inc(up, 1)
                        if u >= 2:
                            lower(c, u - 2)
                    lower(c, U - 2)
                    lower(c, U - 1)

            @block.scalar
            def _(act):
                with act.Fori(0, NC) as c:
                    for u in range(U):
                        n = c * U + u
                        act.wait_ge(up, n + 1)
                        if u >= 3:
                            act.wait_ge(hid_out, n - 2)
                        act.activation(gel[:, u % 3, :], k.ps[:, 2 * (u % 3), :], ACT.Gelu).then_inc(gel_out, 1)
                    act.wait_ge(down, c * U + U)
                    act.activation(sig[:, :], k.ps[:, 6, :], ACT.Sigmoid).then_inc(sig_out, 1)

            @block.vector
            def _(v):
                def pick(c, e):
                    if e >= 2:
                        v.wait_ge(up, c * U + (e - 1) * NI)
                    if e == 0:
                        v.tensor_copy(xc[:, 0, :], k.xnT[:, bass.ds(c * CH, CH)]).then_inc(picked, 1)
                    else:
                        v.scalar_tensor_tensor(out=xc[:, e % 2, :], in0=chosen[:, bass.ds(c * CH, CH)], scalar=float(e - 1),
                                               in1=k.xnT[:, bass.ds(c * CH, CH)], op0=ALU.is_equal, op1=ALU.mult)\
                         .then_inc(picked, 1)

                with v.Fori(0, NC) as c:
                    pick(c, 0)
                    pick(c, 1)
                    for u in range(U):
                        n = c * U + u
                        v.wait_ge(gel_out, n + 1)
                        if u >= 3:
                            v.wait_ge(down, n - 2)
                        v.tensor_tensor(hid[:, u % 3, :], gel[:, u % 3, :], k.ps[:, 2 * (u % 3) + 1, :], ALU.mult)\
                         .then_inc(hid_out, 1)
                        if u % NI == NI - 1 and u // NI + 2 <= NE:
                            pick(c, u // NI + 2)
                    v.wait_ge(sig_out, c + 1)
                    v.tensor_tensor(rows[:, :], sig[:, :], k.ps[:, 6, :], ALU.mult).then_inc(gated, 1)
                    r = rows[:, :].rearrange("p (t d) -> p t d", d=D)
                    at = bass.ds(c * 4, 4)
                    v.wait_ge(gated, c + 1)
                    v.tensor_tensor(r, r, k.hs[:, at, :], ALU.mult).then_inc(weighed, 1)
                    v.wait_ge(weighed, c + 1)
                    v.tensor_tensor(k.x[:, at, :], k.x[:, at, :], r, ALU.add).then_inc(added, 1)

            @block.sync
            def _(sp):
                with sp.Fori(0, NC) as c:
                    sp.wait_ge(added, c + 1)
                    sp.dma_start(ov[:, bass.ds(c * 4, 4), :], k.x[:, bass.ds(c * 4, 4), :]).then_inc(sent, 16)
                sp.wait_ge(sent, 16 * NC)


def build(nc, io, out):
    with ExitStack() as ctx:
        sb = lambda n, s, d=F32: ctx.enter_context(nc.sbuf_tensor(n, s, d))
        sem = lambda n: ctx.enter_context(nc.semaphore(n))
        k = Names()
        k.x, k.xn, k.hs = (sb(n, [P, NT, D]) for n in ("x", "xn", "hs"))
        k.xnT = sb("xnT", [P, T])
        k.wT = sb("wT", [P, 2048])
        k.ln_cols = sb("ln_cols", [P, 4])
        k.bias_cols, k.bias_rows = sb("bias_cols", [P, 9]), sb("bias_rows", [P, 3 * P])
        k.ident, k.identb = sb("ident", [P, P]), sb("identb", [P, P], BF16)
        k.half_ident, k.half_mask, k.half_maskT = (sb(n, [P, 2, P], BF16) for n in ("half_ident", "half_mask", "half_maskT"))
        k.mask = sb("mask", [P, P], BF16)
        k.perm = sb("perm", [P, P])
        k.eps, k.ones_row = sb("eps", [P, 1]), sb("ones_row", [P, P])
        k.ps = ctx.enter_context(nc.psum_tensor("ps", [P, 8, CH], F32))
        k.x_loaded = [sem(f"x_loaded{q}") for q in range(4)]
        dram = lambda n, s, d=F32: nc.dram_tensor(n, s, d, kind="Internal").ap()
        k.split_dram = [dram(f"split{i}", [PAIRS, 2, QROWS, S], BF16) for i in range(2)]
        k.o_dram = [dram(f"o{i}", [2 * PAIRS, HD + 1, S]) for i in range(2)]
        k.r_dram = dram("r", [2 * PAIRS, S])
        k.choice_dram = dram("choices", [T])
        stage_weights(nc, sem, io, k)
        with ExitStack() as heads:
            k.v_rows = heads.enter_context(nc.sbuf_tensor("v_rows", [P, B, H // 2, TPB, 2, HD + 1], F32))
            k.v_pairs = k.v_rows[:, :, :, :, :, :].rearrange("p b a t h d -> p (b a) t h d")
            with ExitStack() as turned:
                k.hT = turned.enter_context(nc.sbuf_tensor("hT", [P, T], F32))
                stage_norms(nc, sem, io, k)
                stage_qkv(nc, sem, k)
            stage_attention0(nc, sem, k)
        stage_project(nc, sem, k)
        stage_gate0(nc, sem, io, k)
        stage_attention1(nc, sem, k)
        stage_experts(nc, sem, io, k, out)


_INS = (["L0_attn_hs"] + [f"L0_attn_ln{i}_{n}" for i in (1, 2) for n in "gb"]
        + [f"L0_attn_{c}_{n}" for c in ("ca", "cp", "cf", "cm")
           for n in ("sub_w", "Wl_w", "W_w", "B_w", "sub_b", "Wl_b", "W_b", "B_b")]
        + [f"L0_ffn_cn_{n}{i}" for i in range(1, 5) for n in "wb"] + [f"L0_ffn_gc_{n}{i}" for i in range(1, 4) for n in "wb"]
        + ["L0_ffn_adaptive_range", "L1_attn_Wq", "L1_attn_Wk", "L1_attn_Wv", "L1_attn_Wo", "L1_ffn_w1s", "L1_ffn_w2s",
           "L1_ffn_w3s", "L1_ffn_W1", "L1_ffn_W2", "L1_ffn_W3", "L1_ffn_Wg"])


def kernel(**inputs):
    import numpy as _np
    import concourse.bacc as _bacc
    from concourse import mybir as _mybir
    from concourse.bass_utils import run_bass_kernel_spmd as _run

    nc = _bacc.Bacc("TRN2", target_bir_lowering=False, num_devices=1)
    arrays, io = {}, {}
    for name in _INS:
        a = _np.ascontiguousarray(inputs[name])
        arrays[f"in_{name}_dram"] = a
        io[name] = nc.dram_tensor(f"in_{name}_dram", a.shape, _mybir.dt.from_np(a.dtype), kind="ExternalInput").ap()
    out = nc.dram_tensor("out_0_dram", (B, S, D), F32, kind="ExternalOutput").ap()
    with nc.allow_non_contiguous_dma(reason="bias columns and the choices, a few thousand elements"):
        build(nc, io, out)
    r = _run(nc, [arrays], core_ids=[0])
    return r.results[0]["out_0_dram"]
```

```python
from contextlib import ExitStack

import concourse.bass as bass
from concourse import mybir

ALU = mybir.AluOpType
ACT = mybir.ActivationFunctionType
AX = mybir.AxisListType
F32 = mybir.dt.float32
BF16 = mybir.dt.bfloat16

P = 128
B, S, D = 4, 1024, 128
T = B * S
NT = T // P
TPB = S // P
CH = 512
NC = T // CH
H, HD = 16, 8
PAIRS = B * H // 2
INTER = 512
NI = INTER // P
NE = 8
EPS = 1e-5
BIG = -1e30
TERMS = [(0, 0), (0, 1), (1, 0), (0, 2), (1, 1), (2, 0)]
QROWS = len(TERMS) * HD
MROWS = 65
SROWS = MROWS + 3

W_CA, W_CP, W_CF, W_CM = 0, 384, 512, 1024
C_CA, C_CP, C_CF, C_CM = 1536, 1539, 1540, 1544
R_V, R_CP, R_CM = 1545, 1673, 1801
GEN = 1929


def tokens(x):
    return x.rearrange("b s d -> (b s) d").rearrange("(t p) d -> p t d", p=P)


def after(engine, semaphore, count):
    if isinstance(count, int) and count <= 0:
        return
    engine.wait_ge(semaphore, count)


def stage_weights(nc, sem, io, k):
    with ExitStack() as ctx:
        sb = lambda n, s, d=F32: ctx.enter_context(nc.sbuf_tensor(n, s, d))
        gs = {n: sb(f"gen_{n}", [P, GEN]) for n in ("s0", "s1", "W", "B")}
        gen = sb("gen_out", [P, GEN])
        wl = sb("wl", [P, 16])
        l1w = sb("l1w", [P, 4, P])
        loaded, consts, blended, squashed, scaled, done, turned = (
            sem(n) for n in ("w_loaded", "w_consts", "w_blended", "w_squashed", "w_scaled", "w_done", "w_turned"))
        consts0, emptied = sem("w_consts0"), sem("w_emptied")
        empty = k.empty
        lin = {n: {m: io[f"L0_attn_{n}_{m}"] for m in ("sub_w", "Wl_w", "W_w", "B_w", "sub_b", "Wl_b", "W_b", "B_b")}
               for n in ("ca", "cp", "cf", "cm")}
        order = ("ca", "cp", "cf", "cm")
        loads = []
        for g in ("s0", "s1", "W", "B"):
            for n, at, cols in (("ca", W_CA, 3), ("cp", W_CP, 1), ("cf", W_CF, 4)):
                src = lin[n]["sub_w"][int(g[1])] if g[0] == "s" else lin[n][g + "_w"]
                loads.append((gs[g][:, at:at + cols * P].rearrange("p (c i) -> p c i", i=P),
                              src.rearrange("(c p) i -> p c i", p=P)))
            src = lin["cm"]["sub_w"][int(g[1])] if g[0] == "s" else lin["cm"][g + "_w"]
            loads.append((gs[g][:, W_CM:W_CM + INTER], src))
            for n, at, cols in (("ca", C_CA, 3), ("cp", C_CP, 1), ("cf", C_CF, 4), ("cm", C_CM, 1)):
                src = lin[n]["sub_b"][int(g[1])] if g[0] == "s" else lin[n][g + "_b"]
                loads.append((gs[g][:, at:at + cols], src.rearrange("(c p) -> p c", p=P)))
            for n, at, lo in (("ca", R_V, 256), ("cp", R_CP, 0), ("cm", R_CM, 0)):
                src = lin[n]["sub_b"][int(g[1])] if g[0] == "s" else lin[n][g + "_b"]
                loads.append((gs[g][:, at:at + P], src[lo:lo + P].partition_broadcast(P)))
        for j, n in enumerate(order):
            loads.append((wl[:, 2 * j:2 * j + 2], lin[n]["Wl_w"][0].partition_broadcast(P)))
            loads.append((wl[:, 8 + 2 * j:10 + 2 * j], lin[n]["Wl_b"][0].partition_broadcast(P)))
        for j, n in enumerate(("Wq", "Wk", "Wv", "Wo")):
            loads.append((l1w[:, j, :], io["L1_attn_" + n]))
        parts = [(W_CA, 384, 0), (W_CP, P, 2), (W_CF, 512, 4), (W_CM, 512, 6), (C_CA, 3, 8), (C_CP, 1, 10),
                 (C_CF, 4, 12), (C_CM, 1, 14), (R_V, P, 8), (R_CP, P, 10), (R_CM, P, 14)]
        xv = tokens(io["L0_attn_hs"])
        ln_cols = [(k.ln_cols[:, j:j + 1], io["L0_attn_" + n].rearrange("(p a) -> p a", a=1))
                   for j, n in enumerate(("ln1_g", "ln1_b", "ln2_g", "ln2_b"))]
        loads += ln_cols
        half = len(loads) // 2

        with nc.Block() as block:
            @block.sync
            def _(sp):
                for q in range(4):
                    sp.dma_start(k.x[:, 8 * q:8 * q + 8, :], xv[:, 8 * q:8 * q + 8, :]).then_inc(k.x_loaded[q], 16)
                for dst, src in loads[:half]:
                    sp.dma_start(dst, src).then_inc(loaded, 16)

            @block.scalar
            def _(act):
                for dst, src in loads[half:]:
                    act.dma_start(dst, src).then_inc(loaded, 16)
                act.wait_ge(emptied, 1)
                act.dma_start(k.xs_dram.rearrange("(i p) d -> p i d", p=P),
                              empty[:, :].unsqueeze(1).broadcast_to([P, BLOCKS, D])).then_inc(k.rows_cleared, 16)
                act.wait_ge(blended, 2 * len(parts))
                act.activation(gen[:, :], gen[:, :], ACT.Tanh).then_inc(squashed, 1)
                for c in range(2):
                    act.wait_ge(done, 4 * c + 4)
                    act.copy(k.wT[:, c * CH:(c + 1) * CH], k.ps[:, c, :]).then_inc(turned, 1)

            @block.gpsimd
            def _(pool):
                pool.memset(empty[:, :], 0.0).then_inc(emptied, 1)
                pool.memset(k.ident[:, :], 0.0).then_inc(consts0, 1)
                pool.memset(k.identb[:, :], 0.0).then_inc(consts0, 1)
                pool.memset(k.maskT[:, :], 0.0).then_inc(consts0, 1)
                pool.memset(k.mask[:, :], 0.0).then_inc(consts0, 1)
                pool.memset(k.perm[:, :], 0.0).then_inc(consts0, 1)
                pool.memset(k.eps[:, :], EPS).then_inc(consts, 1)
                pool.memset(k.ones_row[:, :], 1.0).then_inc(consts, 1)
                pool.wait_ge(consts0, 5)
                for t in (k.ident, k.identb):
                    pool.affine_select(out=t[:, :], in_=t[:, :], compare_op=ALU.not_equal, fill=1.0, base=0,
                                       pattern=[[-1, P]], channel_multiplier=1).then_inc(consts, 1)
                pool.affine_select(out=k.mask[:, :], in_=k.mask[:, :], compare_op=ALU.is_ge, fill=BIG, base=0,
                                   pattern=[[-1, P]], channel_multiplier=1).then_inc(consts, 1)
                pool.affine_select(out=k.maskT[:, :], in_=k.maskT[:, :], compare_op=ALU.is_ge, fill=BIG, base=0,
                                   pattern=[[1, P]], channel_multiplier=-1).then_inc(consts, 1)
                n = 6
                for lo, at, sign in ((64, 0, 1.0), (96, 32, -1.0), (0, 64, -1.0), (32, 96, 1.0)):
                    pool.wait_ge(consts, n)
                    t = k.perm[lo:lo + 32, at:at + 32]
                    pool.affine_select(out=t, in_=t, compare_op=ALU.not_equal, fill=sign, base=0,
                                       pattern=[[-1, 32]], channel_multiplier=1).then_inc(consts, 1)
                    n += 1

            @block.vector
            def _(v):
                v.wait_ge(loaded, 16 * len(loads))
                for n, (at, cols, w) in enumerate(parts):
                    v.tensor_scalar(gen[:, at:at + cols], gs["s0"][:, at:at + cols], wl[:, w:w + 1], None,
                                    ALU.mult).then_inc(blended, 1)
                v.wait_ge(blended, len(parts))
                for n, (at, cols, w) in enumerate(parts):
                    v.scalar_tensor_tensor(out=gen[:, at:at + cols], in0=gs["s1"][:, at:at + cols],
                                           scalar=wl[:, w + 1:w + 2], in1=gen[:, at:at + cols],
                                           op0=ALU.mult, op1=ALU.add).then_inc(blended, 1)
                v.wait_ge(squashed, 1)
                v.tensor_tensor(gen[:, :], gen[:, :], gs["W"][:, :], ALU.mult).then_inc(scaled, 1)
                v.wait_ge(scaled, 1)
                v.tensor_tensor(gen[:, :], gen[:, :], gs["B"][:, :], ALU.add).then_inc(scaled, 1)
                v.wait_ge(scaled, 2)
                v.tensor_copy(k.bias_cols[:, :], gen[:, C_CA:C_CA + 9]).then_inc(turned, 1)
                v.tensor_copy(k.bias_rows[:, :], gen[:, R_V:R_V + 3 * P]).then_inc(turned, 1)
                for c in range(2, 4):
                    v.wait_ge(done, 4 * c + 4)
                    v.tensor_copy(k.wT[:, c * CH:(c + 1) * CH], k.ps[:, c, :]).then_inc(turned, 1)

            @block.tensor
            def _(pe):
                pe.wait_ge(consts, 10)
                pe.wait_ge(scaled, 2)
                for n in range(16):
                    src = gen[:, n * P:(n + 1) * P] if n < 12 else l1w[:, n - 12, :]
                    pe.transpose(k.ps[:, n // 4, (n % 4) * P:(n % 4 + 1) * P], src, k.ident[:, :]).then_inc(done, 1)


def layer_norm_vector(v, src, out, work, s, ready):
    for t in range(NT):
        ready(t)
        v.bn_stats(work.stats[:, t, :], src[:, t, :]).then_inc(s.stats, 1)
    v.wait_ge(s.stats, NT)
    for t in range(NT):
        v.bn_aggr(work.mv[:, t, :], work.stats[:, t, :]).then_inc(s.mv, 1)
    v.wait_ge(s.std, 1)
    v.reciprocal(work.rstd[:, :], work.std[:, :]).then_inc(s.rstd, 1)
    v.wait_ge(s.rstd, 1)
    for t in range(NT):
        v.tensor_scalar(out[:, t, :], src[:, t, :], work.mv[:, t, 0:1], work.rstd[:, t:t + 1],
                        ALU.subtract, ALU.mult).then_inc(s.out, 1)


def layer_norm_scalar(act, k, work, s):
    act.wait_ge(s.mv, NT)
    act.activation(work.std[:, :], work.mv[:, :, 1], ACT.Sqrt, bias=k.eps[:, 0:1]).then_inc(s.std, 1)


class Names:
    pass


def layer_norm_names(sem, tag):
    s = Names()
    s.stats, s.mv, s.std, s.rstd, s.out = (sem(f"{tag}_{n}") for n in ("stats", "mv", "std", "rstd", "out"))
    return s


def layer_norm_work(sb, tag):
    w = Names()
    w.stats = sb(f"{tag}_w_stats", [P, NT, 6])
    w.mv = sb(f"{tag}_w_mv", [P, NT, 2])
    w.std = sb(f"{tag}_w_std", [P, NT])
    w.rstd = sb(f"{tag}_w_rstd", [P, NT])
    return w


def turn_tensor(pe, k, src, ready, bank0, free, turned):
    for t in range(NT):
        ready(t)
        if t % 4 == 0:
            after(pe, free, t // 4 - 1)
        pe.transpose(k.ps[:, bank0 + t // 4 % 2, (t % 4) * P:(t % 4 + 1) * P], src[:, t, :],
                     k.ident[:, :]).then_inc(turned, 1)


def stage_norms(nc, sem, io, k):
    with ExitStack() as ctx:
        sb = lambda n, s, d=F32: ctx.enter_context(nc.sbuf_tensor(n, s, d))
        w0, w1 = layer_norm_work(sb, "n0"), layer_norm_work(sb, "n1")
        h = sb("h_rows", [P, NT, D])
        s0, s1 = layer_norm_names(sem, "n0"), layer_norm_names(sem, "n1")
        xn_turned, h_turned, xn_out, h_out = (sem(n) for n in ("xn_turned", "h_turned", "xn_out", "h_out"))
        with nc.Block() as block:
            @block.vector
            def _(v):
                layer_norm_vector(v, k.x, k.xn, w0, s0,
                                  lambda t: v.wait_ge(k.x_loaded[t // 8], 16) if t % 8 == 0 else None)
                layer_norm_vector(v, k.xn, h, w1, s1, lambda t: v.wait_ge(s0.out, t + 1))
                for c in range(NC):
                    v.wait_ge(h_turned, 4 * c + 4)
                    v.tensor_scalar(k.hT[:, c * CH:(c + 1) * CH], k.ps[:, 2 + c % 2, :], k.ln_cols[:, 0:1],
                                    k.ln_cols[:, 1:2], ALU.mult, ALU.add).then_inc(h_out, 1)

            @block.scalar
            def _(act):
                layer_norm_scalar(act, k, w0, s0)
                layer_norm_scalar(act, k, w1, s1)
                for c in range(NC):
                    act.wait_ge(xn_turned, 4 * c + 4)
                    act.copy(k.xnT[:, c * CH:(c + 1) * CH], k.ps[:, c % 2, :]).then_inc(xn_out, 1)

            @block.tensor
            def _(pe):
                turn_tensor(pe, k, k.xn, lambda t: pe.wait_ge(s0.out, t + 1), 0, xn_out, xn_turned)
                turn_tensor(pe, k, h, lambda t: pe.wait_ge(s1.out, t + 1), 2, h_out, h_turned)


def stage_qkv(nc, sem, k):
    with ExitStack() as ctx:
        sb = lambda n, s, d=F32: ctx.enter_context(nc.sbuf_tensor(n, s, d))
        whole = [sb(f"whole{i}", [P, 2, CH]) for i in range(2)]
        rest = [sb(f"rest{i}", [P, 2, CH]) for i in range(2)]
        part = [sb(f"part{i}", [P, 2, 3, S], BF16) for i in range(2)]
        proj, whole_out = sem("qk_proj"), sem("qk_whole")
        chain = [sem(f"qk_chain{i}") for i in range(2)]
        stored = [[sem(f"qk_stored{i}_{j}") for j in range(2)] for i in range(2)]
        v_proj, v_out, v_ones = sem("v_proj"), sem("v_out"), sem("v_ones")
        WAYS = len(TERMS)
        with nc.Block() as block:
            @block.tensor
            def _(pe):
                for c in range(NC):
                    for i in range(2):
                        after(pe, whole_out, 2 * (c - 1) + i)
                        pe.matmul(k.ps[:, 2 * (c % 2) + i, :], k.wT[:, i * P:(i + 1) * P],
                                  k.hT[:, c * CH:(c + 1) * CH], start=True, stop=True).then_inc(proj, 1)
                    after(pe, v_out, 4 * (c - 1))
                    for t in range(4 * c, 4 * c + 4):
                        pe.matmul(k.ps[:, 4 + c % 2, (t % 4) * P:(t % 4 + 1) * P], k.hT[:, t * P:(t + 1) * P],
                                  k.wT[:, 2 * P:3 * P], start=True, stop=True).then_inc(v_proj, 1)

            @block.scalar
            def _(act):
                for c in range(NC):
                    for i in range(2):
                        act.wait_ge(proj, 2 * c + i + 1)
                        after(act, chain[i], 5 * (c - 1))
                        act.activation(whole[i][:, c % 2, :], k.ps[:, 2 * (c % 2) + i, :], ACT.Identity,
                                       bias=k.bias_cols[:, i:i + 1]).then_inc(whole_out, 1)

            def split(e, i, between):
                for c in range(NC):
                    b, at = c // 2, (c % 2) * CH
                    w, r = whole[i][:, c % 2, :], rest[i][:, c % 2, :]
                    p0, p1, p2 = (part[i][:, b % 2, j, at:at + CH] for j in range(3))
                    e.wait_ge(whole_out, 2 * c + i + 1)
                    if c % 2 == 0:
                        after(e, stored[i][b % 2], 16 * WAYS * (b // 2))
                    e.tensor_copy(p0, w).then_inc(chain[i], 1)
                    e.wait_ge(chain[i], 5 * c + 1)
                    e.tensor_tensor(r, w, p0, ALU.subtract).then_inc(chain[i], 1)
                    e.wait_ge(chain[i], 5 * c + 2)
                    e.tensor_copy(p1, r).then_inc(chain[i], 1)
                    e.wait_ge(chain[i], 5 * c + 3)
                    e.tensor_tensor(p2, r, p1, ALU.subtract).then_inc(chain[i], 2)
                    between(c)

            @block.gpsimd
            def _(pool):
                split(pool, 1, lambda c: None)

            @block.vector
            def _(v):
                v.memset(k.v_rows[:, :, :, :, :, :], 1.0).then_inc(v_ones, 1)
                v.wait_ge(v_ones, 1)

                def v_rows(c):
                    v.wait_ge(v_proj, 4 * c + 4)
                    for t in range(4 * c, 4 * c + 4):
                        v.tensor_tensor(k.v_rows[:, t // TPB, :, t % TPB, :, 0:HD],
                                        k.ps[:, 4 + c % 2, (t % 4) * P:(t % 4 + 1) * P].rearrange(
                                            "p (a h d) -> p a h d", a=H // 2, h=2),
                                        k.bias_rows[:, 0:P].rearrange("p (a h d) -> p a h d", a=H // 2, h=2),
                                        ALU.add).then_inc(v_out, 1)
                split(v, 0, v_rows)

            @block.sync
            def _(sp):
                for b in range(B):
                    for i in range(2):
                        sp.wait_ge(chain[i], 5 * (2 * b + 2))
                        dst = k.split_dram[i][b * (H // 2):(b + 1) * (H // 2)].rearrange(
                            "a h (t d) s -> t (a h) d s", d=HD)
                        for t, term in enumerate(TERMS):
                            sp.dma_start(dst[t], part[i][:, b % 2, term[i], :]).then_inc(stored[i][b % 2], 16)
                for i in range(2):
                    for j in range(2):
                        sp.wait_ge(stored[i][j], 16 * WAYS * (B // 2))


MAX_UNITS = [(t, c * CH, min(CH, (t + 1) * P - c * CH), c == t * P // CH)
             for t in range(TPB) for c in range(t * P // CH + 1)]
EXP_UNITS = [(t, max(c * CH, t * P), (c + 1) * CH - max(c * CH, t * P), t * P >= c * CH)
             for c in range(S // CH) for t in range(4 * c + 4)]
NU = len(MAX_UNITS)
GROUPS = len(EXP_UNITS) // 2


def stage_attention0(nc, sem, k):
    with ExitStack() as ctx:
        sb = lambda n, s, d=F32: ctx.enter_context(nc.sbuf_tensor(n, s, d))
        Q = [sb(f"q{i}", [P, 2, S], BF16) for i in range(4)]
        K = [sb(f"k{i}", [P, 2, S], BF16) for i in range(4)]
        V = [sb(f"v{i}", [P, TPB, 2, HD + 1]) for i in range(4)]
        probs = sb("probs", [P, 8, CH])
        nmax = [sb(f"nmax{i}", [P, 2, TPB]) for i in range(2)]
        nmax2 = [sb(f"nmax2{i}", [P, 2, 4]) for i in range(2)]
        nrest = [sb(f"nrest{i}", [P, 2, TPB]) for i in range(2)]
        nrest2 = [sb(f"nrest2{i}", [P, 2, TPB]) for i in range(2)]
        zero = sb("zero", [P, 2, TPB])
        shift = [sb(f"shift{i}", [P, 2, 32], BF16) for i in range(2)]
        shiftT = [sb(f"shiftT{i}", [P, 2, 32], BF16) for i in range(2)]
        ev = [sb(f"ev{i}", [P, CH]) for i in range(2)]
        loaded = [sem(f"a_loaded{i}") for i in range(4)]
        shift_in = [sem(f"a_shift_in{i}") for i in range(4)]
        scored, maxed, split, shifted = sem("a_scored"), sem("a_maxed"), sem("a_split"), sem("a_shifted")
        scoredT, exped, pv_done, ev_ready = sem("a_scoredT"), sem("a_exped"), sem("a_pv"), sem("a_ev")
        ev_stored = [sem(f"a_ev_stored{i}") for i in range(2)]
        ready, joined = sem("a_ready"), sem("a_joined")
        PV = k.ps[:, 7, :]
        LOADS, SHIFTS = 16 * 5, 16 * 8

        def bodies(run):
            for j in range(4):
                run(0, j)
            with run.engine.Fori(1, PAIRS // 4 - 1) as r:
                for j in range(4):
                    run(r, j)
            for j in range(4):
                run(PAIRS // 4 - 1, j)

        def has(r, j, ahead):
            return not (isinstance(r, int) and 4 * r + j + ahead >= PAIRS)

        with nc.Block() as block:
            @block.sync
            def _(sp):
                def load(r, j):
                    p = r * 4 + j
                    r, j = r + j // 4, j % 4
                    after(sp, pv_done, (p - 3) * GROUPS)
                    for h in range(2):
                        sp.dma_start(Q[j][0:QROWS, h, :], k.split_dram[0][bass.ds(p, 1), h]
                                     .rearrange("a r s -> (a r) s")).then_inc(loaded[j], 16)
                        sp.dma_start(K[j][0:QROWS, h, :], k.split_dram[1][bass.ds(p, 1), h]
                                     .rearrange("a r s -> (a r) s")).then_inc(loaded[j], 16)
                    sp.dma_start(V[j][:, :, :, :], k.v_pairs[:, bass.ds(p, 1), :, :, :]
                                 .rearrange("p a t h d -> p (a t) h d")).then_inc(loaded[j], 16)

                def put_shift(r, j):
                    p = r * 4 + j
                    r, j = r + j // 4, j % 4
                    sp.wait_ge(shifted, p + 1)
                    for h in range(2):
                        dst = Q[j][MROWS:SROWS, h, :].rearrange("r (t a i) -> r t a i", a=4, i=32)
                        for a in range(4):
                            sp.dma_start(dst[:, :, a, :], shiftT[j % 2][32 * a:32 * a + 24, h, :])\
                              .then_inc(shift_in[j], 16)

                def store(r, j, c):
                    p = r * 4 + j
                    sp.wait_ge(ev_ready, p * 2 + (c + 1))
                    for par in range(2):
                        for h in range(2):
                            g = 32 * (2 * par + h)
                            sp.dma_start(k.o_dram[par][bass.ds(p * 2 + h, 1), :, c * CH:(c + 1) * CH]
                                         .rearrange("a r s -> (a r) s"),
                                         ev[c][g:g + HD + 1, :]).then_inc(ev_stored[c], 16)

                sp.wait_ge(ready, 17)
                for j in range(3):
                    load(0, j)
                put_shift(0, 0)

                def run(r, j):
                    if not (isinstance(r, int) and r * 4 + j == 0):
                        store(r if j else r - 1, (j - 1) % 4, 1)
                    if has(r, j, 1):
                        put_shift(r, j + 1)
                    if has(r, j, 3):
                        load(r, j + 3)
                    store(r, j, 0)
                run.engine = sp
                bodies(run)
                store(PAIRS // 4 - 1, 3, 1)
                for c in range(2):
                    sp.wait_ge(ev_stored[c], 64 * PAIRS)

            @block.gpsimd
            def _(pool):
                for j in range(4):
                    pool.memset(Q[j][:, :, :], 0.0).then_inc(ready, 1)
                    pool.memset(K[j][:, :, :], 0.0).then_inc(ready, 1)
                pool.wait_ge(ready, 8)
                for j in range(4):
                    pool.memset(K[j][64:P, :, :], 1.0).then_inc(ready, 1)
                pool.wait_ge(ready, 12)
                pool.memset(zero[:, :, :], 0.0).then_inc(ready, 1)
                for i in range(2):
                    pool.memset(shift[i][:, :, :], 0.0).then_inc(ready, 1)
                    pool.memset(ev[i][:, :], 0.0).then_inc(ready, 1)

                def parts(r, j):
                    p = r * 4 + j
                    i = j % 2
                    part = [shift[i][:, :, 8 * n:8 * n + 8] for n in range(3)]
                    pool.wait_ge(joined, p + 1)
                    after(pool, shifted, p - 1)
                    pool.tensor_tensor(part[0], nmax[i][:, :, :], zero[:, :, :], ALU.add).then_inc(split, 1)
                    pool.wait_ge(split, p * 4 + 1)
                    pool.tensor_tensor(nrest[i][:, :, :], nmax[i][:, :, :], part[0], ALU.subtract).then_inc(split, 1)
                    pool.wait_ge(split, p * 4 + 2)
                    pool.tensor_tensor(part[1], nrest[i][:, :, :], zero[:, :, :], ALU.add).then_inc(split, 1)
                    pool.wait_ge(split, p * 4 + 3)
                    pool.tensor_tensor(part[2], nrest[i][:, :, :], part[1], ALU.subtract).then_inc(split, 1)

                parts(0, 0)
                parts(0, 1)

                def run(r, j):
                    if has(r, j, 2):
                        parts(r + (j + 2) // 4, (j + 2) % 4)
                run.engine = pool
                bodies(run)

            @block.vector
            def _(v):
                def row_max(r, j, u):
                    p = r * 4 + j
                    t, c0, n, _ = MAX_UNITS[u]
                    if u == 0:
                        after(v, split, (p - 1) * 4)
                    v.wait_ge(scored, p * NU + (u + 1))
                    out = nmax[j % 2][:, :, t:t + 1] if c0 == 0 else nmax2[j % 2][:, :, t - 4:t - 3]
                    v.tensor_reduce(out, k.ps[:, 2 * (u % 2):2 * (u % 2) + 2, 0:n], AX.X, ALU.max,
                                    negate=True).then_inc(maxed, 1)
                    if u == NU - 1:
                        v.wait_ge(maxed, (p + 1) * NU)
                        v.tensor_tensor(nmax[j % 2][:, :, 4:8], nmax[j % 2][:, :, 4:8], nmax2[j % 2][:, :, :], ALU.min)\
                         .then_inc(joined, 1)

                def turn(r, j):
                    p = r * 4 + j
                    r2, j2 = (r, j - 2) if j >= 2 else (r - 1, j + 2)
                    v.wait_ge(split, p * 4 + 4)
                    if not (isinstance(p, int) and p < 2):
                        after(v, shift_in[j2], SHIFTS * (r2 + 1))
                    v.transpose(shiftT[j % 2][:, :, :], shift[j % 2][:, :, :]).then_inc(shifted, 1)

                def evacuate(r, j, c):
                    p = r * 4 + j
                    after(v, ev_stored[c], p * 64)
                    v.wait_ge(pv_done, p * GROUPS + (2 if c == 0 else GROUPS))
                    if c == 0:
                        v.tensor_copy(ev[0][0:64, 0:P], PV[0:64, 0:P])
                        v.tensor_copy(ev[0][:, P:CH], PV[:, P:CH]).then_inc(ev_ready, 1)
                    else:
                        v.tensor_copy(ev[1][:, :], PV[:, :]).then_inc(ev_ready, 1)

                v.wait_ge(ready, 17)
                v.memset(PV, 0.0).then_inc(ready, 1)
                for j in range(2):
                    for u in range(NU):
                        row_max(0, j, u)
                turn(0, 0)

                def run(r, j):
                    for u in range(NU):
                        if has(r, j, 2):
                            row_max(r + (j + 2) // 4, (j + 2) % 4, u)
                        if u == 2 and has(r, j, 1):
                            turn(r + (j + 1) // 4, (j + 1) % 4)
                        if u == 5:
                            evacuate(r, j, 0)
                    evacuate(r, j, 1)
                run.engine = v
                bodies(run)

            @block.scalar
            def _(act):
                def run(r, j):
                    p = r * 4 + j
                    for e in range(4 * GROUPS):
                        n = EXP_UNITS[e // 2][2]
                        if e % 4 == 0:
                            after(act, pv_done, p * GROUPS + (e // 4 - 1))
                        act.wait_ge(scoredT, p * (4 * GROUPS) + (e + 1))
                        act.activation(probs[:, e % 8, 0:n], k.ps[:, 4 + e % 3, 0:n], ACT.Exp,
                                       scale=float(HD) ** -0.5).then_inc(exped, 1)
                run.engine = act
                bodies(run)

            @block.tensor
            def _(pe):
                def scores(r, j, u):
                    p = r * 4 + j
                    t, c0, n, diag = MAX_UNITS[u]
                    out = [k.ps[:, 2 * (u % 2) + h, :] for h in range(2)]
                    if u == 0:
                        pe.wait_ge(loaded[j], LOADS * (r + 1))
                    after(pe, maxed, p * NU + (u - 1))
                    for h in range(2):
                        mm = pe.matmul(out[h][:, 0:n], Q[j][0:MROWS, h, t * P:(t + 1) * P],
                                       K[j][0:MROWS, h, c0:c0 + n], start=True, stop=True)
                        if diag:
                            mm = pe.matmul(out[h][:, n - P:n], k.identb[:, :], k.mask[:, :], start=False, stop=True,
                                           skip_group_check=True)
                    mm.then_inc(scored, 1)

                def scores_t(r, j, u):
                    p = r * 4 + j
                    t, q0, n, diag = EXP_UNITS[u]
                    if u == 0:
                        pe.wait_ge(shift_in[j], SHIFTS * (r + 1))
                    for h in range(2):
                        out = k.ps[:, 4 + (2 * u + h) % 3, :]
                        after(pe, exped, p * (4 * GROUPS) + (2 * u + h - 2))
                        mm = pe.matmul(out[:, 0:n], K[j][0:SROWS, h, t * P:(t + 1) * P],
                                       Q[j][0:SROWS, h, q0:q0 + n], start=True, stop=True)
                        if diag:
                            mm = pe.matmul(out[:, 0:P], k.identb[:, :], k.maskT[:, :], start=False, stop=True,
                                           skip_group_check=True)
                        mm.then_inc(scoredT, 1)

                def weigh(r, j, g):
                    p = r * 4 + j
                    pe.wait_ge(exped, p * (4 * GROUPS) + 4 * (g + 1))
                    if g in (0, 2):
                        after(pe, ev_ready, p * 2 + (1 if g else 0))
                    for par in range(2):
                        t, q0, n, _ = EXP_UNITS[2 * g + par]
                        for h in range(2):
                            e = 4 * g + 2 * par + h
                            lo = 32 * (2 * par + h)
                            mm = pe.matmul(PV[lo:lo + HD + 1, CH - n:CH], V[j][:, t, h, :], probs[:, e % 8, 0:n],
                                           start=(g in (0, 2)), stop=True, skip_group_check=True)
                    mm.then_inc(pv_done, 1)

                pe.wait_ge(ready, 18)
                for j in range(2):
                    for u in range(NU):
                        scores(0, j, u)

                def run(r, j):
                    for u in range(NU):
                        scores_t(r, j, u)
                        if has(r, j, 2):
                            if u:
                                scores(r + (j + 2) // 4, (j + 2) % 4, u - 1)
                            if u == NU - 1:
                                scores(r + (j + 2) // 4, (j + 2) % 4, u)
                        if u % 2 and u > 1:
                            weigh(r, j, u // 2 - 1)
                    weigh(r, j, GROUPS - 1)
                run.engine = pe
                bodies(run)


def stage_project(nc, sem, k):
    with ExitStack() as ctx:
        sb = lambda n, s, d=F32: ctx.enter_context(nc.sbuf_tensor(n, s, d))
        even, odd, over = sb("o_even", [P, T]), sb("o_odd", [P, T]), sb("o_over", [P, T])
        sums = sb("sums", [P, 2, CH])
        rsum = sb("rsum", [P, CH])
        in_sums, in_o, in_over = sem("p_in_sums"), [sem(f"p_in_o{b}") for b in range(B)], sem("p_in_over")
        total, inverse, joined, normed, rstored = (sem(f"p_{n}") for n in ("total", "inverse", "joined", "normed", "rstored"))
        proj, biased, hs_out = sem("p_proj"), sem("p_biased"), sem("p_hs")
        with nc.Block() as block:
            @block.sync
            def _(sp):
                for par in range(2):
                    sp.dma_start(sums[:, par, :], k.o_dram[par][:, HD, :].rearrange("g (c s) -> g c s", s=CH))\
                      .then_inc(in_sums, 16)
                for b in range(B):
                    for par, dst in enumerate((even, odd)):
                        sp.dma_start(dst[:, b * S:(b + 1) * S], k.o_dram[par][b * H:(b + 1) * H, 0:HD, :])\
                          .then_inc(in_o[b], 16)
                sp.wait_ge(inverse, 1)
                sp.dma_start(k.r_dram.rearrange("g (c s) -> g c s", s=CH), rsum[:, :]).then_inc(rstored, 16)
                sp.wait_ge(rstored, 16)
                for b in range(B):
                    src = k.r_dram[b * H:(b + 1) * H, :].unsqueeze(1).broadcast_to([H, HD, S])
                    sp.dma_start(over[:, b * S:(b + 1) * S], src).then_inc(in_over, 16)

            @block.vector
            def _(v):
                v.wait_ge(in_sums, 32)
                v.tensor_tensor(sums[:, 0, :], sums[:, 0, :], sums[:, 1, :], ALU.add).then_inc(total, 1)
                v.wait_ge(total, 1)
                v.reciprocal(rsum[:, :], sums[:, 0, :]).then_inc(inverse, 1)
                v.wait_ge(in_over, 64)
                for b in range(B):
                    at = slice(b * S, (b + 1) * S)
                    v.wait_ge(joined, b + 1)
                    v.tensor_tensor(even[:, at], even[:, at], over[:, at], ALU.mult).then_inc(normed, 1)
                for c in range(NC):
                    v.wait_ge(proj, 4 * c + 4)
                    rows = k.hs[:, 4 * c:4 * c + 4, :]
                    v.tensor_tensor(rows, k.ps[:, c % 2, :].rearrange("p (t d) -> p t d", d=D),
                                    k.xn[:, 4 * c:4 * c + 4, :], ALU.add).then_inc(biased, 1)
                    for t in range(4 * c, 4 * c + 4):
                        if t % 4 == 0:
                            v.wait_ge(biased, c + 1)
                        v.tensor_tensor(k.hs[:, t, :], k.hs[:, t, :], k.bias_rows[:, P:2 * P], ALU.add)\
                         .then_inc(hs_out, 1)

            @block.gpsimd
            def _(pool):
                for b in range(B):
                    at = slice(b * S, (b + 1) * S)
                    pool.wait_ge(in_o[b], 32)
                    pool.tensor_tensor(even[:, at], even[:, at], odd[:, at], ALU.add).then_inc(joined, 1)

            @block.tensor
            def _(pe):
                for t in range(NT):
                    pe.wait_ge(normed, t // TPB + 1)
                    if t % 4 == 0:
                        after(pe, biased, t // 4 - 1)
                    pe.matmul(k.ps[:, t // 4 % 2, (t % 4) * P:(t % 4 + 1) * P], even[:, t * P:(t + 1) * P],
                              k.wT[:, W_CP:W_CP + P], start=True, stop=True).then_inc(proj, 1)

    with ExitStack() as ctx:
        sb = lambda n, s, d=F32: ctx.enter_context(nc.sbuf_tensor(n, s, d))
        w = layer_norm_work(sb, "n2")
        s = layer_norm_names(sem, "n2")
        rows = sb("h2_rows", [P, NT, D])
        hT = sb("h2T", [P, T])
        mid = sb("mid", [P, 4, CH])
        turned, hT_out, up, act_out, down, summed, s_out = (sem(f"m_{n}") for n in ("turned", "hT", "up", "act", "down", "summed", "s"))
        with nc.Block() as block:
            @block.vector
            def _(v):
                layer_norm_vector(v, k.hs, rows, w, s, lambda t: None)
                for c in range(NC):
                    v.wait_ge(turned, 4 * c + 4)
                    v.tensor_scalar(hT[:, c * CH:(c + 1) * CH], k.ps[:, c % 2, :], k.ln_cols[:, 2:3],
                                    k.ln_cols[:, 3:4], ALU.mult, ALU.add).then_inc(hT_out, 1)
                for c in range(NC):
                    v.wait_ge(down, c + 1)
                    v.tensor_tensor(k.hs[:, 4 * c:4 * c + 4, :], k.hs[:, 4 * c:4 * c + 4, :],
                                    k.ps[:, 6 + c % 2, :].rearrange("p (t d) -> p t d", d=D), ALU.add).then_inc(summed, 1)
                    v.wait_ge(summed, c + 1)
                    for t in range(4 * c, 4 * c + 4):
                        v.tensor_tensor(k.hs[:, t, :], k.hs[:, t, :], k.bias_rows[:, 2 * P:3 * P], ALU.add)\
                         .then_inc(s_out, 1)

            @block.scalar
            def _(act):
                layer_norm_scalar(act, k, w, s)
                for c in range(NC):
                    for i in range(NI):
                        n = NI * c + i
                        act.wait_ge(up, n + 1)
                        after(act, down, c)
                        act.activation(mid[:, i, :], k.ps[:, 2 + n % 4, :], ACT.Gelu_apprx_tanh,
                                       bias=k.bias_cols[:, 4 + i:5 + i]).then_inc(act_out, 1)

            @block.tensor
            def _(pe):
                turn_tensor(pe, k, rows, lambda t: pe.wait_ge(s.out, t + 1), 0, hT_out, turned)
                for c in range(NC):
                    pe.wait_ge(hT_out, c + 1)
                    for i in range(NI):
                        n = NI * c + i
                        after(pe, act_out, n - 3)
                        pe.matmul(k.ps[:, 2 + n % 4, :], k.wT[:, W_CF + i * P:W_CF + (i + 1) * P],
                                  hT[:, c * CH:(c + 1) * CH], start=True, stop=True).then_inc(up, 1)
                    pe.wait_ge(act_out, NI * c + NI)
                    after(pe, summed, c - 1)
                    for t in range(4):
                        for i in range(NI):
                            mm = pe.matmul(k.ps[:, 6 + c % 2, t * P:(t + 1) * P], mid[:, i, t * P:(t + 1) * P],
                                           k.wT[:, W_CM + i * P:W_CM + (i + 1) * P], start=(i == 0), stop=(i == NI - 1))
                    mm.then_inc(down, 1)


CYCLES = 3


def stage_gate0(nc, sem, io, k):
    with ExitStack() as ctx:
        sb = lambda n, s, d=F32: ctx.enter_context(nc.sbuf_tensor(n, s, d))
        w1, w2, w3, w4 = sb("cn1", [P, 128]), sb("cn2", [P, 64]), sb("cn3", [P, 64]), sb("cn4", [P, 1])
        w4w = sb("cn4w", [P, 4, P])
        b1, b2, b3, b4 = sb("cb1", [P, 1]), sb("cb2", [P, 1]), sb("cb3", [P, 1]), sb("cb4", [P, 1])
        u1, u2, u3, u3w = sb("gc1", [P, 64]), sb("gc2", [64, 32]), sb("gc3", [32, 1]), sb("gc3w", [32, P])
        d1, d2, d3 = sb("gb1", [64, 1]), sb("gb2", [32, 1]), sb("gb3", [P, 1])
        rng = sb("range", [P, 1])
        mean, g1, g2, gf = sb("mean", [P, B]), sb("g1", [64, B]), sb("g2", [32, B]), sb("gf", [P, B])
        c0, c1, half_b4 = sb("c0", [P, B]), sb("c1", [P, 1]), sb("half_b4", [P, 1])
        a1, a2, a3 = sb("a1", [P, 4, CH]), sb("a2", [P, 2, CH]), sb("a3", [P, CH])
        th, move = sb("th", [P, 2, CH]), sb("move", [P, 2, CH])
        name = lambda n: io["L0_ffn_" + n]
        col = lambda n: name(n).rearrange("(p a) -> p a", a=1)
        pre = [(w1[:, :], name("cn_w1")), (w2[:, :], name("cn_w2")), (u1[:, :], name("gc_w1")),
               (u2[:, :], name("gc_w2")), (u3[:, :], name("gc_w3")), (b1[:, :], col("cn_b1")),
               (d1[:, :], col("gc_b1")), (d2[:, :], col("gc_b2")), (b4[:, :], name("cn_b4").partition_broadcast(P)),
               (d3[:, :], name("gc_b3").partition_broadcast(P)), (rng[:, :], name("adaptive_range").partition_broadcast(P))]
        pre += [(b2[64 * i:64 * i + 64, :], col("cn_b2")) for i in range(2)]
        pre += [(b3[32 * i:32 * i + 32, :], col("cn_b3")) for i in range(4)]
        pre += [(w4[32 * i:32 * i + 32, :], name("cn_w4")) for i in range(4)]
        blocks = [(w3[64 * i:64 * i + 64, 32 * i:32 * i + 32], name("cn_w3")) for i in range(2)]
        loaded, zeroed, small, gl_mm, gl_act, coef = (sem(f"g_{n}") for n in ("loaded", "zeroed", "small", "gl_mm", "gl_act", "coef"))
        mm1, mm2, mm3, mm4 = (sem(f"g_mm{i}") for i in range(4))
        a1_out, a2_out, a3_out, th_out, twisted, moved, stepped, coupled = (
            sem(f"g_{n}") for n in ("a1", "a2", "a3", "th", "twisted", "moved", "stepped", "coupled"))
        QUADS = CYCLES * NC // 4
        chunk = lambda m: slice(m % NC * CH, (m % NC + 1) * CH)
        twist_bank = lambda m: 3 if m % 2 else 7
        with nc.Block() as block:
            @block.sync
            def _(sp):
                for dst, src in pre:
                    sp.dma_start(dst, src).then_inc(loaded, 16)
                sp.wait_ge(zeroed, 1)
                for dst, src in blocks:
                    sp.dma_start(dst, src).then_inc(loaded, 16)

            @block.gpsimd
            def _(pool):
                pool.memset(w3[:, :], 0.0).then_inc(zeroed, 1)
                pool.memset(w4w[:, :, :], 0.0).then_inc(zeroed, 1)
                for m in range(4 * QUADS):
                    pool.wait_ge(moved, m + 1)
                    pool.tensor_tensor(k.xnT[:, chunk(m)], k.xnT[:, chunk(m)], move[:, m % 2, :], ALU.add)\
                        .then_inc(stepped, 1)

            @block.vector
            def _(v):
                v.tensor_reduce(mean[:, :], k.xnT[:, :].rearrange("p (b s) -> p b s", s=S), AX.X, ALU.add).then_inc(small, 1)
                v.wait_ge(small, 1)
                v.tensor_scalar(mean[:, :], mean[:, :], 1.0 / S, None, ALU.mult).then_inc(small, 1)
                v.wait_ge(loaded, 16 * (len(pre) + len(blocks)))
                v.wait_ge(zeroed, 2)
                v.tensor_scalar(u3w[:, :], k.ones_row[0:32, :], u3[:, 0:1], None, ALU.mult).then_inc(small, 1)
                v.tensor_scalar(half_b4[:, :], b4[:, :], 0.5, None, ALU.mult).then_inc(small, 1)
                for i in range(4):
                    rows = slice(32 * i, 32 * i + 32)
                    v.tensor_scalar(w4w[rows, i, :], k.ones_row[rows, :], w4[rows, 0:1], None, ALU.mult).then_inc(small, 1)
                v.tensor_scalar(c1[:, :], rng[:, :], 0.3, None, ALU.mult).then_inc(coef, 1)
                v.wait_ge(gl_act, 3)
                v.tensor_scalar(c0[:, :], gf[:, :], 1.4, 0.3 - 1.0, ALU.mult, ALU.add).then_inc(coef, 1)
                v.wait_ge(coef, 2)
                v.tensor_scalar(c0[:, :], c0[:, :], rng[:, 0:1], 0.1, ALU.mult, ALU.add).then_inc(coef, 1)
                v.wait_ge(coef, 3)
                for m in range(4 * QUADS):
                    b = m % NC // (NC // B)
                    v.wait_ge(th_out, m + 1)
                    v.tensor_scalar(th[:, m % 2, :], th[:, m % 2, :], c1[:, 0:1], c0[:, b:b + 1], ALU.mult, ALU.add)\
                     .then_inc(coupled, 1)
                    v.wait_ge(twisted, m + 1)
                    v.wait_ge(coupled, m + 1)
                    after(v, stepped, m - 1)
                    v.tensor_tensor(move[:, m % 2, :], th[:, m % 2, :], k.ps[:, twist_bank(m), :], ALU.mult).then_inc(moved, 1)

            @block.scalar
            def _(act):
                act.wait_ge(small, 8)
                for src, dst, b, f, rows, n in ((2, g1, d1, ACT.Gelu, 64, 1), (3, g2, d2, ACT.Gelu, 32, 2),
                                                (4, gf, d3, ACT.Sigmoid, P, 3)):
                    act.wait_ge(gl_mm, n)
                    act.activation(dst[:, :], k.ps[0:rows, src, 0:B], f, bias=b[:, 0:1]).then_inc(gl_act, 1)

                def first(n):
                    for m in range(4 * n, 4 * n + 4):
                        act.wait_ge(mm1, m + 1)
                        after(act, mm2, m - 3)
                        act.activation(a1[:, m % 4, :], k.ps[:, m % 2, :], ACT.Gelu, bias=b1[:, 0:1]).then_inc(a1_out, 1)

                first(0)
                for n in range(QUADS):
                    for q in range(2 * n, 2 * n + 2):
                        act.wait_ge(mm2, 2 * q + 2)
                        after(act, mm3, q - 1)
                        act.activation(a2[:, q % 2, :], k.ps[:, 2 + q % 2, :], ACT.Gelu, bias=b2[:, 0:1]).then_inc(a2_out, 1)
                    if n + 1 < QUADS:
                        first(n + 1)
                    act.wait_ge(mm3, 2 * n + 2)
                    after(act, mm4, 4 * n)
                    act.activation(a3[:, :], k.ps[:, 4, :], ACT.Gelu, bias=b3[:, 0:1]).then_inc(a3_out, 1)
                    for m in range(4 * n, 4 * n + 4):
                        act.wait_ge(mm4, m + 1)
                        after(act, moved, m - 1)
                        act.activation(th[:, m % 2, :], k.ps[:, 5 + m % 2, :], ACT.Tanh, bias=half_b4[:, 0:1], scale=0.5)\
                           .then_inc(th_out, 1)

            @block.tensor
            def _(pe):
                pe.wait_ge(small, 8)
                pe.matmul(k.ps[0:64, 2, 0:B], u1[:, :], mean[:, :], start=True, stop=True).then_inc(gl_mm, 1)
                pe.wait_ge(gl_act, 1)
                pe.matmul(k.ps[0:32, 3, 0:B], u2[:, :], g1[:, :], start=True, stop=True).then_inc(gl_mm, 1)
                pe.wait_ge(gl_act, 2)
                pe.matmul(k.ps[:, 4, 0:B], u3w[:, :], g2[:, :], start=True, stop=True).then_inc(gl_mm, 1)
                pe.wait_ge(gl_act, 3)

                def first(n):
                    for m in range(4 * n, 4 * n + 4):
                        after(pe, stepped, m - NC + 1)
                        after(pe, a1_out, m - 1)
                        pe.matmul(k.ps[:, m % 2, :], w1[:, :], k.xnT[:, chunk(m)], start=True, stop=True).then_inc(mm1, 1)

                def twist(m):
                    after(pe, moved, m - 1)
                    pe.matmul(k.ps[:, twist_bank(m), :], k.perm[:, :], k.xnT[:, chunk(m)], start=True, stop=True)\
                      .then_inc(twisted, 1)

                first(0)
                for n in range(QUADS):
                    for q in range(2 * n, 2 * n + 2):
                        after(pe, a2_out, q - 1)
                        if q % 2:
                            after(pe, moved, 4 * n)
                        for i in range(2):
                            pe.wait_ge(a1_out, 2 * q + i + 1)
                            pe.matmul(k.ps[64 * i:64 * i + 64, 2 + q % 2, :], w2[:, :], a1[:, (2 * q + i) % 4, :],
                                      start=True, stop=True).then_inc(mm2, 1)
                    if n + 1 < QUADS:
                        first(n + 1)
                    for q in range(2 * n, 2 * n + 2):
                        after(pe, a3_out, n)
                        pe.wait_ge(a2_out, q + 1)
                        lo = 64 * (q % 2)
                        pe.matmul(k.ps[lo:lo + 64, 4, :], w3[:, :], a2[:, q % 2, :], start=True, stop=True).then_inc(mm3, 1)
                    twist(4 * n)
                    twist(4 * n + 1)
                    for m in range(4 * n, 4 * n + 4):
                        pe.wait_ge(a3_out, n + 1)
                        after(pe, th_out, m - 1)
                        pe.matmul(k.ps[:, 5 + m % 2, :], w4w[:, m % 4, :], a3[:, :], start=True, stop=True).then_inc(mm4, 1)
                    twist(4 * n + 2)
                    twist(4 * n + 3)
    stage_gate(nc, sem, k, "g0", k.xnT)


def stage_gate(nc, sem, k, tag, outT):
    with ExitStack() as ctx:
        sb = lambda n, s, d=F32: ctx.enter_context(nc.sbuf_tensor(n, s, d))
        sig, rows = sb(tag + "sig", [P, 2, CH]), sb(tag + "rows", [P, 2, CH])
        turned, sig_out, gated, weighed, added = (sem(f"{tag}_{n}") for n in ("turned", "sig", "gated", "weighed", "added"))
        with nc.Block() as block:
            @block.tensor
            def _(pe):
                for t in range(NT):
                    if t % 4 == 0:
                        after(pe, gated, t // 4 - 1)
                    pe.transpose(k.ps[:, t // 4 % 2, (t % 4) * P:(t % 4 + 1) * P], outT[:, t * P:(t + 1) * P],
                                 k.ident[:, :]).then_inc(turned, 1)

            @block.scalar
            def _(act):
                for c in range(NC):
                    act.wait_ge(turned, 4 * c + 4)
                    after(act, gated, c - 1)
                    act.activation(sig[:, c % 2, :], k.ps[:, c % 2, :], ACT.Sigmoid).then_inc(sig_out, 1)

            @block.vector
            def _(v):
                for c in range(NC):
                    v.wait_ge(sig_out, c + 1)
                    after(v, weighed, c - 1)
                    v.tensor_tensor(rows[:, c % 2, :], sig[:, c % 2, :], k.ps[:, c % 2, :], ALU.mult).then_inc(gated, 1)

            @block.gpsimd
            def _(pool):
                for c in range(NC):
                    r = rows[:, c % 2, :].rearrange("p (t d) -> p t d", d=D)
                    at = slice(4 * c, 4 * c + 4)
                    pool.wait_ge(gated, c + 1)
                    pool.tensor_tensor(k.hs[:, at, :], r, k.hs[:, at, :], ALU.mult).then_inc(weighed, 1)
                    pool.wait_ge(weighed, c + 1)
                    pool.tensor_tensor(k.x[:, at, :], k.x[:, at, :], k.hs[:, at, :], ALU.add).then_inc(added, 1)


def stage_norm1(nc, sem, k):
    with ExitStack() as ctx:
        sb = lambda n, s, d=F32: ctx.enter_context(nc.sbuf_tensor(n, s, d))
        w = layer_norm_work(sb, "n3")
        s = layer_norm_names(sem, "n3")
        turned, xnT_out = sem("n3_turned"), sem("n3_T")
        with nc.Block() as block:
            @block.vector
            def _(v):
                layer_norm_vector(v, k.x, k.xn, w, s, lambda t: None)

            @block.scalar
            def _(act):
                layer_norm_scalar(act, k, w, s)
                for c in range(NC):
                    act.wait_ge(turned, 4 * c + 4)
                    act.copy(k.xnT[:, c * CH:(c + 1) * CH], k.ps[:, c % 2, :]).then_inc(xnT_out, 1)

            @block.tensor
            def _(pe):
                turn_tensor(pe, k, k.xn, lambda t: pe.wait_ge(s.out, t + 1), 0, xnT_out, turned)


def stage_attention1(nc, sem, io, k):
    with ExitStack() as ctx:
        sb = lambda n, s, d=F32: ctx.enter_context(nc.sbuf_tensor(n, s, d))
        qT, kT = sb("qT", [P, T]), sb("kT", [P, T])
        vr = sb("vr", [P, NT, D])
        probs = sb("probs1", [P, 2, S])
        probsT = sb("probsT1", [P, 2, S])
        outT = sb("outT1", [P, 2, P])
        nmax, bias, sums, inv = (sb("l1_" + n, [P, NT]) for n in ("nmax", "bias", "sums", "inv"))
        qk, qk_out, vv, v_out = (sem(f"l_{n}") for n in ("qk", "qk_out", "v", "v_out"))
        scored, maxed, biased, exped, inverse, normed, turned, turned_out, pv, pv_out, last, last_out = (
            sem(f"l_{n}") for n in ("scored", "maxed", "biased", "exped", "inverse", "normed", "turned", "turned_out",
                                    "pv", "pv_out", "last", "last_out"))
        with nc.Block() as block:
            @block.sync
            def _(sp):
                for e in range(NE):
                    sp.dma_start(k.W1[:, e, :], io["L1_ffn_W1"][e]).then_inc(k.experts_in, 16)
                    sp.dma_start(k.W2[:, e, :], io["L1_ffn_W2"][e]).then_inc(k.experts_in, 16)
                    sp.dma_start(k.W3[:, e, :, :], io["L1_ffn_W3"][e].rearrange("(c p) d -> p c d", p=P))\
                      .then_inc(k.experts_in, 16)

            @block.tensor
            def _(pe):
                for c in range(NC):
                    for i in range(2):
                        after(pe, qk_out, 2 * (c - 1) + i)
                        pe.matmul(k.ps[:, 2 * (c % 2) + i, :], k.wT[:, 1536 + i * P:1536 + (i + 1) * P],
                                  k.xnT[:, c * CH:(c + 1) * CH], start=True, stop=True).then_inc(qk, 1)
                    after(pe, v_out, c - 1)
                    for t in range(4 * c, 4 * c + 4):
                        pe.matmul(k.ps[:, 4 + c % 2, (t % 4) * P:(t % 4 + 1) * P], k.xnT[:, t * P:(t + 1) * P],
                                  k.wT[:, 1536 + 2 * P:1536 + 3 * P], start=True, stop=True).then_inc(vv, 1)

            @block.scalar
            def _(act):
                for c in range(NC):
                    for i, dst in enumerate((qT, kT)):
                        act.wait_ge(qk, 2 * c + i + 1)
                        act.copy(dst[:, c * CH:(c + 1) * CH], k.ps[:, 2 * (c % 2) + i, :]).then_inc(qk_out, 1)

            @block.vector
            def _(v):
                for c in range(NC):
                    v.wait_ge(vv, 4 * c + 4)
                    v.tensor_copy(vr[:, 4 * c:4 * c + 4, :], k.ps[:, 4 + c % 2, :].rearrange("p (t d) -> p t d", d=D))\
                     .then_inc(v_out, 1)

        SC = float(D) ** -0.5
        turns = []
        for t in range(NT):
            q = t % TPB
            turns += [(t, a, min(4, q + 1 - a)) for a in range(0, q + 1, 4)]
        upto = [sum(1 for x in turns if x[0] <= t) for t in range(NT)]
        with nc.Block() as block:
            @block.tensor
            def _(pe):
                def score(t):
                    b, q = t // TPB, t % TPB
                    n = (q + 1) * P
                    after(pe, exped, t - 1)
                    for c in range(0, n, CH):
                        m = min(CH, n - c)
                        diag = c + m == n
                        mm = pe.matmul(k.ps[:, 2 * (t % 2) + c // CH, 0:m], qT[:, t * P:(t + 1) * P],
                                       kT[:, b * S + c:b * S + c + m], start=True, stop=True)
                        if diag:
                            mm = pe.matmul(k.ps[:, 2 * (t % 2) + c // CH, m - P:m], k.identb[:, :], k.mask[:, :],
                                           start=False, stop=True, skip_group_check=True)
                    mm.then_inc(scored, 1)

                def weigh(t):
                    b, q = t // TPB, t % TPB
                    pe.wait_ge(turned_out, upto[t])
                    after(pe, pv_out, t)
                    for a in range(q + 1):
                        mm = pe.matmul(k.ps[:, 6, 0:P], vr[:, b * TPB + a, :], probsT[:, t % 2, a * P:(a + 1) * P],
                                       start=(a == 0), stop=(a == q))
                    mm.then_inc(pv, 1)

                def project(t):
                    pe.wait_ge(pv_out, t + 1)
                    after(pe, last_out, t)
                    pe.matmul(k.ps[:, 7, 0:P], outT[:, t % 2, :], k.wT[:, 1536 + 3 * P:1536 + 4 * P], start=True,
                              stop=True).then_inc(last, 1)

                score(0)
                n = 0
                for t in range(NT):
                    if t + 1 < NT:
                        score(t + 1)
                    if t:
                        weigh(t - 1)
                    pe.wait_ge(normed, t + 1)
                    while n < len(turns) and turns[n][0] == t:
                        _, a, m = turns[n]
                        after(pe, turned_out, n - 1)
                        for i in range(m):
                            mm = pe.transpose(k.ps[:, 4 + n % 2, i * P:(i + 1) * P],
                                              probs[:, t % 2, (a + i) * P:(a + i + 1) * P], k.ident[:, :])
                        mm.then_inc(turned, 1)
                        n += 1
                    if t:
                        project(t - 1)
                weigh(NT - 1)
                project(NT - 1)

            @block.vector
            def _(v):
                for t in range(NT):
                    n = (t % TPB + 1) * P
                    v.wait_ge(scored, t + 1)
                    v.tensor_reduce(nmax[:, t:t + 1], k.ps[:, 2 * (t % 2):2 * (t % 2) + 2, :].rearrange("p a n -> p (a n)")[:, 0:n],
                                    AX.X, ALU.max, negate=True).then_inc(maxed, 1)
                    v.wait_ge(maxed, t + 1)
                    v.tensor_scalar(bias[:, t:t + 1], nmax[:, t:t + 1], SC, None, ALU.mult).then_inc(biased, 1)
                    v.wait_ge(exped, t + 1)
                    v.reciprocal(inv[:, t:t + 1], sums[:, t:t + 1]).then_inc(inverse, 1)
                    v.wait_ge(inverse, t + 1)
                    v.tensor_scalar(probs[:, t % 2, 0:n], probs[:, t % 2, 0:n], inv[:, t:t + 1], None, ALU.mult)\
                     .then_inc(normed, 1)
                    if t:
                        v.wait_ge(last, t)
                        v.tensor_copy(k.hs[:, t - 1, :], k.ps[:, 7, 0:P]).then_inc(last_out, 1)
                v.wait_ge(last, NT)
                v.tensor_copy(k.hs[:, NT - 1, :], k.ps[:, 7, 0:P]).then_inc(last_out, 1)

            @block.scalar
            def _(act):
                n = 0

                def pv_copy(t):
                    act.wait_ge(pv, t + 1)
                    after(act, last, t - 1)
                    act.copy(outT[:, t % 2, :], k.ps[:, 6, 0:P]).then_inc(pv_out, 1)

                for t in range(NT):
                    m = (t % TPB + 1) * P
                    act.wait_ge(biased, t + 1)
                    after(act, turned, upto[t - 2] if t >= 2 else 0)
                    act.activation(probs[:, t % 2, 0:m], k.ps[:, 2 * (t % 2):2 * (t % 2) + 2, :].rearrange("p a n -> p (a n)")[:, 0:m],
                                   ACT.Exp, bias=bias[:, t:t + 1], scale=SC, accum_out=sums[:, t:t + 1]).then_inc(exped, 1)
                    if t:
                        pv_copy(t - 1)
                    while n < len(turns) and turns[n][0] == t:
                        _, a, mm = turns[n]
                        act.wait_ge(turned, n + 1)
                        after(act, pv, t - 1)
                        act.copy(probsT[:, t % 2, a * P:(a + mm) * P], k.ps[:, 4 + n % 2, 0:mm * P]).then_inc(turned_out, 1)
                        n += 1
                pv_copy(NT - 1)


BLOCKS = 40
UNROLL = 4


def stage_route(nc, sem, io, k):
    with ExitStack() as ctx:
        sb = lambda n, s, d=F32: ctx.enter_context(nc.sbuf_tensor(n, s, d))
        big = lambda n: sb(n, [P, NT, NE])
        wg = sb("wg", [P, NE])
        logit, onehot, total, sum_a, sum_b = (big(n) for n in ("logit", "onehot", "total", "sum_a", "sum_b"))
        best = sb("best", [P, NT])
        index = sb("index", [P, NE])
        steps = sb("steps", [P, NT])
        blocks = sb("blocks", [P, BLOCKS])
        over = sb("over", [P, NE, NT])
        nb, cum_a, cum_b = sb("nb", [P, NE]), sb("cum_a", [P, NE]), sb("cum_b", [P, NE])
        before, every = sb("before", [P, P]), sb("every", [P, P])
        beyond, chosen = sb("beyond", [1, BLOCKS, NE]), sb("chosen", [1, BLOCKS])
        place_f = sb("place_f", [P, NT])
        wg_in, made0, made, scored, prefixed, placed = (sem(f"r_{n}") for n in ("wg_in", "made0", "made", "scored", "prefixed", "placed"))
        step = sem("r_step")
        with nc.Block() as block:
            @block.sync
            def _(sp):
                sp.dma_start(wg[:, :], io["L1_ffn_Wg"]).then_inc(wg_in, 16)

            @block.gpsimd
            def _(pool):
                pool.iota(index[:, :], pattern=[[-1, NE]], base=NE, channel_multiplier=0,
                          allow_small_or_imprecise_dtypes=True).then_inc(made, 1)
                pool.iota(steps[:, :], pattern=[[P, NT]], base=0, channel_multiplier=0,
                          allow_small_or_imprecise_dtypes=True).then_inc(made, 1)
                pool.iota(blocks[:, :], pattern=[[1, BLOCKS]], base=0, channel_multiplier=0,
                          allow_small_or_imprecise_dtypes=True).then_inc(made, 1)
                pool.memset(every[:, :], 1.0).then_inc(made, 1)
                pool.memset(before[:, :], 1.0).then_inc(made0, 1)
                pool.wait_ge(made0, 1)
                pool.affine_select(out=before[:, :], in_=before[:, :], compare_op=ALU.is_gt, fill=0.0, base=0,
                                   pattern=[[1, P]], channel_multiplier=-1).then_inc(made, 1)
                for t in range(NT):
                    pool.wait_ge(placed, 2)
                    if t == 0:
                        pool.wait_ge(k.rows_cleared, 16)
                    pool.indirect_dma_start(k.xs_dram[:, :], bass.IndirectOffsetOnAxis(ap=k.place[:, t:t + 1], axis=0),
                                            k.xn[:, t, :], None).then_inc(k.scattered, 16)

            @block.tensor
            def _(pe):
                pe.wait_ge(wg_in, 16)
                for t in range(NT):
                    pe.matmul(k.ps[:, 0, t * NE:(t + 1) * NE], k.xnT[:, t * P:(t + 1) * P], wg[:, :], start=True,
                              stop=True).then_inc(scored, 1)
                pe.wait_ge(made, 5)
                pe.wait_ge(step, 6)
                hot = onehot[:, :, :].rearrange("p t e -> p (t e)")
                pe.matmul(k.ps[:, 1, 0:NT * NE], before[:, :], hot, start=True, stop=True).then_inc(prefixed, 1)
                pe.matmul(k.ps[:, 2, 0:NT * NE], every[:, :], hot, start=True, stop=True).then_inc(prefixed, 1)

            @block.vector
            def _(v):
                n = [0]

                def done(instruction):
                    instruction.then_inc(step, 1)
                    n[0] += 1
                    v.wait_ge(step, n[0])

                def wide(ap, at):
                    return ap.unsqueeze(at).broadcast_to([P, NT, NE])

                v.wait_ge(scored, NT)
                done(v.tensor_copy(logit[:, :, :], k.ps[:, 0, 0:NT * NE].rearrange("p (t e) -> p t e", e=NE)))
                done(v.tensor_reduce(best[:, :], logit[:, :, :], AX.X, ALU.max))
                done(v.tensor_tensor(logit[:, :, :], logit[:, :, :], wide(best[:, :], 2), ALU.is_equal))
                v.wait_ge(made, 5)
                done(v.tensor_tensor(logit[:, :, :], logit[:, :, :], wide(index[:, :], 1), ALU.mult))
                done(v.tensor_reduce(best[:, :], logit[:, :, :], AX.X, ALU.max))
                done(v.tensor_tensor(onehot[:, :, :], logit[:, :, :], wide(best[:, :], 2), ALU.is_equal))
                v.wait_ge(prefixed, 2)
                done(v.tensor_copy(total[:, :, :], k.ps[:, 2, 0:NT * NE].rearrange("p (t e) -> p t e", e=NE)))
                src, dst, by = total, sum_a, 1
                while by < NT:
                    done(v.tensor_copy(dst[:, 0:by, :], src[:, 0:by, :]))
                    done(v.tensor_tensor(dst[:, by:NT, :], src[:, by:NT, :], src[:, 0:NT - by, :], ALU.add))
                    src, dst, by = dst, sum_b if dst is sum_a else sum_a, 2 * by
                upto, rank = src, dst
                done(v.tensor_tensor(over[:, :, :], upto[:, NT - 1, :].unsqueeze(2).broadcast_to([P, NE, NT]),
                                     steps[:, :].unsqueeze(1).broadcast_to([P, NE, NT]), ALU.is_gt))
                done(v.tensor_reduce(nb[:, :], over[:, :, :], AX.X, ALU.add))
                src, dst, by = nb, cum_a, 1
                while by < NE:
                    done(v.tensor_copy(dst[:, 0:by], src[:, 0:by]))
                    done(v.tensor_tensor(dst[:, by:NE], src[:, by:NE], src[:, 0:NE - by], ALU.add))
                    src, dst, by = dst, cum_b if dst is cum_a else cum_a, 2 * by
                ends, starts = src, dst
                done(v.tensor_tensor(rank[:, :, :], upto[:, :, :], total[:, :, :], ALU.subtract))
                done(v.tensor_tensor(rank[:, :, :], rank[:, :, :],
                                     k.ps[:, 1, 0:NT * NE].rearrange("p (t e) -> p t e", e=NE), ALU.add))
                done(v.tensor_tensor(starts[:, :], ends[:, :], nb[:, :], ALU.subtract))
                done(v.tensor_scalar(starts[:, :], starts[:, :], float(P), None, ALU.mult))
                done(v.tensor_tensor(rank[:, :, :], rank[:, :, :], wide(starts[:, :], 1), ALU.add))
                done(v.tensor_tensor(rank[:, :, :], rank[:, :, :], onehot[:, :, :], ALU.mult))
                done(v.tensor_reduce(place_f[:, :], rank[:, :, :], AX.X, ALU.add))
                v.tensor_copy(k.place[:, :], place_f[:, :]).then_inc(placed, 1)
                done(v.tensor_tensor(beyond[:, :, :], blocks[0:1, :].unsqueeze(2).broadcast_to([1, BLOCKS, NE]),
                                     ends[0:1, :].unsqueeze(1).broadcast_to([1, BLOCKS, NE]), ALU.is_ge))
                done(v.tensor_reduce(chosen[:, :], beyond[:, :, :], AX.X, ALU.add))
                v.tensor_scalar(k.block_expert[:, :], chosen[:, :], float(NE - 1), None, ALU.min).then_inc(placed, 1)


def stage_experts(nc, sem, io, k, out):
    with ExitStack() as ctx:
        sb = lambda n, s, d=F32: ctx.enter_context(nc.sbuf_tensor(n, s, d))
        xb = [sb(f"xb{i}", [P, D]) for i in range(UNROLL)]
        xT, gel, hid, hidT = (sb("b_" + n, [P, 2, w]) for n, w in (("xT", P), ("gel", CH), ("hid", CH), ("hidT", CH)))
        yb = sb("b_y", [P, 2, D])
        x_in = [sem(f"b_x_in{i}") for i in range(UNROLL)]
        stored = [sem(f"b_stored{i}") for i in range(2)]
        turned, xT_out, up, gel_out, hid_out, hid_turned, hidT_out, down, y_out = (
            sem(f"b_{n}") for n in ("turned", "xT", "up", "gelu", "hid", "hid_turned", "hidT", "down", "y"))
        LAST = BLOCKS // UNROLL

        def steps(engine, step):
            for j in range(UNROLL):
                step(0, j)
            with engine.Fori(1, LAST - 1) as r:
                for j in range(UNROLL):
                    step(r, j)
            for j in range(UNROLL):
                step(LAST - 1, j)
            for j in range(2):
                step(LAST, j)

        def has(r, j, ahead=0):
            if not isinstance(r, int):
                return True
            return 0 <= UNROLL * r + j + ahead < BLOCKS

        with nc.Block() as block:
            @block.sync
            def _(sp):
                sp.wait_ge(k.scattered, 16 * NT)

                def load(r, j):
                    i = r * UNROLL + j
                    after(sp, turned, i - 3)
                    sp.dma_start(xb[j % UNROLL][:, :], k.xs_dram.rearrange("(i p) d -> i p d", p=P)[bass.ds(i, 1)]
                                 .rearrange("i p d -> (i p) d")).then_inc(x_in[j % UNROLL], 16)

                load(0, 0)
                load(0, 1)

                def step(r, j):
                    i = r * UNROLL + j
                    if has(r, j, 2):
                        load(r, j + 2)
                    if has(r, j, -2):
                        sp.wait_ge(y_out, i - 1)
                        sp.dma_start(k.ys_dram.rearrange("(i p) d -> i p d", p=P)[bass.ds(i - 2, 1)]
                                     .rearrange("i p d -> (i p) d"), yb[:, j % 2, :]).then_inc(stored[j % 2], 16)
                steps(sp, step)
                for n in range(2):
                    sp.wait_ge(stored[n], 16 * (BLOCKS // 2))

            @block.tensor
            def _(pe):
                def turn_rows(r, j):
                    i = r * UNROLL + j
                    r, j = r + j // UNROLL, j % UNROLL
                    pe.wait_ge(x_in[j], (r + 1) * 16)
                    after(pe, xT_out, i)
                    pe.transpose(k.ps[:, 7, 0:P], xb[j][:, :], k.ident[:, :]).then_inc(turned, 1)

                pe.wait_ge(k.experts_in, 16 * 3 * NE)
                turn_rows(0, 0)

                def step(r, j):
                    i = r * UNROLL + j
                    if has(r, j, 1):
                        turn_rows(r, j + 1)
                    if has(r, j):
                        e = pe.value_load(k.block_expert[0:1, bass.ds(i, 1)], min_val=0, max_val=NE - 1)
                        pe.wait_ge(xT_out, i + 1)
                        after(pe, hid_out, i - 1)
                        for half, w in ((0, k.W1), (2, k.W2)):
                            mm = pe.matmul(k.ps[:, half + j % 2, :], xT[:, j % 2, :],
                                           w[:, bass.ds(e, 1), :].rearrange("p e n -> p (e n)"), start=True, stop=True)
                        mm.then_inc(up, 1)
                    if has(r, j, -1):
                        pe.wait_ge(hid_out, i)
                        after(pe, hidT_out, i - 2)
                        o = (j - 1) % 2
                        for n in range(NI):
                            mm = pe.transpose(k.ps[:, 4 + o, n * P:(n + 1) * P], hid[:, o, n * P:(n + 1) * P], k.ident[:, :])
                        mm.then_inc(hid_turned, 1)
                    if has(r, j, -2):
                        o = j % 2
                        before = pe.value_load(k.block_expert[0:1, bass.ds(i - 2, 1)], min_val=0, max_val=NE - 1)
                        pe.wait_ge(hidT_out, i - 1)
                        after(pe, y_out, i - 2)
                        for n in range(NI):
                            mm = pe.matmul(k.ps[:, 6, 0:P], hidT[:, o, n * P:(n + 1) * P],
                                           k.W3[:, bass.ds(before, 1), n, :].rearrange("p e n -> p (e n)"),
                                           start=(n == 0), stop=(n == NI - 1))
                        mm.then_inc(down, 1)
                steps(pe, step)

            @block.scalar
            def _(act):
                def step(r, j):
                    i = r * UNROLL + j
                    if has(r, j):
                        act.wait_ge(up, i + 1)
                        after(act, hid_out, i - 1)
                        act.activation(gel[:, j % 2, :], k.ps[:, j % 2, :], ACT.Gelu).then_inc(gel_out, 1)
                    if has(r, j, -1):
                        o = (j - 1) % 2
                        act.wait_ge(hid_turned, i)
                        after(act, down, i - 2)
                        act.copy(hidT[:, o, :], k.ps[:, 4 + o, :]).then_inc(hidT_out, 1)
                steps(act, step)

            @block.vector
            def _(v):
                def rows_out(r, j):
                    i = r * UNROLL + j
                    v.wait_ge(turned, i + 1)
                    after(v, up, i - 1)
                    v.tensor_copy(xT[:, j % 2, :], k.ps[:, 7, 0:P]).then_inc(xT_out, 1)

                rows_out(0, 0)

                def step(r, j):
                    i = r * UNROLL + j
                    if has(r, j, 1):
                        rows_out(r, j + 1)
                    if has(r, j):
                        v.wait_ge(gel_out, i + 1)
                        after(v, hid_turned, i - 1)
                        v.tensor_tensor(hid[:, j % 2, :], gel[:, j % 2, :], k.ps[:, 2 + j % 2, :], ALU.mult).then_inc(hid_out, 1)
                    if has(r, j, -2):
                        v.wait_ge(down, i - 1)
                        if not (isinstance(r, int) and r == 0):
                            v.wait_ge(stored[j % 2], r * 32 + 16 * (j // 2 - 1))
                        v.tensor_copy(yb[:, j % 2, :], k.ps[:, 6, 0:P]).then_inc(y_out, 1)
                steps(v, step)

    with ExitStack() as ctx:
        sb = lambda n, s, d=F32: ctx.enter_context(nc.sbuf_tensor(n, s, d))
        W1, W2, W3 = sb("W1s", [P, INTER]), sb("W2s", [P, INTER]), sb("W3s", [P, NI, D])
        gel, hid = sb("s_gel", [P, 3, CH]), sb("s_hid", [P, 3, CH])
        y, sig = sb("s_y", [P, 2, CH]), sb("s_sig", [P, 2, CH])
        yr = sb("yr", [P, NT, D])
        w_in, up, gel_out, hid_out, down, summed, sig_out, gated, weighed, added, sent = (
            sem(f"s_{n}") for n in ("w_in", "up", "gelu", "hid", "down", "summed", "sig", "gated", "weighed", "added", "sent"))
        gathered = [sem(f"s_gathered{c}") for c in range(NC)]
        U = NC * NI
        ov = tokens(out)
        with nc.Block() as block:
            @block.gpsimd
            def _(pool):
                for t in range(NT):
                    pool.indirect_dma_start(yr[:, t, :], None, k.ys_dram[:, :],
                                            bass.IndirectOffsetOnAxis(ap=k.place[:, t:t + 1], axis=0))\
                        .then_inc(gathered[t // 4], 16)

            @block.sync
            def _(sp):
                sp.dma_start(W1[:, :], io["L1_ffn_w1s"]).then_inc(w_in, 16)
                sp.dma_start(W2[:, :], io["L1_ffn_w2s"]).then_inc(w_in, 16)
                sp.dma_start(W3[:, :, :], io["L1_ffn_w3s"].rearrange("(c p) d -> p c d", p=P)).then_inc(w_in, 16)
                for c in range(NC):
                    sp.wait_ge(added, c + 1)
                    sp.dma_start(ov[:, 4 * c:4 * c + 4, :], k.x[:, 4 * c:4 * c + 4, :]).then_inc(sent, 16)
                sp.wait_ge(sent, 16 * NC)

            @block.tensor
            def _(pe):
                def lower(u):
                    c, i = u // NI, u % NI
                    pe.wait_ge(hid_out, u + 1)
                    if i == 0:
                        after(pe, summed, c - 1)
                    for t in range(4):
                        mm = pe.matmul(k.ps[:, 6 + c % 2, t * P:(t + 1) * P], hid[:, u % 3, t * P:(t + 1) * P],
                                       W3[:, i, :], start=(i == 0 and t == 0), stop=True, skip_group_check=True)
                    mm.then_inc(down, 1)

                pe.wait_ge(w_in, 48)
                for u in range(U):
                    c, i = u // NI, u % NI
                    after(pe, hid_out, u - 2)
                    for b, w in ((2 * (u % 3), W1), (2 * (u % 3) + 1, W2)):
                        mm = pe.matmul(k.ps[:, b, :], w[:, i * P:(i + 1) * P], k.xnT[:, c * CH:(c + 1) * CH],
                                       start=True, stop=True)
                    mm.then_inc(up, 1)
                    if u >= 2:
                        lower(u - 2)
                lower(U - 2)
                lower(U - 1)

            @block.scalar
            def _(act):
                for u in range(U):
                    act.wait_ge(up, u + 1)
                    after(act, hid_out, u - 2)
                    act.activation(gel[:, u % 3, :], k.ps[:, 2 * (u % 3), :], ACT.Gelu).then_inc(gel_out, 1)
                for c in range(NC):
                    act.wait_ge(summed, c + 1)
                    after(act, gated, c - 1)
                    act.activation(sig[:, c % 2, :], k.hs2[:, c, :], ACT.Sigmoid).then_inc(sig_out, 1)

            @block.vector
            def _(v):
                def total(c):
                    v.wait_ge(down, NI * (c + 1))
                    v.wait_ge(gathered[c], 64)
                    v.tensor_tensor(k.hs2[:, c, :], k.ps[:, 6 + c % 2, :],
                                    yr[:, 4 * c:4 * c + 4, :].rearrange("p t d -> p (t d)"), ALU.add).then_inc(summed, 1)

                for u in range(U):
                    v.wait_ge(gel_out, u + 1)
                    after(v, down, u - 2)
                    v.tensor_tensor(hid[:, u % 3, :], gel[:, u % 3, :], k.ps[:, 2 * (u % 3) + 1, :], ALU.mult)\
                     .then_inc(hid_out, 1)
                    if u >= NI and u % NI == 3:
                        total(u // NI - 1)
                total(NC - 1)
                for c in range(NC):
                    at = slice(4 * c, 4 * c + 4)
                    s1 = k.hs[:, at, :].rearrange("p t d -> p (t d)")
                    xr = k.x[:, at, :].rearrange("p t d -> p (t d)")
                    v.wait_ge(summed, NC)
                    v.tensor_tensor(y[:, c % 2, :], k.hs2[:, c, :], s1, ALU.mult).then_inc(weighed, 1)
                    v.wait_ge(weighed, c + 1)
                    v.wait_ge(sig_out, c + 1)
                    v.tensor_tensor(y[:, c % 2, :], y[:, c % 2, :], sig[:, c % 2, :], ALU.mult).then_inc(gated, 1)
                    v.wait_ge(gated, c + 1)
                    v.tensor_tensor(xr, xr, y[:, c % 2, :], ALU.add).then_inc(added, 1)


def build(nc, io, out):
    with ExitStack() as ctx:
        sb = lambda n, s, d=F32: ctx.enter_context(nc.sbuf_tensor(n, s, d))
        sem = lambda n: ctx.enter_context(nc.semaphore(n))
        k = Names()
        k.x, k.xn, k.hs = (sb(n, [P, NT, D]) for n in ("x", "xn", "hs"))
        k.xnT = sb("xnT", [P, T])
        k.wT = sb("wT", [P, 2048])
        k.ln_cols = sb("ln_cols", [P, 4])
        k.bias_cols, k.bias_rows = sb("bias_cols", [P, 9]), sb("bias_rows", [P, 3 * P])
        k.ident, k.identb = sb("ident", [P, P]), sb("identb", [P, P], BF16)
        k.mask, k.maskT = sb("mask", [P, P], BF16), sb("maskT", [P, P], BF16)
        k.perm, k.empty = sb("perm", [P, P]), sb("empty", [P, D])
        k.eps, k.ones_row = sb("eps", [P, 1]), sb("ones_row", [P, P])
        k.ps = ctx.enter_context(nc.psum_tensor("ps", [P, 8, CH], F32))
        k.x_loaded = [sem(f"x_loaded{q}") for q in range(4)]
        dram = lambda n, s, d=F32: nc.dram_tensor(n, s, d, kind="Internal").ap()
        k.split_dram = [dram(f"split{i}", [PAIRS, 2, QROWS, S], BF16) for i in range(2)]
        k.o_dram = [dram(f"o{i}", [2 * PAIRS, HD + 1, S]) for i in range(2)]
        k.r_dram = dram("r", [2 * PAIRS, S])
        k.xs_dram, k.ys_dram = dram("sorted_x", [BLOCKS * P, D]), dram("sorted_y", [BLOCKS * P, D])
        k.place = sb("place", [P, NT], mybir.dt.uint32)
        k.block_expert = sb("block_expert", [1, BLOCKS], mybir.dt.int32)
        k.rows_cleared, k.scattered, k.experts_in = sem("rows_cleared"), sem("scattered"), sem("experts_in")
        early = []

        def sem_early(name):
            early.append(nc.alloc_semaphore(name=name))
            return early[-1]

        stage_weights(nc, sem_early, io, k)
        with ExitStack() as heads:
            k.v_rows = heads.enter_context(nc.sbuf_tensor("v_rows", [P, B, H // 2, TPB, 2, HD + 1], F32))
            k.v_pairs = k.v_rows[:, :, :, :, :, :].rearrange("p b a t h d -> p (b a) t h d")
            with ExitStack() as turned:
                k.hT = turned.enter_context(nc.sbuf_tensor("hT", [P, T], F32))
                stage_norms(nc, sem_early, io, k)
                stage_qkv(nc, sem_early, k)
            stage_attention0(nc, sem_early, k)
        nc.clear_and_free_semaphores(early)
        nc.all_engine_barrier()
        stage_project(nc, sem, k)
        stage_gate0(nc, sem, io, k)
        stage_norm1(nc, sem, k)
        stage_route(nc, sem, io, k)
        with ExitStack() as experts:
            k.W1, k.W2 = (experts.enter_context(nc.sbuf_tensor(n, [P, NE, INTER], F32)) for n in ("W1", "W2"))
            k.W3 = experts.enter_context(nc.sbuf_tensor("W3", [P, NE, NI, D], F32))
            stage_attention1(nc, sem, io, k)
            k.hs2 = k.xn[:, :, :].rearrange("p (c t) d -> p c (t d)", t=4)
            stage_experts(nc, sem, io, k, out)


_INS = (["L0_attn_hs"] + [f"L0_attn_ln{i}_{n}" for i in (1, 2) for n in "gb"]
        + [f"L0_attn_{c}_{n}" for c in ("ca", "cp", "cf", "cm")
           for n in ("sub_w", "Wl_w", "W_w", "B_w", "sub_b", "Wl_b", "W_b", "B_b")]
        + [f"L0_ffn_cn_{n}{i}" for i in range(1, 5) for n in "wb"] + [f"L0_ffn_gc_{n}{i}" for i in range(1, 4) for n in "wb"]
        + ["L0_ffn_adaptive_range", "L1_attn_Wq", "L1_attn_Wk", "L1_attn_Wv", "L1_attn_Wo", "L1_ffn_w1s", "L1_ffn_w2s",
           "L1_ffn_w3s", "L1_ffn_W1", "L1_ffn_W2", "L1_ffn_W3", "L1_ffn_Wg"])


def kernel(**inputs):
    import numpy as _np
    import concourse.bacc as _bacc
    from concourse import mybir as _mybir
    from concourse.bass_utils import run_bass_kernel_spmd as _run

    nc = _bacc.Bacc("TRN2", target_bir_lowering=False, num_devices=1)
    arrays, io = {}, {}
    for name in _INS:
        a = _np.ascontiguousarray(inputs[name])
        arrays[f"in_{name}_dram"] = a
        io[name] = nc.dram_tensor(f"in_{name}_dram", a.shape, _mybir.dt.from_np(a.dtype), kind="ExternalInput").ap()
    out = nc.dram_tensor("out_0_dram", (B, S, D), F32, kind="ExternalOutput").ap()
    with nc.allow_non_contiguous_dma(reason="bias columns and the choices, a few thousand elements"):
        build(nc, io, out)
    r = _run(nc, [arrays], core_ids=[0])
    return r.results[0]["out_0_dram"]
```

```python
from contextlib import ExitStack

import concourse.bass as bass
from concourse import mybir

ALU = mybir.AluOpType
ACT = mybir.ActivationFunctionType
AX = mybir.AxisListType
F32 = mybir.dt.float32
BF16 = mybir.dt.bfloat16

P = 128
B, S, D = 4, 1024, 128
T = B * S
NT = T // P
TPB = S // P
CH = 512
NC = T // CH
H, HD = 16, 8
PAIRS = B * H // 2
INTER = 512
NI = INTER // P
NE = 8
EPS = 1e-5
BIG = -1e30
TERMS = [(0, 0), (0, 1), (1, 0), (0, 2), (1, 1), (2, 0)]
QROWS = len(TERMS) * HD
MROWS = 65
SROWS = MROWS + 3

W_CA, W_CP, W_CF, W_CM = 0, 384, 512, 1024
C_CA, C_CP, C_CF, C_CM = 1536, 1539, 1540, 1544
R_V, R_CP, R_CM = 1545, 1673, 1801
GEN = 1929


def tokens(x):
    return x.rearrange("b s d -> (b s) d").rearrange("(t p) d -> p t d", p=P)


def after(engine, semaphore, count):
    if isinstance(count, int) and count <= 0:
        return
    engine.wait_ge(semaphore, count)


def moments(v, src, work, s, tiles):
    for t in tiles:
        v.bn_stats(work.stats[:, t, :], src[:, t, :]).then_inc(s.stats, 1)
    for t in tiles:
        v.wait_ge(s.stats, t + 1)
        v.bn_aggr(work.mv[:, t, :], work.stats[:, t, :]).then_inc(s.mv, 1)


def normalise(v, src, out, work, s, tiles, n):
    at = slice(tiles[0], tiles[-1] + 1)
    v.wait_ge(s.std, n + 1)
    v.reciprocal(work.rstd[:, at], work.std[:, at]).then_inc(s.rstd, 1)
    v.wait_ge(s.rstd, n + 1)
    for t in tiles:
        v.tensor_scalar(out[:, t, :], src[:, t, :], work.mv[:, t, 0:1], work.rstd[:, t:t + 1],
                        ALU.subtract, ALU.mult).then_inc(s.out, 1)


def layer_norm_vector(v, src, out, work, s, ready):
    groups = [range(t, t + TPB) for t in range(0, NT, TPB)]
    for n, tiles in enumerate(groups):
        ready(n)
        moments(v, src, work, s, tiles)
        if n:
            normalise(v, src, out, work, s, groups[n - 1], n - 1)
    normalise(v, src, out, work, s, groups[-1], len(groups) - 1)


def layer_norm_scalar(act, k, work, s, tiles):
    at = slice(tiles[0], tiles[-1] + 1)
    act.wait_ge(s.mv, tiles[-1] + 1)
    act.activation(work.std[:, at], work.mv[:, at, 1], ACT.Sqrt, bias=k.eps[:, 0:1]).then_inc(s.std, 1)


class Names:
    pass


def layer_norm_names(sem, tag):
    s = Names()
    s.stats, s.mv, s.std, s.rstd, s.out = (sem(f"{tag}_{n}") for n in ("stats", "mv", "std", "rstd", "out"))
    return s


def layer_norm_work(sb, tag):
    w = Names()
    w.stats = sb(f"{tag}_w_stats", [P, NT, 6])
    w.mv = sb(f"{tag}_w_mv", [P, NT, 2])
    w.std = sb(f"{tag}_w_std", [P, NT])
    w.rstd = sb(f"{tag}_w_rstd", [P, NT])
    return w


def turn_tensor(pe, k, src, ready, bank0, free, turned):
    for t in range(NT):
        ready(t)
        if t % 4 == 0:
            after(pe, free, t // 4 - 1)
        pe.transpose(k.ps[:, bank0 + t // 4 % 2, (t % 4) * P:(t % 4 + 1) * P], src[:, t, :],
                     k.ident[:, :]).then_inc(turned, 1)


def stage_weights(nc, sem, io, k):
    with ExitStack() as ctx:
        sb = lambda n, s, d=F32: ctx.enter_context(nc.sbuf_tensor(n, s, d))
        gs = {n: sb(f"gen_{n}", [P, GEN]) for n in ("s0", "s1", "W", "B")}
        gen = gs["s0"]
        wl = sb("wl", [P, 16])
        l1w = sb("l1w", [P, 4, P])
        loaded, consts, blended, squashed, scaled, done, turned = (
            sem(n) for n in ("w_loaded", "w_consts", "w_blended", "w_squashed", "w_scaled", "w_done", "w_turned"))
        consts0, emptied, slots = sem("w_consts0"), sem("w_emptied"), sem("w_slots")
        empty = k.empty
        w0, w1 = layer_norm_work(sb, "n0"), layer_norm_work(sb, "n1")
        h = k.hs
        s0, s1 = layer_norm_names(sem, "n0"), layer_norm_names(sem, "n1")
        xn_turned, h_turned, xn_out, h_out = (sem(n) for n in ("xn_turned", "h_turned", "xn_out", "h_out"))
        lin = {n: {m: io[f"L0_attn_{n}_{m}"] for m in ("sub_w", "Wl_w", "W_w", "B_w", "sub_b", "Wl_b", "W_b", "B_b")}
               for n in ("ca", "cp", "cf", "cm")}
        order = ("ca", "cp", "cf", "cm")
        loads = []
        for g in ("s0", "s1", "W", "B"):
            for n, at, cols in (("ca", W_CA, 3), ("cp", W_CP, 1), ("cf", W_CF, 4)):
                src = lin[n]["sub_w"][int(g[1])] if g[0] == "s" else lin[n][g + "_w"]
                loads.append((gs[g][:, at:at + cols * P].rearrange("p (c i) -> p c i", i=P),
                              src.rearrange("(c p) i -> p c i", p=P)))
            src = lin["cm"]["sub_w"][int(g[1])] if g[0] == "s" else lin["cm"][g + "_w"]
            loads.append((gs[g][:, W_CM:W_CM + INTER], src))
            for n, at, cols in (("ca", C_CA, 3), ("cp", C_CP, 1), ("cf", C_CF, 4), ("cm", C_CM, 1)):
                src = lin[n]["sub_b"][int(g[1])] if g[0] == "s" else lin[n][g + "_b"]
                loads.append((gs[g][:, at:at + cols], src.rearrange("(c p) -> p c", p=P)))
            for n, at, lo in (("ca", R_V, 256), ("cp", R_CP, 0), ("cm", R_CM, 0)):
                src = lin[n]["sub_b"][int(g[1])] if g[0] == "s" else lin[n][g + "_b"]
                loads.append((gs[g][:, at:at + P], src[lo:lo + P].partition_broadcast(P)))
        for j, n in enumerate(order):
            loads.append((wl[:, 2 * j:2 * j + 2], lin[n]["Wl_w"][0].partition_broadcast(P)))
            loads.append((wl[:, 8 + 2 * j:10 + 2 * j], lin[n]["Wl_b"][0].partition_broadcast(P)))
        for j, n in enumerate(("Wq", "Wk", "Wv", "Wo")):
            loads.append((l1w[:, j, :], io["L1_attn_" + n]))
        parts = [(W_CA, 384, 0), (W_CP, P, 2), (W_CF, 512, 4), (W_CM, 512, 6), (C_CA, 3, 8), (C_CP, 1, 10),
                 (C_CF, 4, 12), (C_CM, 1, 14), (R_V, P, 8), (R_CP, P, 10), (R_CM, P, 14)]
        xv = tokens(io["L0_attn_hs"])
        ln_cols = [(k.ln_cols[:, j:j + 1], io["L0_attn_" + n].rearrange("(p a) -> p a", a=1))
                   for j, n in enumerate(("ln1_g", "ln1_b", "ln2_g", "ln2_b"))]
        loads += ln_cols

        with nc.Block() as block:
            @block.sync
            def _(sp):
                for q in range(4):
                    sp.dma_start(k.x[:, 8 * q:8 * q + 8, :], xv[:, 8 * q:8 * q + 8, :]).then_inc(k.x_loaded[q], 16)
                for dst, src in loads:
                    sp.dma_start(dst, src).then_inc(loaded, 16)

            @block.scalar
            def _(act):
                act.wait_ge(consts, 10)
                for w, s in ((w0, s0), (w1, s1)):
                    for t in range(0, NT, TPB):
                        layer_norm_scalar(act, k, w, s, range(t, t + TPB))
                for c in range(NC):
                    act.wait_ge(xn_turned, 4 * c + 4)
                    act.copy(k.xnT[:, c * CH:(c + 1) * CH], k.ps[:, c % 2, :]).then_inc(xn_out, 1)
                act.wait_ge(emptied, 1)
                act.dma_start(k.xs_dram.rearrange("(i p) d -> p i d", p=P),
                              empty[:, :].unsqueeze(1).broadcast_to([P, BLOCKS, D])).then_inc(k.rows_cleared, 16)
                act.wait_ge(blended, 2 * len(parts))
                act.activation(gen[:, :], gen[:, :], ACT.Tanh).then_inc(squashed, 1)
                for c in range(2):
                    act.wait_ge(done, 4 * c + 4)
                    act.copy(k.wT[:, c * CH:(c + 1) * CH], k.ps[:, 4 + c, :]).then_inc(turned, 1)

            @block.gpsimd
            def _(pool):
                pool.memset(empty[:, :], 0.0).then_inc(emptied, 1)
                pool.memset(k.ident[:, :], 0.0).then_inc(consts0, 1)
                pool.memset(k.identb[:, :], 0.0).then_inc(consts0, 1)
                pool.memset(k.maskT[:, :], 0.0).then_inc(consts0, 1)
                pool.memset(k.mask[:, :], 0.0).then_inc(consts0, 1)
                pool.memset(k.perm[:, :], 0.0).then_inc(consts0, 1)
                pool.memset(k.eps[:, :], EPS).then_inc(consts, 1)
                pool.memset(k.ones_row[:, :], 1.0).then_inc(consts, 1)
                pool.wait_ge(consts0, 5)
                for t in (k.ident, k.identb):
                    pool.affine_select(out=t[:, :], in_=t[:, :], compare_op=ALU.not_equal, fill=1.0, base=0,
                                       pattern=[[-1, P]], channel_multiplier=1).then_inc(consts, 1)
                pool.affine_select(out=k.mask[:, :], in_=k.mask[:, :], compare_op=ALU.is_ge, fill=BIG, base=0,
                                   pattern=[[-1, P]], channel_multiplier=1).then_inc(consts, 1)
                pool.affine_select(out=k.maskT[:, :], in_=k.maskT[:, :], compare_op=ALU.is_ge, fill=BIG, base=0,
                                   pattern=[[1, P]], channel_multiplier=-1).then_inc(consts, 1)
                n = 6
                for lo, at, sign in ((64, 0, 1.0), (96, 32, -1.0), (0, 64, -1.0), (32, 96, 1.0)):
                    pool.wait_ge(consts, n)
                    t = k.perm[lo:lo + 32, at:at + 32]
                    pool.affine_select(out=t, in_=t, compare_op=ALU.not_equal, fill=sign, base=0,
                                       pattern=[[-1, 32]], channel_multiplier=1).then_inc(consts, 1)
                    n += 1
                pool.wait_ge(consts, n)
                for j in range(4):
                    pool.memset(k.Q[j][:, :, :], 0.0).then_inc(slots, 1)
                    pool.memset(k.K[j][:, :, :], 0.0).then_inc(slots, 1)
                pool.wait_ge(slots, 8)
                for j in range(4):
                    pool.memset(k.K[j][64:P, :, :], 1.0).then_inc(slots, 1)
                pool.wait_ge(slots, 12)

            @block.vector
            def _(v):
                layer_norm_vector(v, k.x, k.xn, w0, s0, lambda n: v.wait_ge(k.x_loaded[n], 16))
                layer_norm_vector(v, k.xn, h, w1, s1, lambda n: v.wait_ge(s0.out, TPB * (n + 1)))
                v.wait_ge(loaded, 16 * len(loads))
                for c in range(NC):
                    v.wait_ge(h_turned, 4 * c + 4)
                    v.tensor_scalar(k.hT[:, c * CH:(c + 1) * CH], k.ps[:, 2 + c % 2, :], k.ln_cols[:, 0:1],
                                    k.ln_cols[:, 1:2], ALU.mult, ALU.add).then_inc(h_out, 1)
                for n, (at, cols, w) in enumerate(parts):
                    v.tensor_scalar(gen[:, at:at + cols], gs["s0"][:, at:at + cols], wl[:, w:w + 1], None,
                                    ALU.mult).then_inc(blended, 1)
                v.wait_ge(blended, len(parts))
                for n, (at, cols, w) in enumerate(parts):
                    v.scalar_tensor_tensor(out=gen[:, at:at + cols], in0=gs["s1"][:, at:at + cols],
                                           scalar=wl[:, w + 1:w + 2], in1=gen[:, at:at + cols],
                                           op0=ALU.mult, op1=ALU.add).then_inc(blended, 1)
                v.wait_ge(squashed, 1)
                v.tensor_tensor(gen[:, :], gen[:, :], gs["W"][:, :], ALU.mult).then_inc(scaled, 1)
                v.wait_ge(scaled, 1)
                v.tensor_tensor(gen[:, :], gen[:, :], gs["B"][:, :], ALU.add).then_inc(scaled, 1)
                v.wait_ge(scaled, 2)
                v.tensor_copy(k.bias_cols[:, :], gen[:, C_CA:C_CA + 9]).then_inc(turned, 1)
                v.tensor_copy(k.bias_rows[:, :], gen[:, R_V:R_V + 3 * P]).then_inc(turned, 1)
                for c in range(2, 4):
                    v.wait_ge(done, 4 * c + 4)
                    v.tensor_copy(k.wT[:, c * CH:(c + 1) * CH], k.ps[:, 4 + c, :]).then_inc(turned, 1)

            @block.tensor
            def _(pe):
                pe.wait_ge(consts, 10)
                turn_tensor(pe, k, k.xn, lambda t: pe.wait_ge(s0.out, t + 1), 0, xn_out, xn_turned)
                turn_tensor(pe, k, h, lambda t: pe.wait_ge(s1.out, t + 1), 2, h_out, h_turned)
                pe.wait_ge(scaled, 2)
                for n in range(16):
                    src = gen[:, n * P:(n + 1) * P] if n < 12 else l1w[:, n - 12, :]
                    pe.transpose(k.ps[:, 4 + n // 4, (n % 4) * P:(n % 4 + 1) * P], src, k.ident[:, :]).then_inc(done, 1)


def stage_qkv(nc, sem, k):
    with ExitStack() as ctx:
        sb = lambda n, s, d=F32: ctx.enter_context(nc.sbuf_tensor(n, s, d))
        whole = [sb(f"whole{i}", [P, 2, CH]) for i in range(2)]
        rest = [sb(f"rest{i}", [P, 2, CH]) for i in range(2)]
        part = k.part
        proj, whole_out = sem("qk_proj"), sem("qk_whole")
        chain = [sem(f"qk_chain{i}") for i in range(2)]
        stored = k.split_stored = [[sem(f"qk_stored{i}_{j}") for j in range(2)] for i in range(2)]
        halved = [sem(f"qk_halved{i}") for i in range(2)]
        v_proj, v_out, v_ones = sem("v_proj"), sem("v_out"), sem("v_ones")
        WAYS = len(TERMS)
        with nc.Block() as block:
            @block.tensor
            def _(pe):
                for c in range(NC):
                    for i in range(2):
                        after(pe, whole_out, 4 * (c - 1) + 2 * i)
                        pe.matmul(k.ps[:, 2 * (c % 2) + i, :], k.wT[:, i * P:(i + 1) * P],
                                  k.hT[:, c * CH:(c + 1) * CH], start=True, stop=True).then_inc(proj, 1)
                    after(pe, v_out, 4 * (c - 1))
                    for t in range(4 * c, 4 * c + 4):
                        pe.matmul(k.ps[:, 4 + c % 2, (t % 4) * P:(t % 4 + 1) * P], k.hT[:, t * P:(t + 1) * P],
                                  k.wT[:, 2 * P:3 * P], start=True, stop=True).then_inc(v_proj, 1)

            def parts(i, c):
                b, at = c // 2, (c % 2) * CH
                return [part[i][:, b % 2, j, at:at + CH] for j in range(3)]

            @block.scalar
            def _(act):
                def second(c):
                    for i in range(2):
                        act.wait_ge(chain[i], 2 * c if c else 1)
                        act.copy(parts(i, c)[1], rest[i][:, c % 2, :]).then_inc(halved[i], 1)

                for c in range(NC):
                    for i in range(2):
                        p0 = parts(i, c)[0]
                        src = k.ps[:, 2 * (c % 2) + i, :]
                        act.wait_ge(proj, 2 * c + i + 1)
                        after(act, chain[i], 2 * (c - 2) if c > 2 else c - 1)
                        if c % 2 == 0:
                            after(act, stored[i][c // 2 % 2], 16 * WAYS * (c // 4))
                        act.activation(whole[i][:, c % 2, :], src, ACT.Identity, bias=k.bias_cols[:, i:i + 1])\
                           .then_inc(whole_out, 1)
                        act.activation(p0, src, ACT.Identity, bias=k.bias_cols[:, i:i + 1]).then_inc(whole_out, 1)
                    if c:
                        second(c - 1)
                second(NC - 1)

            def split(e, i, between):
                for c in range(NC + 1):
                    if c < NC:
                        p0 = parts(i, c)[0]
                        e.wait_ge(whole_out, 4 * c + 2 * i + 2)
                        after(e, chain[i], 2 * c - 1 if c >= 2 else 0)
                        e.tensor_tensor(rest[i][:, c % 2, :], whole[i][:, c % 2, :], p0, ALU.subtract)\
                         .then_inc(chain[i], 1)
                    if c:
                        e.wait_ge(halved[i], c)
                        e.tensor_tensor(parts(i, c - 1)[2], rest[i][:, (c - 1) % 2, :], parts(i, c - 1)[1],
                                        ALU.subtract).then_inc(chain[i], 1)
                    if c < NC:
                        between(c)

            @block.gpsimd
            def _(pool):
                split(pool, 1, lambda c: None)

            @block.vector
            def _(v):
                v.memset(k.v_rows[:, :, :, :, :, :], 1.0).then_inc(v_ones, 1)
                v.wait_ge(v_ones, 1)

                def v_rows(c):
                    v.wait_ge(v_proj, 4 * c + 4)
                    for t in range(4 * c, 4 * c + 4):
                        v.tensor_tensor(k.v_rows[:, t // TPB, :, t % TPB, :, 0:HD],
                                        k.ps[:, 4 + c % 2, (t % 4) * P:(t % 4 + 1) * P].rearrange(
                                            "p (a h d) -> p a h d", a=H // 2, h=2),
                                        k.bias_rows[:, 0:P].rearrange("p (a h d) -> p a h d", a=H // 2, h=2),
                                        ALU.add).then_inc(v_out, 1)
                split(v, 0, v_rows)

            @block.sync
            def _(sp):
                for b in range(B):
                    for i in range(2):
                        sp.wait_ge(chain[i], 2 * (2 * b + 2) + (b < B - 1))
                        dst = k.split_dram[i][b * (H // 2):(b + 1) * (H // 2)].rearrange(
                            "a h (t d) s -> t (a h) d s", d=HD)
                        for t, term in enumerate(TERMS):
                            sp.dma_start(dst[t], part[i][:, b % 2, term[i], :]).then_inc(stored[i][b % 2], 16)


MAX_UNITS = [(t, c * CH, min(CH, (t + 1) * P - c * CH), c == t * P // CH)
             for t in range(TPB) for c in range(t * P // CH + 1)]
EXP_UNITS = [(t, max(c * CH, t * P), (c + 1) * CH - max(c * CH, t * P), t * P >= c * CH)
             for c in range(S // CH) for t in range(4 * c + 4)]
NU = len(MAX_UNITS)
GROUPS = len(EXP_UNITS) // 2


def stage_attention0(nc, sem, k):
    with ExitStack() as ctx:
        sb = lambda n, s, d=F32: ctx.enter_context(nc.sbuf_tensor(n, s, d))
        Q, K = k.Q, k.K
        V = [sb(f"v{i}", [P, TPB, 2, HD + 1]) for i in range(4)]
        probs = sb("probs", [P, 8, CH])
        nmax = [sb(f"nmax{i}", [P, 2, TPB]) for i in range(2)]
        nmax2 = [sb(f"nmax2{i}", [P, 2, 4]) for i in range(2)]
        nrest = [sb(f"nrest{i}", [P, 2, TPB]) for i in range(2)]
        nrest2 = [sb(f"nrest2{i}", [P, 2, TPB]) for i in range(2)]
        zero = sb("zero", [P, 2, TPB])
        shift = [sb(f"shift{i}", [P, 2, 32], BF16) for i in range(2)]
        shiftT = [sb(f"shiftT{i}", [P, 2, 32], BF16) for i in range(2)]
        ev = [sb(f"ev{i}", [P, CH]) for i in range(2)]
        loaded = [sem(f"a_loaded{i}") for i in range(4)]
        shift_in = [sem(f"a_shift_in{i}") for i in range(4)]
        scored, maxed, split, shifted = sem("a_scored"), sem("a_maxed"), sem("a_split"), sem("a_shifted")
        scoredT, exped, pv_done, ev_ready = sem("a_scoredT"), sem("a_exped"), sem("a_pv"), sem("a_ev")
        ev_stored = [sem(f"a_ev_stored{i}") for i in range(2)]
        ready, joined = sem("a_ready"), sem("a_joined")
        PV = k.ps[:, 7, :]
        LOADS, SHIFTS = 16 * 5, 16 * 8

        def bodies(run):
            for j in range(4):
                run(0, j)
            with run.engine.Fori(1, PAIRS // 4 - 1) as r:
                for j in range(4):
                    run(r, j)
            for j in range(4):
                run(PAIRS // 4 - 1, j)

        def has(r, j, ahead):
            return not (isinstance(r, int) and 4 * r + j + ahead >= PAIRS)

        with nc.Block() as block:
            @block.sync
            def _(sp):
                def load(r, j):
                    p = r * 4 + j
                    r, j = r + j // 4, j % 4
                    after(sp, pv_done, (p - 3) * GROUPS)
                    for h in range(2):
                        sp.dma_start(Q[j][0:QROWS, h, :], k.split_dram[0][bass.ds(p, 1), h]
                                     .rearrange("a r s -> (a r) s")).then_inc(loaded[j], 16)
                        sp.dma_start(K[j][0:QROWS, h, :], k.split_dram[1][bass.ds(p, 1), h]
                                     .rearrange("a r s -> (a r) s")).then_inc(loaded[j], 16)
                    sp.dma_start(V[j][:, :, :, :], k.v_pairs[:, bass.ds(p, 1), :, :, :]
                                 .rearrange("p a t h d -> p (a t) h d")).then_inc(loaded[j], 16)

                def put_shift(r, j):
                    p = r * 4 + j
                    r, j = r + j // 4, j % 4
                    sp.wait_ge(shifted, p + 1)
                    for h in range(2):
                        dst = Q[j][MROWS:SROWS, h, :].rearrange("r (t a i) -> r t a i", a=4, i=32)
                        for a in range(4):
                            sp.dma_start(dst[:, :, a, :], shiftT[j % 2][32 * a:32 * a + 24, h, :])\
                              .then_inc(shift_in[j], 16)

                def store(r, j, c):
                    p = r * 4 + j
                    sp.wait_ge(ev_ready, p * 2 + (c + 1))
                    for par in range(2):
                        for h in range(2):
                            g = 32 * (2 * par + h)
                            sp.dma_start(k.o_dram[par][bass.ds(p * 2 + h, 1), :, c * CH:(c + 1) * CH]
                                         .rearrange("a r s -> (a r) s"),
                                         ev[c][g:g + HD + 1, :]).then_inc(ev_stored[c], 16)

                for i in range(2):
                    sp.wait_ge(k.split_stored[i][0], 16 * len(TERMS))
                for j in range(3):
                    load(0, j)
                put_shift(0, 0)

                def run(r, j):
                    if isinstance(r, int) and r * 4 + j == 1:
                        for i in range(2):
                            for n in range(2):
                                sp.wait_ge(k.split_stored[i][n], 16 * len(TERMS) * (B // 2))
                    if not (isinstance(r, int) and r * 4 + j == 0):
                        store(r if j else r - 1, (j - 1) % 4, 1)
                    if has(r, j, 1):
                        put_shift(r, j + 1)
                    if has(r, j, 3):
                        load(r, j + 3)
                    store(r, j, 0)
                run.engine = sp
                bodies(run)
                store(PAIRS // 4 - 1, 3, 1)
                for c in range(2):
                    sp.wait_ge(ev_stored[c], 64 * PAIRS)

            @block.gpsimd
            def _(pool):
                pool.memset(zero[:, :, :], 0.0).then_inc(ready, 1)
                for i in range(2):
                    pool.memset(shift[i][:, :, :], 0.0).then_inc(ready, 1)
                    pool.memset(ev[i][:, :], 0.0).then_inc(ready, 1)

                pool.wait_ge(ready, 6)

                def parts(r, j):
                    p = r * 4 + j
                    i = j % 2
                    part = [shift[i][:, :, 8 * n:8 * n + 8] for n in range(3)]
                    pool.wait_ge(joined, p + 1)
                    after(pool, shifted, p - 1)
                    pool.tensor_tensor(part[0], nmax[i][:, :, :], zero[:, :, :], ALU.add).then_inc(split, 1)
                    pool.wait_ge(split, p * 4 + 1)
                    pool.tensor_tensor(nrest[i][:, :, :], nmax[i][:, :, :], part[0], ALU.subtract).then_inc(split, 1)
                    pool.wait_ge(split, p * 4 + 2)
                    pool.tensor_tensor(part[1], nrest[i][:, :, :], zero[:, :, :], ALU.add).then_inc(split, 1)
                    pool.wait_ge(split, p * 4 + 3)
                    pool.tensor_tensor(part[2], nrest[i][:, :, :], part[1], ALU.subtract).then_inc(split, 1)

                parts(0, 0)
                parts(0, 1)

                def run(r, j):
                    if has(r, j, 2):
                        parts(r + (j + 2) // 4, (j + 2) % 4)
                run.engine = pool
                bodies(run)

            @block.vector
            def _(v):
                def row_max(r, j, u):
                    p = r * 4 + j
                    t, c0, n, _ = MAX_UNITS[u]
                    if u == 0:
                        after(v, split, (p - 1) * 4)
                    v.wait_ge(scored, p * NU + (u + 1))
                    out = nmax[j % 2][:, :, t:t + 1] if c0 == 0 else nmax2[j % 2][:, :, t - 4:t - 3]
                    v.tensor_reduce(out, k.ps[:, 2 * (u % 2):2 * (u % 2) + 2, 0:n], AX.X, ALU.max,
                                    negate=True).then_inc(maxed, 1)
                    if u == NU - 1:
                        v.wait_ge(maxed, (p + 1) * NU)
                        v.tensor_tensor(nmax[j % 2][:, :, 4:8], nmax[j % 2][:, :, 4:8], nmax2[j % 2][:, :, :], ALU.min)\
                         .then_inc(joined, 1)

                def turn(r, j):
                    p = r * 4 + j
                    r2, j2 = (r, j - 2) if j >= 2 else (r - 1, j + 2)
                    v.wait_ge(split, p * 4 + 4)
                    if not (isinstance(p, int) and p < 2):
                        after(v, shift_in[j2], SHIFTS * (r2 + 1))
                    v.transpose(shiftT[j % 2][:, :, :], shift[j % 2][:, :, :]).then_inc(shifted, 1)

                def evacuate(r, j, c):
                    p = r * 4 + j
                    after(v, ev_stored[c], p * 64)
                    v.wait_ge(pv_done, p * GROUPS + (2 if c == 0 else GROUPS))
                    if c == 0:
                        v.tensor_copy(ev[0][0:64, 0:P], PV[0:64, 0:P])
                        v.tensor_copy(ev[0][:, P:CH], PV[:, P:CH]).then_inc(ev_ready, 1)
                    else:
                        v.tensor_copy(ev[1][:, :], PV[:, :]).then_inc(ev_ready, 1)

                v.memset(PV, 0.0).then_inc(ready, 1)
                v.wait_ge(ready, 6)
                for j in range(2):
                    for u in range(NU):
                        row_max(0, j, u)
                turn(0, 0)

                def run(r, j):
                    for u in range(NU):
                        if has(r, j, 2):
                            row_max(r + (j + 2) // 4, (j + 2) % 4, u)
                        if u == 2 and has(r, j, 1):
                            turn(r + (j + 1) // 4, (j + 1) % 4)
                        if u == 5:
                            evacuate(r, j, 0)
                    evacuate(r, j, 1)
                run.engine = v
                bodies(run)

            @block.scalar
            def _(act):
                def run(r, j):
                    p = r * 4 + j
                    for e in range(4 * GROUPS):
                        n = EXP_UNITS[e // 2][2]
                        if e % 4 == 0:
                            after(act, pv_done, p * GROUPS + (e // 4 - 1))
                        act.wait_ge(scoredT, p * (4 * GROUPS) + (e + 1))
                        act.activation(probs[:, e % 8, 0:n], k.ps[:, 4 + e % 3, 0:n], ACT.Exp,
                                       scale=float(HD) ** -0.5).then_inc(exped, 1)
                run.engine = act
                bodies(run)

            @block.tensor
            def _(pe):
                def scores(r, j, u):
                    p = r * 4 + j
                    t, c0, n, diag = MAX_UNITS[u]
                    out = [k.ps[:, 2 * (u % 2) + h, :] for h in range(2)]
                    if u == 0:
                        pe.wait_ge(loaded[j], LOADS * (r + 1))
                    after(pe, maxed, p * NU + (u - 1))
                    for h in range(2):
                        mm = pe.matmul(out[h][:, 0:n], Q[j][0:MROWS, h, t * P:(t + 1) * P],
                                       K[j][0:MROWS, h, c0:c0 + n], start=True, stop=True)
                        if diag:
                            mm = pe.matmul(out[h][:, n - P:n], k.identb[:, :], k.mask[:, :], start=False, stop=True,
                                           skip_group_check=True)
                    mm.then_inc(scored, 1)

                def scores_t(r, j, u):
                    p = r * 4 + j
                    t, q0, n, diag = EXP_UNITS[u]
                    if u == 0:
                        pe.wait_ge(shift_in[j], SHIFTS * (r + 1))
                    for h in range(2):
                        out = k.ps[:, 4 + (2 * u + h) % 3, :]
                        after(pe, exped, p * (4 * GROUPS) + (2 * u + h - 2))
                        mm = pe.matmul(out[:, 0:n], K[j][0:SROWS, h, t * P:(t + 1) * P],
                                       Q[j][0:SROWS, h, q0:q0 + n], start=True, stop=True)
                        if diag:
                            mm = pe.matmul(out[:, 0:P], k.identb[:, :], k.maskT[:, :], start=False, stop=True,
                                           skip_group_check=True)
                        mm.then_inc(scoredT, 1)

                def weigh(r, j, g):
                    p = r * 4 + j
                    pe.wait_ge(exped, p * (4 * GROUPS) + 4 * (g + 1))
                    if g in (0, 2):
                        after(pe, ev_ready, p * 2 + (1 if g else 0))
                    for par in range(2):
                        t, q0, n, _ = EXP_UNITS[2 * g + par]
                        for h in range(2):
                            e = 4 * g + 2 * par + h
                            lo = 32 * (2 * par + h)
                            mm = pe.matmul(PV[lo:lo + HD + 1, CH - n:CH], V[j][:, t, h, :], probs[:, e % 8, 0:n],
                                           start=(g in (0, 2)), stop=True, skip_group_check=True)
                    mm.then_inc(pv_done, 1)

                pe.wait_ge(ready, 6)
                for j in range(2):
                    for u in range(NU):
                        scores(0, j, u)

                def run(r, j):
                    for u in range(NU):
                        scores_t(r, j, u)
                        if has(r, j, 2):
                            if u:
                                scores(r + (j + 2) // 4, (j + 2) % 4, u - 1)
                            if u == NU - 1:
                                scores(r + (j + 2) // 4, (j + 2) % 4, u)
                        if u % 2 and u > 1:
                            weigh(r, j, u // 2 - 1)
                    weigh(r, j, GROUPS - 1)
                run.engine = pe
                bodies(run)


CYCLES = 3


def stage_gate0(nc, sem, io, k):
    with ExitStack() as ctx:
        sb = lambda n, s, d=F32: ctx.enter_context(nc.sbuf_tensor(n, s, d))
        w1, w2, w3, w4 = sb("cn1", [P, 128]), sb("cn2", [P, 64]), sb("cn3", [P, 64]), sb("cn4", [P, 1])
        w4w = sb("cn4w", [P, 4, P])
        b1, b2, b3, b4 = sb("cb1", [P, 1]), sb("cb2", [P, 1]), sb("cb3", [P, 1]), sb("cb4", [P, 1])
        u1, u2, u3, u3w = sb("gc1", [P, 64]), sb("gc2", [64, 32]), sb("gc3", [32, 1]), sb("gc3w", [32, P])
        d1, d2, d3 = sb("gb1", [64, 1]), sb("gb2", [32, 1]), sb("gb3", [P, 1])
        rng = sb("range", [P, 1])
        mean, g1, g2, gf = sb("mean", [P, B]), sb("g1", [64, B]), sb("g2", [32, B]), sb("gf", [P, B])
        c0, c1, half_b4 = sb("c0", [P, B]), sb("c1", [P, 1]), sb("half_b4", [P, 1])
        a1, a2, a3 = sb("a1", [P, 4, CH]), sb("a2", [P, 2, CH]), sb("a3", [P, CH])
        th, move = sb("th", [P, 2, CH]), sb("move", [P, 2, CH])
        even, odd, over = k.heads_out, sb("o_odd", [P, T]), sb("o_over", [P, T])
        sums, rsum = sb("sums", [P, 2, CH]), sb("rsum", [P, CH])
        in_sums, in_o, in_over = sem("p_in_sums"), [sem(f"p_in_o{b}") for b in range(B)], sem("p_in_over")
        total, inverse, joined, normed, rstored, begun = (
            sem(f"p_{n}") for n in ("total", "inverse", "joined", "normed", "rstored", "begun"))
        name = lambda n: io["L0_ffn_" + n]
        col = lambda n: name(n).rearrange("(p a) -> p a", a=1)
        pre = [(w1[:, :], name("cn_w1")), (w2[:, :], name("cn_w2")), (u1[:, :], name("gc_w1")),
               (u2[:, :], name("gc_w2")), (u3[:, :], name("gc_w3")), (b1[:, :], col("cn_b1")),
               (d1[:, :], col("gc_b1")), (d2[:, :], col("gc_b2")), (b4[:, :], name("cn_b4").partition_broadcast(P)),
               (d3[:, :], name("gc_b3").partition_broadcast(P)), (rng[:, :], name("adaptive_range").partition_broadcast(P))]
        pre += [(b2[64 * i:64 * i + 64, :], col("cn_b2")) for i in range(2)]
        pre += [(b3[32 * i:32 * i + 32, :], col("cn_b3")) for i in range(4)]
        pre += [(w4[32 * i:32 * i + 32, :], name("cn_w4")) for i in range(4)]
        blocks = [(w3[64 * i:64 * i + 64, 32 * i:32 * i + 32], name("cn_w3")) for i in range(2)]
        loaded, zeroed, small, gl_mm, gl_act, coef = (sem(f"g_{n}") for n in ("loaded", "zeroed", "small", "gl_mm", "gl_act", "coef"))
        mm1, mm2, mm3, mm4 = (sem(f"g_mm{i}") for i in range(4))
        a1_out, a2_out, a3_out, th_out, twisted, moved, stepped, coupled = (
            sem(f"g_{n}") for n in ("a1", "a2", "a3", "th", "twisted", "moved", "stepped", "coupled"))
        QUADS = CYCLES * NC // 4
        chunk = lambda m: slice(m % NC * CH, (m % NC + 1) * CH)
        twist_bank = lambda m: 3 if m % 2 else 7
        with nc.Block() as block:
            @block.sync
            def _(sp):
                for dst, src in pre:
                    sp.dma_start(dst, src).then_inc(loaded, 16)
                sp.wait_ge(zeroed, 1)
                for dst, src in blocks:
                    sp.dma_start(dst, src).then_inc(loaded, 16)
                for par in range(2):
                    sp.dma_start(sums[:, par, :], k.o_dram[par][:, HD, :].rearrange("g (c s) -> g c s", s=CH))\
                      .then_inc(in_sums, 16)
                for b in range(B):
                    for par, dst in enumerate((even, odd)):
                        sp.dma_start(dst[:, b * S:(b + 1) * S], k.o_dram[par][b * H:(b + 1) * H, 0:HD, :])\
                          .then_inc(in_o[b], 16)
                sp.wait_ge(inverse, 1)
                sp.dma_start(k.r_dram.rearrange("g (c s) -> g c s", s=CH), rsum[:, :]).then_inc(rstored, 16)
                sp.wait_ge(rstored, 16)
                for b in range(B):
                    src = k.r_dram[b * H:(b + 1) * H, :].unsqueeze(1).broadcast_to([H, HD, S])
                    sp.dma_start(over[:, b * S:(b + 1) * S], src).then_inc(in_over, 16)

            @block.gpsimd
            def _(pool):
                pool.memset(w3[:, :], 0.0).then_inc(zeroed, 1)
                pool.memset(w4w[:, :, :], 0.0).then_inc(zeroed, 1)
                for c in range(NC):
                    at = slice(4 * c, 4 * c + 4)
                    pool.tensor_tensor(k.hs[:, at, :], k.xn[:, at, :],
                                       k.bias_rows[:, P:2 * P].unsqueeze(1).broadcast_to([P, 4, D]), ALU.add)\
                        .then_inc(begun, 1)
                pool.wait_ge(begun, NC)
                for m in range(4 * QUADS):
                    pool.wait_ge(moved, m + 1)
                    pool.tensor_tensor(k.xnT[:, chunk(m)], k.xnT[:, chunk(m)], move[:, m % 2, :], ALU.add)\
                        .then_inc(stepped, 1)
                    if m % NC == NC - 1 and m > NC:
                        for b in range(m // NC * 2 - 2, m // NC * 2):
                            at = slice(b * S, (b + 1) * S)
                            pool.wait_ge(in_o[b], 32)
                            pool.tensor_tensor(even[:, at], even[:, at], odd[:, at], ALU.add).then_inc(joined, 1)

            @block.vector
            def _(v):
                v.tensor_reduce(mean[:, :], k.xnT[:, :].rearrange("p (b s) -> p b s", s=S), AX.X, ALU.add).then_inc(small, 1)
                v.wait_ge(small, 1)
                v.tensor_scalar(mean[:, :], mean[:, :], 1.0 / S, None, ALU.mult).then_inc(small, 1)
                v.wait_ge(loaded, 16 * (len(pre) + len(blocks)))
                v.wait_ge(zeroed, 2)
                v.tensor_scalar(u3w[:, :], k.ones_row[0:32, :], u3[:, 0:1], None, ALU.mult).then_inc(small, 1)
                v.tensor_scalar(half_b4[:, :], b4[:, :], 0.5, None, ALU.mult).then_inc(small, 1)
                for i in range(4):
                    rows = slice(32 * i, 32 * i + 32)
                    v.tensor_scalar(w4w[rows, i, :], k.ones_row[rows, :], w4[rows, 0:1], None, ALU.mult).then_inc(small, 1)
                v.tensor_scalar(c1[:, :], rng[:, :], 0.3, None, ALU.mult).then_inc(coef, 1)
                v.wait_ge(gl_act, 3)
                v.tensor_scalar(c0[:, :], gf[:, :], 1.4, 0.3 - 1.0, ALU.mult, ALU.add).then_inc(coef, 1)
                v.wait_ge(coef, 2)
                v.tensor_scalar(c0[:, :], c0[:, :], rng[:, 0:1], 0.1, ALU.mult, ALU.add).then_inc(coef, 1)
                v.wait_ge(coef, 3)
                v.wait_ge(in_sums, 32)
                v.tensor_tensor(sums[:, 0, :], sums[:, 0, :], sums[:, 1, :], ALU.add).then_inc(total, 1)
                v.wait_ge(total, 1)
                v.reciprocal(rsum[:, :], sums[:, 0, :]).then_inc(inverse, 1)
                for m in range(4 * QUADS):
                    b = m % NC // (NC // B)
                    v.wait_ge(th_out, m + 1)
                    v.tensor_scalar(th[:, m % 2, :], th[:, m % 2, :], c1[:, 0:1], c0[:, b:b + 1], ALU.mult, ALU.add)\
                     .then_inc(coupled, 1)
                    v.wait_ge(twisted, m + 1)
                    v.wait_ge(coupled, m + 1)
                    after(v, stepped, m - 1)
                    v.tensor_tensor(move[:, m % 2, :], th[:, m % 2, :], k.ps[:, twist_bank(m), :], ALU.mult).then_inc(moved, 1)
                v.wait_ge(in_over, 64)
                for b in range(B):
                    at = slice(b * S, (b + 1) * S)
                    v.wait_ge(joined, b + 1)
                    v.tensor_tensor(even[:, at], even[:, at], over[:, at], ALU.mult).then_inc(normed, 1)
                v.wait_ge(normed, B)

            @block.scalar
            def _(act):
                act.wait_ge(small, 8)
                for src, dst, b, f, rows, n in ((2, g1, d1, ACT.Gelu, 64, 1), (3, g2, d2, ACT.Gelu, 32, 2),
                                                (4, gf, d3, ACT.Sigmoid, P, 3)):
                    act.wait_ge(gl_mm, n)
                    act.activation(dst[:, :], k.ps[0:rows, src, 0:B], f, bias=b[:, 0:1]).then_inc(gl_act, 1)

                def first(n):
                    for m in range(4 * n, 4 * n + 4):
                        act.wait_ge(mm1, m + 1)
                        after(act, mm2, m - 3)
                        act.activation(a1[:, m % 4, :], k.ps[:, m % 2, :], ACT.Gelu, bias=b1[:, 0:1]).then_inc(a1_out, 1)

                first(0)
                for n in range(QUADS):
                    for q in range(2 * n, 2 * n + 2):
                        act.wait_ge(mm2, 2 * q + 2)
                        after(act, mm3, q - 1)
                        act.activation(a2[:, q % 2, :], k.ps[:, 2 + q % 2, :], ACT.Gelu, bias=b2[:, 0:1]).then_inc(a2_out, 1)
                    if n + 1 < QUADS:
                        first(n + 1)
                    act.wait_ge(mm3, 2 * n + 2)
                    after(act, mm4, 4 * n)
                    act.activation(a3[:, :], k.ps[:, 4, :], ACT.Gelu, bias=b3[:, 0:1]).then_inc(a3_out, 1)
                    for m in range(4 * n, 4 * n + 4):
                        act.wait_ge(mm4, m + 1)
                        after(act, moved, m - 1)
                        act.activation(th[:, m % 2, :], k.ps[:, 5 + m % 2, :], ACT.Tanh, bias=half_b4[:, 0:1], scale=0.5)\
                           .then_inc(th_out, 1)

            @block.tensor
            def _(pe):
                pe.wait_ge(small, 8)
                pe.matmul(k.ps[0:64, 2, 0:B], u1[:, :], mean[:, :], start=True, stop=True).then_inc(gl_mm, 1)
                pe.wait_ge(gl_act, 1)
                pe.matmul(k.ps[0:32, 3, 0:B], u2[:, :], g1[:, :], start=True, stop=True).then_inc(gl_mm, 1)
                pe.wait_ge(gl_act, 2)
                pe.matmul(k.ps[:, 4, 0:B], u3w[:, :], g2[:, :], start=True, stop=True).then_inc(gl_mm, 1)
                pe.wait_ge(gl_act, 3)

                def first(n):
                    for m in range(4 * n, 4 * n + 4):
                        after(pe, stepped, m - NC + 1)
                        after(pe, a1_out, m - 1)
                        pe.matmul(k.ps[:, m % 2, :], w1[:, :], k.xnT[:, chunk(m)], start=True, stop=True).then_inc(mm1, 1)

                def twist(m):
                    after(pe, moved, m - 1)
                    pe.matmul(k.ps[:, twist_bank(m), :], k.perm[:, :], k.xnT[:, chunk(m)], start=True, stop=True)\
                      .then_inc(twisted, 1)

                first(0)
                for n in range(QUADS):
                    for q in range(2 * n, 2 * n + 2):
                        after(pe, a2_out, q - 1)
                        if q % 2:
                            after(pe, moved, 4 * n)
                        for i in range(2):
                            pe.wait_ge(a1_out, 2 * q + i + 1)
                            pe.matmul(k.ps[64 * i:64 * i + 64, 2 + q % 2, :], w2[:, :], a1[:, (2 * q + i) % 4, :],
                                      start=True, stop=True).then_inc(mm2, 1)
                    if n + 1 < QUADS:
                        first(n + 1)
                    for q in range(2 * n, 2 * n + 2):
                        after(pe, a3_out, n)
                        pe.wait_ge(a2_out, q + 1)
                        lo = 64 * (q % 2)
                        pe.matmul(k.ps[lo:lo + 64, 4, :], w3[:, :], a2[:, q % 2, :], start=True, stop=True).then_inc(mm3, 1)
                    twist(4 * n)
                    twist(4 * n + 1)
                    for m in range(4 * n, 4 * n + 4):
                        pe.wait_ge(a3_out, n + 1)
                        after(pe, th_out, m - 1)
                        pe.matmul(k.ps[:, 5 + m % 2, :], w4w[:, m % 4, :], a3[:, :], start=True, stop=True).then_inc(mm4, 1)
                    twist(4 * n + 2)
                    twist(4 * n + 3)


def stage_mlp(nc, sem, k):
    with ExitStack() as ctx:
        sb = lambda n, s, d=F32: ctx.enter_context(nc.sbuf_tensor(n, s, d))
        sig, silu = sb("m_sig", [P, 2, CH]), sb("m_silu", [P, NC, CH])
        w, w3 = layer_norm_work(sb, "n2"), layer_norm_work(sb, "n3")
        s, s3 = layer_norm_names(sem, "n2"), layer_norm_names(sem, "n3")
        rows, hT = sb("h2_rows", [P, NT, D]), sb("h2T", [P, 2, CH])
        mid = sb("mid", [P, 2, NI, CH])
        gate_turned, sig_out, gated, proj, joined, turned, hT_out, up, act_out, down, summed, biased, weighed, added = (
            sem(f"m_{n}") for n in ("gate_turned", "sig", "gated", "proj", "joined", "turned", "hT", "up", "act", "down",
                                    "summed", "biased", "weighed", "added"))
        turned3, xnT_out = sem("n3_turned"), sem("n3_T")
        tiles = lambda c: range(4 * c, 4 * c + 4)
        chunk = lambda x, c: x[:, 4 * c:4 * c + 4, :]
        as_rows = lambda ap: ap.rearrange("p (t d) -> p t d", d=D)
        GROUPS2 = [range(8 * g, 8 * g + 8) for g in range(4)]
        GROUPS3 = [range(0, NT - 8), range(NT - 8, NT)]
        with nc.Block() as block:
            @block.tensor
            def _(pe):
                def turn(c):
                    after(pe, hT_out, c - 1)
                    for t in tiles(c):
                        pe.wait_ge(s.out, t + 1)
                        mm = pe.transpose(k.ps[:, c % 2, (t % 4) * P:(t % 4 + 1) * P], rows[:, t, :], k.ident[:, :])
                    mm.then_inc(turned, 1)

                def raise_(c):
                    pe.wait_ge(hT_out, c + 1)
                    for i in range(NI):
                        n = NI * c + i
                        if n == 0:
                            pe.wait_ge(gated, NC)
                        after(pe, act_out, n - 3)
                        pe.matmul(k.ps[:, 2 + n % 4, :], k.wT[:, W_CF + i * P:W_CF + (i + 1) * P],
                                  hT[:, c % 2, :], start=True, stop=True).then_inc(up, 1)

                def lower(c):
                    pe.wait_ge(act_out, NI * c + NI)
                    after(pe, summed, c - 1)
                    if c == 0:
                        pe.wait_ge(joined, NC)
                    for t in range(4):
                        for i in range(NI):
                            mm = pe.matmul(k.ps[:, 6 + c % 2, t * P:(t + 1) * P], mid[:, c % 2, i, t * P:(t + 1) * P],
                                           k.wT[:, W_CM + i * P:W_CM + (i + 1) * P], start=(i == 0), stop=(i == NI - 1))
                    mm.then_inc(down, 1)

                def project(c):
                    after(pe, joined, c - 1)
                    for t in tiles(c):
                        mm = pe.matmul(k.ps[:, 6 + c % 2, (t % 4) * P:(t % 4 + 1) * P],
                                       k.heads_out[:, t * P:(t + 1) * P], k.wT[:, W_CP:W_CP + P], start=True, stop=True)
                    mm.then_inc(proj, 1)

                project(0)
                project(1)
                for c in range(NC):
                    after(pe, gated, c - 3)
                    for t in tiles(c):
                        mm = pe.transpose(k.ps[:, 2 + c % 4, (t % 4) * P:(t % 4 + 1) * P], k.xnT[:, t * P:(t + 1) * P],
                                          k.ident[:, :])
                    mm.then_inc(gate_turned, 1)
                    if c + 2 < NC:
                        project(c + 2)
                turn(0)
                turn(1)
                raise_(0)
                for c in range(NC):
                    if c + 2 < NC:
                        turn(c + 2)
                    if c + 1 < NC:
                        raise_(c + 1)
                    lower(c)
                pe.wait_ge(hT_out, NC)
                for c in range(NC):
                    after(pe, xnT_out, c - 1)
                    for t in tiles(c):
                        pe.wait_ge(s3.out, t + 1)
                        mm = pe.transpose(k.ps[:, c % 2, (t % 4) * P:(t % 4 + 1) * P], k.xn[:, t, :], k.ident[:, :])
                    mm.then_inc(turned3, 1)

            @block.scalar
            def _(act):
                def turn_out(c):
                    act.wait_ge(turned, c + 1)
                    after(act, up, NI * (c - 1))
                    act.activation(hT[:, c % 2, :], k.ps[:, c % 2, :], ACT.Identity, bias=k.ln_cols[:, 3:4],
                                   scale=k.ln_cols[:, 2:3]).then_inc(hT_out, 1)

                for c in range(NC):
                    act.wait_ge(gate_turned, c + 1)
                    after(act, gated, c - 1)
                    act.activation(sig[:, c % 2, :], k.ps[:, 2 + c % 4, :], ACT.Sigmoid).then_inc(sig_out, 1)
                for group in GROUPS2:
                    layer_norm_scalar(act, k, w, s, group)
                turn_out(0)
                for c in range(NC):
                    if c + 1 < NC:
                        turn_out(c + 1)
                    for i in range(NI):
                        n = NI * c + i
                        act.wait_ge(up, n + 1)
                        after(act, down, c - 1)
                        act.activation(mid[:, c % 2, i, :], k.ps[:, 2 + n % 4, :], ACT.Gelu_apprx_tanh,
                                       bias=k.bias_cols[:, 4 + i:5 + i]).then_inc(act_out, 1)
                for group in GROUPS3:
                    layer_norm_scalar(act, k, w3, s3, group)
                for c in range(NC):
                    act.wait_ge(turned3, c + 1)
                    act.copy(k.xnT[:, c * CH:(c + 1) * CH], k.ps[:, c % 2, :]).then_inc(xnT_out, 1)

            @block.vector
            def _(v):
                for c in range(NC):
                    v.wait_ge(sig_out, c + 1)
                    v.tensor_tensor(silu[:, c, :], sig[:, c % 2, :], k.ps[:, 2 + c % 4, :], ALU.mult).then_inc(gated, 1)
                    v.wait_ge(proj, c + 1)
                    v.tensor_tensor(chunk(k.hs, c), chunk(k.hs, c), as_rows(k.ps[:, 6 + c % 2, :]), ALU.add).then_inc(joined, 1)
                for g, group in enumerate(GROUPS2):
                    v.wait_ge(joined, 2 * g + 2)
                    moments(v, k.hs, w, s, group)
                    if g:
                        normalise(v, k.hs, rows, w, s, GROUPS2[g - 1], g - 1)
                normalise(v, k.hs, rows, w, s, GROUPS2[-1], 3)
                for c in range(NC):
                    v.wait_ge(down, c + 1)
                    v.wait_ge(s.out, 4 * c + 4)
                    v.tensor_tensor(chunk(k.hs, c), chunk(k.hs, c), as_rows(k.ps[:, 6 + c % 2, :]), ALU.add).then_inc(summed, 1)
                    if c >= 2:
                        v.wait_ge(added, c - 1)
                        moments(v, k.x, w3, s3, tiles(c - 2))
                normalise(v, k.x, k.xn, w3, s3, GROUPS3[0], 0)
                for c in range(NC - 2, NC):
                    v.wait_ge(added, c + 1)
                    moments(v, k.x, w3, s3, tiles(c))
                normalise(v, k.x, k.xn, w3, s3, GROUPS3[1], 1)

            @block.gpsimd
            def _(pool):
                for c in range(NC):
                    pool.wait_ge(summed, c + 1)
                    pool.tensor_tensor(chunk(k.hs, c), chunk(k.hs, c),
                                       k.bias_rows[:, 2 * P:3 * P].unsqueeze(1).broadcast_to([P, 4, D]), ALU.add)\
                        .then_inc(biased, 1)
                    pool.wait_ge(biased, c + 1)
                    pool.tensor_tensor(chunk(k.hs, c), as_rows(silu[:, c, :]), chunk(k.hs, c), ALU.mult).then_inc(weighed, 1)
                    pool.wait_ge(weighed, c + 1)
                    pool.tensor_tensor(chunk(k.x, c), chunk(k.x, c), chunk(k.hs, c), ALU.add).then_inc(added, 1)


BLOCKS = 40
UNROLL = 4


def stage_route(nc, sem, io, k):
    with ExitStack() as ctx:
        sb = lambda n, s, d=F32: ctx.enter_context(nc.sbuf_tensor(n, s, d))
        big = lambda n: sb(n, [P, NT, NE])
        wg = sb("wg", [P, NE])
        logit, onehot, total, sum_a, sum_b = (big(n) for n in ("logit", "onehot", "total", "sum_a", "sum_b"))
        best = sb("best", [P, NT])
        index = sb("index", [P, NE])
        steps = sb("steps", [P, NT])
        blocks = sb("blocks", [P, BLOCKS])
        over = sb("over", [P, NE, NT])
        nb, cum_a, cum_b = sb("nb", [P, NE]), sb("cum_a", [P, NE]), sb("cum_b", [P, NE])
        before, every = sb("before", [P, P]), sb("every", [P, P])
        beyond, chosen = sb("beyond", [1, BLOCKS, NE]), sb("chosen", [1, BLOCKS])
        place_f = sb("place_f", [P, NT])
        wg_in, made0, made, scored, prefixed, placed = (sem(f"r_{n}") for n in ("wg_in", "made0", "made", "scored", "prefixed", "placed"))
        step = sem("r_step")
        qk, qk_out, vv, v_out = (sem(f"l_{n}") for n in ("qk", "qk_out", "v", "v_out"))
        with nc.Block() as block:
            @block.sync
            def _(sp):
                sp.dma_start(wg[:, :], io["L1_ffn_Wg"]).then_inc(wg_in, 16)
                for e in range(NE):
                    sp.dma_start(k.W1[:, e, :], io["L1_ffn_W1"][e]).then_inc(k.experts_in, 16)
                    sp.dma_start(k.W2[:, e, :], io["L1_ffn_W2"][e]).then_inc(k.experts_in, 16)
                    sp.dma_start(k.W3[:, e, :, :], io["L1_ffn_W3"][e].rearrange("(c p) d -> p c d", p=P))\
                      .then_inc(k.experts_in, 16)

            @block.gpsimd
            def _(pool):
                pool.iota(index[:, :], pattern=[[-1, NE]], base=NE, channel_multiplier=0,
                          allow_small_or_imprecise_dtypes=True).then_inc(made, 1)
                pool.iota(steps[:, :], pattern=[[P, NT]], base=0, channel_multiplier=0,
                          allow_small_or_imprecise_dtypes=True).then_inc(made, 1)
                pool.iota(blocks[:, :], pattern=[[1, BLOCKS]], base=0, channel_multiplier=0,
                          allow_small_or_imprecise_dtypes=True).then_inc(made, 1)
                pool.memset(every[:, :], 1.0).then_inc(made, 1)
                pool.memset(before[:, :], 1.0).then_inc(made0, 1)
                pool.wait_ge(made0, 1)
                pool.affine_select(out=before[:, :], in_=before[:, :], compare_op=ALU.is_gt, fill=0.0, base=0,
                                   pattern=[[1, P]], channel_multiplier=-1).then_inc(made, 1)

            @block.tensor
            def _(pe):
                pe.wait_ge(wg_in, 16)
                for t in range(NT):
                    pe.matmul(k.ps[:, 6, t * NE:(t + 1) * NE], k.xnT[:, t * P:(t + 1) * P], wg[:, :], start=True,
                              stop=True).then_inc(scored, 1)
                for c in range(NC):
                    for i in range(2):
                        after(pe, qk_out, 2 * (c - 1) + i)
                        pe.matmul(k.ps[:, 2 * (c % 2) + i, :], k.wT[:, 1536 + i * P:1536 + (i + 1) * P],
                                  k.xnT[:, c * CH:(c + 1) * CH], start=True, stop=True).then_inc(qk, 1)
                    after(pe, v_out, c - 1)
                    for t in range(4 * c, 4 * c + 4):
                        mm = pe.matmul(k.ps[:, 4 + c % 2, (t % 4) * P:(t % 4 + 1) * P], k.xnT[:, t * P:(t + 1) * P],
                                       k.wT[:, 1536 + 2 * P:1536 + 3 * P], start=True, stop=True)
                    mm.then_inc(vv, 1)
                    if c == 2:
                        pe.wait_ge(made, 5)
                        pe.wait_ge(step, 6)
                        hot = onehot[:, :, :].rearrange("p t e -> p (t e)")
                        pe.matmul(k.ps[:, 7, 0:NT * NE], before[:, :], hot, start=True, stop=True).then_inc(prefixed, 1)
                        pe.matmul(k.ps[:, 7, NT * NE:2 * NT * NE], every[:, :], hot, start=True, stop=True)\
                          .then_inc(prefixed, 1)

            @block.scalar
            def _(act):
                for c in range(NC):
                    for i, dst in enumerate((k.qT, k.kT)):
                        act.wait_ge(qk, 2 * c + i + 1)
                        act.copy(dst[:, c * CH:(c + 1) * CH], k.ps[:, 2 * (c % 2) + i, :]).then_inc(qk_out, 1)
                    act.wait_ge(vv, c + 1)
                    act.copy(k.vr[:, 4 * c:4 * c + 4, :], k.ps[:, 4 + c % 2, :].rearrange("p (t d) -> p t d", d=D))\
                       .then_inc(v_out, 1)

            @block.vector
            def _(v):
                n = [0]

                def done(instruction):
                    instruction.then_inc(step, 1)
                    n[0] += 1
                    v.wait_ge(step, n[0])

                def wide(ap, at):
                    return ap.unsqueeze(at).broadcast_to([P, NT, NE])

                v.wait_ge(scored, NT)
                done(v.tensor_copy(logit[:, :, :], k.ps[:, 6, 0:NT * NE].rearrange("p (t e) -> p t e", e=NE)))
                done(v.tensor_reduce(best[:, :], logit[:, :, :], AX.X, ALU.max))
                done(v.tensor_tensor(logit[:, :, :], logit[:, :, :], wide(best[:, :], 2), ALU.is_equal))
                v.wait_ge(made, 5)
                done(v.tensor_tensor(logit[:, :, :], logit[:, :, :], wide(index[:, :], 1), ALU.mult))
                done(v.tensor_reduce(best[:, :], logit[:, :, :], AX.X, ALU.max))
                done(v.tensor_tensor(onehot[:, :, :], logit[:, :, :], wide(best[:, :], 2), ALU.is_equal))
                v.wait_ge(prefixed, 2)
                done(v.tensor_copy(total[:, :, :], k.ps[:, 7, NT * NE:2 * NT * NE].rearrange("p (t e) -> p t e", e=NE)))
                src, dst, by = total, sum_a, 1
                while by < NT:
                    done(v.tensor_copy(dst[:, 0:by, :], src[:, 0:by, :]))
                    done(v.tensor_tensor(dst[:, by:NT, :], src[:, by:NT, :], src[:, 0:NT - by, :], ALU.add))
                    src, dst, by = dst, sum_b if dst is sum_a else sum_a, 2 * by
                upto, rank = src, dst
                done(v.tensor_tensor(over[:, :, :], upto[:, NT - 1, :].unsqueeze(2).broadcast_to([P, NE, NT]),
                                     steps[:, :].unsqueeze(1).broadcast_to([P, NE, NT]), ALU.is_gt))
                done(v.tensor_reduce(nb[:, :], over[:, :, :], AX.X, ALU.add))
                src, dst, by = nb, cum_a, 1
                while by < NE:
                    done(v.tensor_copy(dst[:, 0:by], src[:, 0:by]))
                    done(v.tensor_tensor(dst[:, by:NE], src[:, by:NE], src[:, 0:NE - by], ALU.add))
                    src, dst, by = dst, cum_b if dst is cum_a else cum_a, 2 * by
                ends, starts = src, dst
                done(v.tensor_tensor(rank[:, :, :], upto[:, :, :], total[:, :, :], ALU.subtract))
                done(v.tensor_tensor(rank[:, :, :], rank[:, :, :],
                                     k.ps[:, 7, 0:NT * NE].rearrange("p (t e) -> p t e", e=NE), ALU.add))
                done(v.tensor_tensor(starts[:, :], ends[:, :], nb[:, :], ALU.subtract))
                done(v.tensor_scalar(starts[:, :], starts[:, :], float(P), None, ALU.mult))
                done(v.tensor_tensor(rank[:, :, :], rank[:, :, :], wide(starts[:, :], 1), ALU.add))
                done(v.tensor_tensor(rank[:, :, :], rank[:, :, :], onehot[:, :, :], ALU.mult))
                done(v.tensor_reduce(place_f[:, :], rank[:, :, :], AX.X, ALU.add))
                v.tensor_copy(k.place[:, :], place_f[:, :]).then_inc(placed, 1)
                done(v.tensor_tensor(beyond[:, :, :], blocks[0:1, :].unsqueeze(2).broadcast_to([1, BLOCKS, NE]),
                                     ends[0:1, :].unsqueeze(1).broadcast_to([1, BLOCKS, NE]), ALU.is_ge))
                done(v.tensor_reduce(chosen[:, :], beyond[:, :, :], AX.X, ALU.add))
                v.tensor_scalar(k.block_expert[:, :], chosen[:, :], float(NE - 1), None, ALU.min).then_inc(placed, 1)


def stage_attention1(nc, sem, k):
    with ExitStack() as ctx:
        sb = lambda n, s, d=F32: ctx.enter_context(nc.sbuf_tensor(n, s, d))
        qT, kT, vr = k.qT, k.kT, k.vr
        probs = sb("probs1", [P, 2, S])
        probsT = sb("probsT1", [P, 2, S])
        outT = sb("outT1", [P, 2, P])
        nmax, bias, sums, inv = (sb("l1_" + n, [P, NT]) for n in ("nmax", "bias", "sums", "inv"))
        scored, maxed, biased, exped, inverse, normed, turned, turned_out, pv, pv_out, last, last_out = (
            sem(f"l_{n}") for n in ("scored", "maxed", "biased", "exped", "inverse", "normed", "turned", "turned_out",
                                    "pv", "pv_out", "last", "last_out"))
        SC = float(D) ** -0.5
        turns = []
        for t in range(NT):
            q = t % TPB
            turns += [(t, a, min(4, q + 1 - a)) for a in range(0, q + 1, 4)]
        upto = [sum(1 for x in turns if x[0] <= t) for t in range(NT)]
        with nc.Block() as block:
            @block.gpsimd
            def _(pool):
                pool.wait_ge(k.rows_cleared, 16)
                for t in range(NT):
                    pool.indirect_dma_start(k.xs_dram[:, :], bass.IndirectOffsetOnAxis(ap=k.place[:, t:t + 1], axis=0),
                                            k.xn[:, t, :], None).then_inc(k.scattered, 16)

            @block.tensor
            def _(pe):
                def score(t):
                    b, q = t // TPB, t % TPB
                    n = (q + 1) * P
                    after(pe, exped, t - 1)
                    for c in range(0, n, CH):
                        m = min(CH, n - c)
                        diag = c + m == n
                        mm = pe.matmul(k.ps[:, 2 * (t % 2) + c // CH, 0:m], qT[:, t * P:(t + 1) * P],
                                       kT[:, b * S + c:b * S + c + m], start=True, stop=True)
                        if diag:
                            mm = pe.matmul(k.ps[:, 2 * (t % 2) + c // CH, m - P:m], k.identb[:, :], k.mask[:, :],
                                           start=False, stop=True, skip_group_check=True)
                    mm.then_inc(scored, 1)

                def weigh(t):
                    b, q = t // TPB, t % TPB
                    pe.wait_ge(turned_out, upto[t])
                    after(pe, pv_out, t)
                    for a in range(q + 1):
                        mm = pe.matmul(k.ps[:, 6, 0:P], vr[:, b * TPB + a, :], probsT[:, t % 2, a * P:(a + 1) * P],
                                       start=(a == 0), stop=(a == q))
                    mm.then_inc(pv, 1)

                def project(t):
                    pe.wait_ge(pv_out, t + 1)
                    after(pe, last_out, t)
                    pe.matmul(k.ps[:, 7, 0:P], outT[:, t % 2, :], k.wT[:, 1536 + 3 * P:1536 + 4 * P], start=True,
                              stop=True).then_inc(last, 1)

                score(0)
                n = 0
                for t in range(NT):
                    if t + 1 < NT:
                        score(t + 1)
                    if t:
                        weigh(t - 1)
                    pe.wait_ge(normed, t + 1)
                    while n < len(turns) and turns[n][0] == t:
                        _, a, m = turns[n]
                        after(pe, turned_out, n - 1)
                        for i in range(m):
                            mm = pe.transpose(k.ps[:, 4 + n % 2, i * P:(i + 1) * P],
                                              probs[:, t % 2, (a + i) * P:(a + i + 1) * P], k.ident[:, :])
                        mm.then_inc(turned, 1)
                        n += 1
                    if t:
                        project(t - 1)
                weigh(NT - 1)
                project(NT - 1)

            @block.vector
            def _(v):
                for t in range(NT):
                    n = (t % TPB + 1) * P
                    v.wait_ge(scored, t + 1)
                    v.tensor_reduce(nmax[:, t:t + 1], k.ps[:, 2 * (t % 2):2 * (t % 2) + 2, :].rearrange("p a n -> p (a n)")[:, 0:n],
                                    AX.X, ALU.max, negate=True).then_inc(maxed, 1)
                    v.wait_ge(maxed, t + 1)
                    v.tensor_scalar(bias[:, t:t + 1], nmax[:, t:t + 1], SC, None, ALU.mult).then_inc(biased, 1)
                    v.wait_ge(exped, t + 1)
                    v.reciprocal(inv[:, t:t + 1], sums[:, t:t + 1]).then_inc(inverse, 1)
                    v.wait_ge(inverse, t + 1)
                    v.tensor_scalar(probs[:, t % 2, 0:n], probs[:, t % 2, 0:n], inv[:, t:t + 1], None, ALU.mult)\
                     .then_inc(normed, 1)
                    if t:
                        v.wait_ge(last, t)
                        v.tensor_copy(k.hs[:, t - 1, :], k.ps[:, 7, 0:P]).then_inc(last_out, 1)
                v.wait_ge(last, NT)
                v.tensor_copy(k.hs[:, NT - 1, :], k.ps[:, 7, 0:P]).then_inc(last_out, 1)

            @block.scalar
            def _(act):
                n = 0

                def pv_copy(t):
                    act.wait_ge(pv, t + 1)
                    after(act, last, t - 1)
                    act.copy(outT[:, t % 2, :], k.ps[:, 6, 0:P]).then_inc(pv_out, 1)

                for t in range(NT):
                    m = (t % TPB + 1) * P
                    act.wait_ge(biased, t + 1)
                    after(act, turned, upto[t - 2] if t >= 2 else 0)
                    act.activation(probs[:, t % 2, 0:m], k.ps[:, 2 * (t % 2):2 * (t % 2) + 2, :].rearrange("p a n -> p (a n)")[:, 0:m],
                                   ACT.Exp, bias=bias[:, t:t + 1], scale=SC, accum_out=sums[:, t:t + 1]).then_inc(exped, 1)
                    if t:
                        pv_copy(t - 1)
                    while n < len(turns) and turns[n][0] == t:
                        _, a, mm = turns[n]
                        act.wait_ge(turned, n + 1)
                        after(act, pv, t - 1)
                        act.copy(probsT[:, t % 2, a * P:(a + mm) * P], k.ps[:, 4 + n % 2, 0:mm * P]).then_inc(turned_out, 1)
                        n += 1
                pv_copy(NT - 1)


def stage_experts(nc, sem, io, k, out):
    with ExitStack() as ctx:
        sb = lambda n, s, d=F32: ctx.enter_context(nc.sbuf_tensor(n, s, d))
        xb = [sb(f"xb{i}", [P, D]) for i in range(UNROLL)]
        xT, gel, hid, hidT = (sb("b_" + n, [P, 2, w]) for n, w in (("xT", P), ("gel", CH), ("hid", CH), ("hidT", CH)))
        yb = sb("b_y", [P, 2, D])
        x_in = [sem(f"b_x_in{i}") for i in range(UNROLL)]
        stored = [sem(f"b_stored{i}") for i in range(2)]
        turned, xT_out, up, gel_out, hid_out, hid_turned, hidT_out, down, y_out = (
            sem(f"b_{n}") for n in ("turned", "xT", "up", "gelu", "hid", "hid_turned", "hidT", "down", "y"))
        LAST = BLOCKS // UNROLL

        def steps(engine, step):
            for j in range(UNROLL):
                step(0, j)
            with engine.Fori(1, LAST - 1) as r:
                for j in range(UNROLL):
                    step(r, j)
            for j in range(UNROLL):
                step(LAST - 1, j)
            for j in range(2):
                step(LAST, j)

        def has(r, j, ahead=0):
            if not isinstance(r, int):
                return True
            return 0 <= UNROLL * r + j + ahead < BLOCKS

        with nc.Block() as block:
            @block.sync
            def _(sp):
                sp.wait_ge(k.scattered, 16 * NT)

                def load(r, j):
                    i = r * UNROLL + j
                    after(sp, turned, i - 3)
                    sp.dma_start(xb[j % UNROLL][:, :], k.xs_dram.rearrange("(i p) d -> i p d", p=P)[bass.ds(i, 1)]
                                 .rearrange("i p d -> (i p) d")).then_inc(x_in[j % UNROLL], 16)

                load(0, 0)
                load(0, 1)

                def step(r, j):
                    i = r * UNROLL + j
                    if has(r, j, 2):
                        load(r, j + 2)
                    if has(r, j, -2):
                        sp.wait_ge(y_out, i - 1)
                        sp.dma_start(k.ys_dram.rearrange("(i p) d -> i p d", p=P)[bass.ds(i - 2, 1)]
                                     .rearrange("i p d -> (i p) d"), yb[:, j % 2, :]).then_inc(stored[j % 2], 16)
                steps(sp, step)
                for n in range(2):
                    sp.wait_ge(stored[n], 16 * (BLOCKS // 2))

            @block.tensor
            def _(pe):
                def turn_rows(r, j):
                    i = r * UNROLL + j
                    r, j = r + j // UNROLL, j % UNROLL
                    pe.wait_ge(x_in[j], (r + 1) * 16)
                    after(pe, xT_out, i)
                    pe.transpose(k.ps[:, 7, 0:P], xb[j][:, :], k.ident[:, :]).then_inc(turned, 1)

                pe.wait_ge(k.experts_in, 16 * 3 * NE)
                turn_rows(0, 0)

                def step(r, j):
                    i = r * UNROLL + j
                    if has(r, j, 1):
                        turn_rows(r, j + 1)
                    if has(r, j):
                        e = pe.value_load(k.block_expert[0:1, bass.ds(i, 1)], min_val=0, max_val=NE - 1)
                        pe.wait_ge(xT_out, i + 1)
                        after(pe, hid_out, i - 1)
                        for half, w in ((0, k.W1), (2, k.W2)):
                            mm = pe.matmul(k.ps[:, half + j % 2, :], xT[:, j % 2, :],
                                           w[:, bass.ds(e, 1), :].rearrange("p e n -> p (e n)"), start=True, stop=True)
                        mm.then_inc(up, 1)
                    if has(r, j, -1):
                        pe.wait_ge(hid_out, i)
                        after(pe, hidT_out, i - 2)
                        o = (j - 1) % 2
                        for n in range(NI):
                            mm = pe.transpose(k.ps[:, 4 + o, n * P:(n + 1) * P], hid[:, o, n * P:(n + 1) * P], k.ident[:, :])
                        mm.then_inc(hid_turned, 1)
                    if has(r, j, -2):
                        o = j % 2
                        before = pe.value_load(k.block_expert[0:1, bass.ds(i - 2, 1)], min_val=0, max_val=NE - 1)
                        pe.wait_ge(hidT_out, i - 1)
                        after(pe, y_out, i - 2)
                        for n in range(NI):
                            mm = pe.matmul(k.ps[:, 6, 0:P], hidT[:, o, n * P:(n + 1) * P],
                                           k.W3[:, bass.ds(before, 1), n, :].rearrange("p e n -> p (e n)"),
                                           start=(n == 0), stop=(n == NI - 1))
                        mm.then_inc(down, 1)
                steps(pe, step)

            @block.scalar
            def _(act):
                def step(r, j):
                    i = r * UNROLL + j
                    if has(r, j):
                        act.wait_ge(up, i + 1)
                        after(act, hid_out, i - 1)
                        act.activation(gel[:, j % 2, :], k.ps[:, j % 2, :], ACT.Gelu).then_inc(gel_out, 1)
                    if has(r, j, -1):
                        o = (j - 1) % 2
                        act.wait_ge(hid_turned, i)
                        after(act, down, i - 2)
                        act.copy(hidT[:, o, :], k.ps[:, 4 + o, :]).then_inc(hidT_out, 1)
                steps(act, step)

            @block.vector
            def _(v):
                def rows_out(r, j):
                    i = r * UNROLL + j
                    v.wait_ge(turned, i + 1)
                    after(v, up, i - 1)
                    v.tensor_copy(xT[:, j % 2, :], k.ps[:, 7, 0:P]).then_inc(xT_out, 1)

                rows_out(0, 0)

                def step(r, j):
                    i = r * UNROLL + j
                    if has(r, j, 1):
                        rows_out(r, j + 1)
                    if has(r, j):
                        v.wait_ge(gel_out, i + 1)
                        after(v, hid_turned, i - 1)
                        v.tensor_tensor(hid[:, j % 2, :], gel[:, j % 2, :], k.ps[:, 2 + j % 2, :], ALU.mult).then_inc(hid_out, 1)
                    if has(r, j, -2):
                        v.wait_ge(down, i - 1)
                        if not (isinstance(r, int) and r == 0):
                            v.wait_ge(stored[j % 2], r * 32 + 16 * (j // 2 - 1))
                        v.tensor_copy(yb[:, j % 2, :], k.ps[:, 6, 0:P]).then_inc(y_out, 1)
                steps(v, step)

    with ExitStack() as ctx:
        sb = lambda n, s, d=F32: ctx.enter_context(nc.sbuf_tensor(n, s, d))
        W1, W2, W3 = sb("W1s", [P, INTER]), sb("W2s", [P, INTER]), sb("W3s", [P, NI, D])
        gel, hid = sb("s_gel", [P, 3, CH]), sb("s_hid", [P, 3, CH])
        y, sig = sb("s_y", [P, 2, CH]), sb("s_sig", [P, 2, CH])
        yr = sb("yr", [P, NT, D])
        w_in, up, gel_out, hid_out, down, summed, sig_out, gated, weighed, added, sent = (
            sem(f"s_{n}") for n in ("w_in", "up", "gelu", "hid", "down", "summed", "sig", "gated", "weighed", "added", "sent"))
        gathered = [sem(f"s_gathered{c}") for c in range(NC)]
        U = NC * NI
        ov = tokens(out)
        with nc.Block() as block:
            @block.gpsimd
            def _(pool):
                for t in range(NT):
                    pool.indirect_dma_start(yr[:, t, :], None, k.ys_dram[:, :],
                                            bass.IndirectOffsetOnAxis(ap=k.place[:, t:t + 1], axis=0))\
                        .then_inc(gathered[t // 4], 16)

            @block.sync
            def _(sp):
                sp.dma_start(W1[:, :], io["L1_ffn_w1s"]).then_inc(w_in, 16)
                sp.dma_start(W2[:, :], io["L1_ffn_w2s"]).then_inc(w_in, 16)
                sp.dma_start(W3[:, :, :], io["L1_ffn_w3s"].rearrange("(c p) d -> p c d", p=P)).then_inc(w_in, 16)
                for c in range(NC):
                    sp.wait_ge(added, c + 1)
                    sp.dma_start(ov[:, 4 * c:4 * c + 4, :], k.x[:, 4 * c:4 * c + 4, :]).then_inc(sent, 16)
                sp.wait_ge(sent, 16 * NC)

            @block.tensor
            def _(pe):
                def lower(u):
                    c, i = u // NI, u % NI
                    pe.wait_ge(hid_out, u + 1)
                    if i == 0:
                        after(pe, summed, c - 1)
                    for t in range(4):
                        mm = pe.matmul(k.ps[:, 6 + c % 2, t * P:(t + 1) * P], hid[:, u % 3, t * P:(t + 1) * P],
                                       W3[:, i, :], start=(i == 0 and t == 0), stop=True, skip_group_check=True)
                    mm.then_inc(down, 1)

                pe.wait_ge(w_in, 48)
                for u in range(U):
                    c, i = u // NI, u % NI
                    after(pe, hid_out, u - 2)
                    for b, w in ((2 * (u % 3), W1), (2 * (u % 3) + 1, W2)):
                        mm = pe.matmul(k.ps[:, b, :], w[:, i * P:(i + 1) * P], k.xnT[:, c * CH:(c + 1) * CH],
                                       start=True, stop=True)
                    mm.then_inc(up, 1)
                    if u >= 2:
                        lower(u - 2)
                lower(U - 2)
                lower(U - 1)

            @block.scalar
            def _(act):
                for u in range(U):
                    act.wait_ge(up, u + 1)
                    after(act, hid_out, u - 2)
                    act.activation(gel[:, u % 3, :], k.ps[:, 2 * (u % 3), :], ACT.Gelu).then_inc(gel_out, 1)
                for c in range(NC):
                    act.wait_ge(summed, c + 1)
                    after(act, gated, c - 1)
                    act.activation(sig[:, c % 2, :], k.hs2[:, c, :], ACT.Sigmoid).then_inc(sig_out, 1)

            @block.vector
            def _(v):
                def total(c):
                    v.wait_ge(down, NI * (c + 1))
                    v.wait_ge(gathered[c], 64)
                    v.tensor_tensor(k.hs2[:, c, :], k.ps[:, 6 + c % 2, :],
                                    yr[:, 4 * c:4 * c + 4, :].rearrange("p t d -> p (t d)"), ALU.add).then_inc(summed, 1)

                for u in range(U):
                    v.wait_ge(gel_out, u + 1)
                    after(v, down, u - 2)
                    v.tensor_tensor(hid[:, u % 3, :], gel[:, u % 3, :], k.ps[:, 2 * (u % 3) + 1, :], ALU.mult)\
                     .then_inc(hid_out, 1)
                    if u >= NI and u % NI == 3:
                        total(u // NI - 1)
                total(NC - 1)
                for c in range(NC):
                    at = slice(4 * c, 4 * c + 4)
                    s1 = k.hs[:, at, :].rearrange("p t d -> p (t d)")
                    xr = k.x[:, at, :].rearrange("p t d -> p (t d)")
                    v.wait_ge(summed, NC)
                    v.tensor_tensor(y[:, c % 2, :], k.hs2[:, c, :], s1, ALU.mult).then_inc(weighed, 1)
                    v.wait_ge(weighed, c + 1)
                    v.wait_ge(sig_out, c + 1)
                    v.tensor_tensor(y[:, c % 2, :], y[:, c % 2, :], sig[:, c % 2, :], ALU.mult).then_inc(gated, 1)
                    v.wait_ge(gated, c + 1)
                    v.tensor_tensor(xr, xr, y[:, c % 2, :], ALU.add).then_inc(added, 1)


def build(nc, io, out):
    with ExitStack() as ctx:
        sb = lambda n, s, d=F32: ctx.enter_context(nc.sbuf_tensor(n, s, d))
        sem = lambda n: ctx.enter_context(nc.semaphore(n))
        k = Names()
        k.x, k.xn, k.hs = (sb(n, [P, NT, D]) for n in ("x", "xn", "hs"))
        k.xnT = sb("xnT", [P, T])
        k.wT = sb("wT", [P, 2048])
        k.ln_cols = sb("ln_cols", [P, 4])
        k.bias_cols, k.bias_rows = sb("bias_cols", [P, 9]), sb("bias_rows", [P, 3 * P])
        k.ident, k.identb = sb("ident", [P, P]), sb("identb", [P, P], BF16)
        k.mask, k.maskT = sb("mask", [P, P], BF16), sb("maskT", [P, P], BF16)
        k.perm, k.empty = sb("perm", [P, P]), sb("empty", [P, D])
        k.eps, k.ones_row = sb("eps", [P, 1]), sb("ones_row", [P, P])
        k.ps = ctx.enter_context(nc.psum_tensor("ps", [P, 8, CH], F32))
        k.x_loaded = [sem(f"x_loaded{q}") for q in range(4)]
        dram = lambda n, s, d=F32: nc.dram_tensor(n, s, d, kind="Internal").ap()
        k.split_dram = [dram(f"split{i}", [PAIRS, 2, QROWS, S], BF16) for i in range(2)]
        k.o_dram = [dram(f"o{i}", [2 * PAIRS, HD + 1, S]) for i in range(2)]
        k.r_dram = dram("r", [2 * PAIRS, S])
        k.xs_dram, k.ys_dram = dram("sorted_x", [BLOCKS * P, D]), dram("sorted_y", [BLOCKS * P, D])
        k.place = sb("place", [P, NT], mybir.dt.uint32)
        k.block_expert = sb("block_expert", [1, BLOCKS], mybir.dt.int32)
        k.rows_cleared, k.scattered, k.experts_in = sem("rows_cleared"), sem("scattered"), sem("experts_in")
        early = []

        def sem_early(name):
            early.append(nc.alloc_semaphore(name=name))
            return early[-1]

        with ExitStack() as heads:
            k.v_rows = heads.enter_context(nc.sbuf_tensor("v_rows", [P, B, H // 2, TPB, 2, HD + 1], F32))
            k.v_pairs = k.v_rows[:, :, :, :, :, :].rearrange("p b a t h d -> p (b a) t h d")
            k.Q, k.K = ([heads.enter_context(nc.sbuf_tensor(f"{n}{i}", [P, 2, S], BF16)) for i in range(4)] for n in "qk")
            k.part = [heads.enter_context(nc.sbuf_tensor(f"part{i}", [P, 2, 3, S], BF16)) for i in range(2)]
            with ExitStack() as turned:
                k.hT = turned.enter_context(nc.sbuf_tensor("hT", [P, T], F32))
                stage_weights(nc, sem_early, io, k)
                stage_qkv(nc, sem_early, k)
            stage_attention0(nc, sem_early, k)
        nc.clear_and_free_semaphores(early)
        nc.all_engine_barrier()
        with ExitStack() as heads:
            k.heads_out = heads.enter_context(nc.sbuf_tensor("heads_out", [P, T], F32))
            stage_gate0(nc, sem, io, k)
            stage_mlp(nc, sem, k)
        with ExitStack() as experts:
            k.W1, k.W2 = (experts.enter_context(nc.sbuf_tensor(n, [P, NE, INTER], F32)) for n in ("W1", "W2"))
            k.W3 = experts.enter_context(nc.sbuf_tensor("W3", [P, NE, NI, D], F32))
            with ExitStack() as heads:
                k.qT, k.kT = (heads.enter_context(nc.sbuf_tensor(n, [P, T], F32)) for n in ("qT", "kT"))
                k.vr = heads.enter_context(nc.sbuf_tensor("vr", [P, NT, D], F32))
                stage_route(nc, sem, io, k)
                stage_attention1(nc, sem, k)
            k.hs2 = k.xn[:, :, :].rearrange("p (c t) d -> p c (t d)", t=4)
            stage_experts(nc, sem, io, k, out)


_INS = (["L0_attn_hs"] + [f"L0_attn_ln{i}_{n}" for i in (1, 2) for n in "gb"]
        + [f"L0_attn_{c}_{n}" for c in ("ca", "cp", "cf", "cm")
           for n in ("sub_w", "Wl_w", "W_w", "B_w", "sub_b", "Wl_b", "W_b", "B_b")]
        + [f"L0_ffn_cn_{n}{i}" for i in range(1, 5) for n in "wb"] + [f"L0_ffn_gc_{n}{i}" for i in range(1, 4) for n in "wb"]
        + ["L0_ffn_adaptive_range", "L1_attn_Wq", "L1_attn_Wk", "L1_attn_Wv", "L1_attn_Wo", "L1_ffn_w1s", "L1_ffn_w2s",
           "L1_ffn_w3s", "L1_ffn_W1", "L1_ffn_W2", "L1_ffn_W3", "L1_ffn_Wg"])


def kernel(**inputs):
    import numpy as _np
    import concourse.bacc as _bacc
    from concourse import mybir as _mybir
    from concourse.bass_utils import run_bass_kernel_spmd as _run

    nc = _bacc.Bacc("TRN2", target_bir_lowering=False, num_devices=1)
    arrays, io = {}, {}
    for name in _INS:
        a = _np.ascontiguousarray(inputs[name])
        arrays[f"in_{name}_dram"] = a
        io[name] = nc.dram_tensor(f"in_{name}_dram", a.shape, _mybir.dt.from_np(a.dtype), kind="ExternalInput").ap()
    out = nc.dram_tensor("out_0_dram", (B, S, D), F32, kind="ExternalOutput").ap()
    with nc.allow_non_contiguous_dma(reason="bias columns and the choices, a few thousand elements"):
        build(nc, io, out)
    r = _run(nc, [arrays], core_ids=[0])
    return r.results[0]["out_0_dram"]
```
